# Optimizing a Trainium2 kernel written in Bass

```python
import numpy as np
import jax
import jax.numpy as jnp

def _softmax(x, axis=-1):
    return jax.nn.softmax(x, axis=axis)

def _gelu(x):
    return jax.nn.gelu(x, approximate=True)

def _silu(x):
    return jax.nn.silu(x)

def _sigmoid(x):
    return jax.nn.sigmoid(x)

def _layernorm(x, axis=-1, eps=1e-05):
    m = jnp.mean(x, axis=axis, keepdims=True)
    v = jnp.var(x, axis=axis, keepdims=True)
    return (x - m) / jnp.sqrt(v + eps)

def _scatter_add(tgt, idx, src, axis=0):
    return tgt.at[idx].add(src)

def _segment_sum(src, seg, n):
    return jax.ops.segment_sum(src, seg, n)
kernel_name = 'mk_flamingo_gated_d2_seqx_r8_b8f67b'

def setup_inputs(seed: int=0):
    np.random.seed(seed)
    _w = jnp.asarray

    def _rec_inputs():
        import jax
        import jax.numpy as jnp
        _rk = jax.random.key(seed)
        x = -4.161e-06 + 1 * jax.random.normal(jax.random.fold_in(_rk, 1), (4, 256, 256), jnp.float32)
        _lenS = 256 - jax.random.randint(jax.random.fold_in(_rk, 7), (4,), 0, max(1, 256 // 4) + 1, jnp.int32)
        _lenS2 = 1601 - jax.random.randint(jax.random.fold_in(_rk, 8), (4,), 0, max(1, 1601 // 4) + 1, jnp.int32)
        _ctx_2048P = jax.random.normal(jax.random.fold_in(_rk, 11), (4, 16, 256), jnp.float32)
        _ctx_2048c = jax.random.dirichlet(jax.random.fold_in(_rk, 511), 0.3 * jnp.ones((16,), jnp.float32), (4, 1601))
        _ctx_2048t = jnp.einsum('bsk,bkd->bsd', _ctx_2048c, _ctx_2048P)
        _ctx_2048t = _ctx_2048t * jax.lax.rsqrt(jnp.mean(jnp.square(_ctx_2048t)) + 1e-12) * 0.953939
        ctx_2048 = -0.000192764 + 0.999654 * (_ctx_2048t + 0.3 * jax.random.normal(jax.random.fold_in(_rk, 611), (4, 1601, 256), jnp.float32))
        _g = jax.random.normal(jax.random.fold_in(_rk, 9001), (2, 2), jnp.float32)
        _g = jnp.sign(_g) * jnp.maximum(jnp.abs(_g), 1.0) + (_g == 0) * 1.0
        g_xattn = _g[0]
        g_ffn = _g[1]
        return (x, ctx_2048, g_xattn, g_ffn)
    x, ctx_2048, g_xattn, g_ffn = _rec_inputs()

    def _L0_xattn_setup():
        import jax, jax.numpy as jnp
        import numpy as np
        FP8_MAX = 448.0
        EPS = 1e-05

        def _fp8_roundtrip(x):
            return x.astype(jnp.float8_e4m3fn).astype(jnp.float32)

        def _div_clamp_fp8(x, scale):
            y = jnp.clip(x.astype(jnp.float32) / scale, -FP8_MAX, FP8_MAX)
            y = y.astype(jnp.bfloat16).astype(jnp.float32)
            return _fp8_roundtrip(y)

        def _ln(x, w, b):
            mu = jnp.mean(x, axis=-1, keepdims=True)
            var = jnp.mean(jnp.square(x - mu), axis=-1, keepdims=True)
            return (x - mu) * jax.lax.rsqrt(var + EPS) * w + b

        def _fp8_linear_pertensor(x, wq, w_scale, in_scale):
            xq = _div_clamp_fp8(x, in_scale)
            return jnp.einsum('bsi,oi->bso', xq * in_scale, wq) * w_scale

        def _gqa(q, k, v):
            scale = 1.0 / np.sqrt(q.shape[-1])
            scores = jnp.einsum('bsghd,btgd->bghst', q, k) * scale
            p = jax.nn.softmax(scores, axis=-1)
            return jnp.einsum('bghst,btgd->bsghd', p, v)
        key = jax.random.key(seed)
        ks = jax.random.split(key, 8)
        B, S, SC, H, NH, G, D = (2, 256, 64, 256, 16, 8, 128)

        def qw(k, out_f, in_f):
            w = jax.random.normal(k, (out_f, in_f), jnp.float32) * 0.02
            sc = jnp.max(jnp.abs(w)) / FP8_MAX
            return (_fp8_roundtrip(w / sc), sc.astype(jnp.float32))
        wq, wq_s = qw(ks[0], NH * D, H)
        wqx, wqx_s = qw(ks[1], NH * D, H)
        wk, wk_s = qw(ks[2], G * D, H)
        wv, wv_s = qw(ks[3], G * D, H)
        wproj, wp_s = qw(ks[4], H, 2 * NH * D)
        return {'hidden_states': jax.random.normal(ks[5], (B, S, H), jnp.float32), 'cond': jax.random.normal(ks[6], (B, SC, H), jnp.float32), 'ln_w': jnp.ones((H,), jnp.float32), 'ln_b': jnp.zeros((H,), jnp.float32), 'wq': wq, 'wq_scale': wq_s, 'q_in_scale': jnp.full((H,), 0.05, jnp.float32), 'wqx': wqx, 'wqx_scale': wqx_s, 'qx_in_scale': jnp.full((H,), 0.05, jnp.float32), 'wk': wk, 'wk_scale': wk_s, 'k_in_scale': jnp.full((H,), 0.05, jnp.float32), 'wv': wv, 'wv_scale': wv_s, 'v_in_scale': jnp.full((H,), 0.05, jnp.float32), 'w_kv_x': jax.random.normal(ks[7], (2 * G * D, H), jnp.float32) * 0.02, 'qln_w': jnp.ones((D,), jnp.float32), 'qln_b': jnp.zeros((D,), jnp.float32), 'kln_w': jnp.ones((D,), jnp.float32), 'kln_b': jnp.zeros((D,), jnp.float32), 'qxln_w': jnp.ones((D,), jnp.float32), 'qxln_b': jnp.zeros((D,), jnp.float32), 'kxln_w': jnp.ones((D,), jnp.float32), 'kxln_b': jnp.zeros((D,), jnp.float32), 'wproj': wproj, 'proj_w_scale': wp_s, 'proj_in_scale': jnp.asarray(0.05, jnp.float32), 'proj_smooth': jnp.full((2 * NH * D,), 0.05, jnp.float32)}
    _L0_xattn_all = _L0_xattn_setup()
    _L0_xattn_in = {k: v for k, v in _L0_xattn_all.items() if k in ('ln_w', 'ln_b', 'wq', 'wq_scale', 'q_in_scale', 'wqx', 'wqx_scale', 'qx_in_scale', 'wk', 'wk_scale', 'k_in_scale', 'wv', 'wv_scale', 'v_in_scale', 'w_kv_x', 'qln_w', 'qln_b', 'kln_w', 'kln_b', 'qxln_w', 'qxln_b', 'kxln_w', 'kxln_b', 'wproj', 'proj_w_scale', 'proj_in_scale', 'proj_smooth')}
    del _L0_xattn_all

    def _L0_ffn_setup():
        import jax, jax.numpy as jnp
        import numpy as np
        B, S, H = (2, 256, 256)
        FFN = 128
        E = 8
        TOP_K = 2
        key = jax.random.key(seed)
        ks = jax.random.split(key, 5)
        scale = 0.02
        hidden_states = jax.random.normal(ks[0], (B, S, H), dtype=jnp.float32)
        Wg = jax.random.normal(ks[1], (E, H), dtype=jnp.float32) * scale
        W1 = jax.random.normal(ks[2], (E, FFN, H), dtype=jnp.float32) * scale
        W3 = jax.random.normal(ks[3], (E, FFN, H), dtype=jnp.float32) * scale
        W2 = jax.random.normal(ks[4], (E, H, FFN), dtype=jnp.float32) * scale
        bias = jnp.zeros((E,), dtype=jnp.float32)
        return {'hidden_states': hidden_states, 'Wg': Wg, 'W1': W1, 'W2': W2, 'W3': W3, 'bias': bias}
    _L0_ffn_all = _L0_ffn_setup()
    _L0_ffn_in = {k: v for k, v in _L0_ffn_all.items() if k in ('Wg', 'W1', 'W2', 'W3', 'bias')}
    del _L0_ffn_all

    def _L1_xattn_setup():
        import jax, jax.numpy as jnp
        import numpy as np
        DIM = 256
        NHEADS = 32
        HEAD_DIM = DIM // NHEADS
        EPS = 1e-06

        def _rmsnorm(t):
            return t * jax.lax.rsqrt(jnp.mean(t * t, axis=-1, keepdims=True) + EPS)
        key = jax.random.key(seed)
        kx, kc, kq, kk, kv = jax.random.split(key, 5)
        x = jax.random.normal(kx, (2, 512, DIM), dtype=jnp.float32)
        context = jax.random.normal(kc, (2, 64, DIM), dtype=jnp.float32)
        std = 0.02
        Wq = jax.random.normal(kq, (DIM, DIM), dtype=jnp.float32) * std
        Wk = jax.random.normal(kk, (DIM, DIM), dtype=jnp.float32) * std
        Wv = jax.random.normal(kv, (DIM, DIM), dtype=jnp.float32) * std
        return {'x': x, 'context': context, 'Wq': Wq, 'Wk': Wk, 'Wv': Wv}
    _L1_xattn_all = _L1_xattn_setup()
    _L1_xattn_in = {k: v for k, v in _L1_xattn_all.items() if k in ('Wq', 'Wk', 'Wv')}
    del _L1_xattn_all

    def _L1_ffn_setup():
        import jax, jax.numpy as jnp
        import numpy as np
        NBITS = 4
        OUT_F = 256
        IN_F = 256

        def _bit_ste(w, nbits):
            step = float(2 ** nbits - 1)
            w = jnp.clip(w, -1.0, 1.0)
            return jnp.round(jnp.abs(w) * step) / step * jnp.sign(w)
        key = jax.random.key(seed)
        ks = jax.random.split(key, 6)
        ex = np.arange(NBITS - 1, -1, -1)
        exps = jnp.asarray(2.0 ** ex / (2.0 ** NBITS - 1), dtype=jnp.float32)
        inp = {'input': jax.random.normal(ks[0], (8, 256, IN_F), dtype=jnp.float32), 'pweight': jax.random.normal(ks[1], (OUT_F, IN_F, NBITS), dtype=jnp.float32), 'nweight': jax.random.normal(ks[2], (OUT_F, IN_F, NBITS), dtype=jnp.float32), 'exps': exps, 'bexps': exps, 'mask_weight': jnp.ones((NBITS,), dtype=jnp.float32), 'scale': jnp.array([0.05], dtype=jnp.float32), 'pbias': jax.random.uniform(ks[3], (OUT_F, NBITS), dtype=jnp.float32, minval=0.0, maxval=float(2 ** NBITS - 1)) // 1.0 % 2.0, 'nbias': jax.random.uniform(ks[4], (OUT_F, NBITS), dtype=jnp.float32, minval=0.0, maxval=float(2 ** NBITS - 1)) // 1.0 % 2.0, 'biasscale': jnp.array([0.05], dtype=jnp.float32)}
        return inp
    _L1_ffn_all = _L1_ffn_setup()
    _L1_ffn_in = {k: v for k, v in _L1_ffn_all.items() if k in ('pweight', 'nweight', 'exps', 'bexps', 'mask_weight', 'scale', 'pbias', 'nbias', 'biasscale')}
    del _L1_ffn_all
    return {'x': x, 'ctx_2048': ctx_2048, 'g_xattn': g_xattn, 'g_ffn': g_ffn, 'L0_xattn_ln_w': _L0_xattn_in['ln_w'], 'L0_xattn_ln_b': _L0_xattn_in['ln_b'], 'L0_xattn_wq': _L0_xattn_in['wq'], 'L0_xattn_wq_scale': _L0_xattn_in['wq_scale'], 'L0_xattn_q_in_scale': _L0_xattn_in['q_in_scale'], 'L0_xattn_wqx': _L0_xattn_in['wqx'], 'L0_xattn_wqx_scale': _L0_xattn_in['wqx_scale'], 'L0_xattn_qx_in_scale': _L0_xattn_in['qx_in_scale'], 'L0_xattn_wk': _L0_xattn_in['wk'], 'L0_xattn_wk_scale': _L0_xattn_in['wk_scale'], 'L0_xattn_k_in_scale': _L0_xattn_in['k_in_scale'], 'L0_xattn_wv': _L0_xattn_in['wv'], 'L0_xattn_wv_scale': _L0_xattn_in['wv_scale'], 'L0_xattn_v_in_scale': _L0_xattn_in['v_in_scale'], 'L0_xattn_w_kv_x': _L0_xattn_in['w_kv_x'], 'L0_xattn_qln_w': _L0_xattn_in['qln_w'], 'L0_xattn_qln_b': _L0_xattn_in['qln_b'], 'L0_xattn_kln_w': _L0_xattn_in['kln_w'], 'L0_xattn_kln_b': _L0_xattn_in['kln_b'], 'L0_xattn_qxln_w': _L0_xattn_in['qxln_w'], 'L0_xattn_qxln_b': _L0_xattn_in['qxln_b'], 'L0_xattn_kxln_w': _L0_xattn_in['kxln_w'], 'L0_xattn_kxln_b': _L0_xattn_in['kxln_b'], 'L0_xattn_wproj': _L0_xattn_in['wproj'], 'L0_xattn_proj_w_scale': _L0_xattn_in['proj_w_scale'], 'L0_xattn_proj_in_scale': _L0_xattn_in['proj_in_scale'], 'L0_xattn_proj_smooth': _L0_xattn_in['proj_smooth'], 'L0_ffn_Wg': _L0_ffn_in['Wg'], 'L0_ffn_W1': _L0_ffn_in['W1'], 'L0_ffn_W2': _L0_ffn_in['W2'], 'L0_ffn_W3': _L0_ffn_in['W3'], 'L0_ffn_bias': _L0_ffn_in['bias'], 'L1_xattn_Wq': _L1_xattn_in['Wq'], 'L1_xattn_Wk': _L1_xattn_in['Wk'], 'L1_xattn_Wv': _L1_xattn_in['Wv'], 'L1_ffn_pweight': _L1_ffn_in['pweight'], 'L1_ffn_nweight': _L1_ffn_in['nweight'], 'L1_ffn_exps': _L1_ffn_in['exps'], 'L1_ffn_bexps': _L1_ffn_in['bexps'], 'L1_ffn_mask_weight': _L1_ffn_in['mask_weight'], 'L1_ffn_scale': _L1_ffn_in['scale'], 'L1_ffn_pbias': _L1_ffn_in['pbias'], 'L1_ffn_nbias': _L1_ffn_in['nbias'], 'L1_ffn_biasscale': _L1_ffn_in['biasscale']}

def reference(x, ctx_2048, g_xattn, g_ffn, L0_xattn_ln_w, L0_xattn_ln_b, L0_xattn_wq, L0_xattn_wq_scale, L0_xattn_q_in_scale, L0_xattn_wqx, L0_xattn_wqx_scale, L0_xattn_qx_in_scale, L0_xattn_wk, L0_xattn_wk_scale, L0_xattn_k_in_scale, L0_xattn_wv, L0_xattn_wv_scale, L0_xattn_v_in_scale, L0_xattn_w_kv_x, L0_xattn_qln_w, L0_xattn_qln_b, L0_xattn_kln_w, L0_xattn_kln_b, L0_xattn_qxln_w, L0_xattn_qxln_b, L0_xattn_kxln_w, L0_xattn_kxln_b, L0_xattn_wproj, L0_xattn_proj_w_scale, L0_xattn_proj_in_scale, L0_xattn_proj_smooth, L0_ffn_Wg, L0_ffn_W1, L0_ffn_W2, L0_ffn_W3, L0_ffn_bias, L1_xattn_Wq, L1_xattn_Wk, L1_xattn_Wv, L1_ffn_pweight, L1_ffn_nweight, L1_ffn_exps, L1_ffn_bexps, L1_ffn_mask_weight, L1_ffn_scale, L1_ffn_pbias, L1_ffn_nbias, L1_ffn_biasscale):
    import jax
    import jax.numpy as jnp

    def _L0_xattn_ref(hidden_states, cond, ln_w, ln_b, wq, wq_scale, q_in_scale, wqx, wqx_scale, qx_in_scale, wk, wk_scale, k_in_scale, wv, wv_scale, v_in_scale, w_kv_x, qln_w, qln_b, kln_w, kln_b, qxln_w, qxln_b, kxln_w, kxln_b, wproj, proj_w_scale, proj_in_scale, proj_smooth):
        import jax, jax.numpy as jnp
        import numpy as np
        FP8_MAX = 448.0
        EPS = 1e-05

        def _fp8_roundtrip(x):
            return x.astype(jnp.float8_e4m3fn).astype(jnp.float32)

        def _div_clamp_fp8(x, scale):
            y = jnp.clip(x.astype(jnp.float32) / scale, -FP8_MAX, FP8_MAX)
            y = y.astype(jnp.bfloat16).astype(jnp.float32)
            return _fp8_roundtrip(y)

        def _ln(x, w, b):
            mu = jnp.mean(x, axis=-1, keepdims=True)
            var = jnp.mean(jnp.square(x - mu), axis=-1, keepdims=True)
            return (x - mu) * jax.lax.rsqrt(var + EPS) * w + b

        def _fp8_linear_pertensor(x, wq, w_scale, in_scale):
            xq = _div_clamp_fp8(x, in_scale)
            return jnp.einsum('bsi,oi->bso', xq * in_scale, wq) * w_scale

        def _gqa(q, k, v):
            scale = 1.0 / np.sqrt(q.shape[-1])
            scores = jnp.einsum('bsghd,btgd->bghst', q, k) * scale
            p = jax.nn.softmax(scores, axis=-1)
            return jnp.einsum('bghst,btgd->bsghd', p, v)
        b, s, _ = hidden_states.shape
        sc = cond.shape[1]
        d = qln_w.shape[0]
        nh = wq.shape[0] // d
        g = wk.shape[0] // d
        hpg = nh // g
        ln_out = _ln(hidden_states, ln_w, ln_b)
        q = _fp8_linear_pertensor(ln_out, wq, wq_scale, q_in_scale).reshape(b, s, g, hpg, d)
        q = _ln(q, qln_w, qln_b)
        k = _fp8_linear_pertensor(ln_out, wk, wk_scale, k_in_scale).reshape(b, s, g, d)
        k = _ln(k, kln_w, kln_b)
        v = _fp8_linear_pertensor(ln_out, wv, wv_scale, v_in_scale).reshape(b, s, g, d)
        core = _gqa(q, k, v).reshape(b, s, nh * d)
        qx = _fp8_linear_pertensor(ln_out, wqx, wqx_scale, qx_in_scale).reshape(b, s, g, hpg, d)
        qx = _ln(qx, qxln_w, qxln_b)
        kvx = jnp.einsum('bsi,oi->bso', cond, w_kv_x)
        kx, vx = jnp.split(kvx, 2, axis=-1)
        kx = _ln(kx.reshape(b, sc, g, d), kxln_w, kxln_b)
        vx = vx.reshape(b, sc, g, d)
        xout = _gqa(qx, kx, vx).reshape(b, s, nh * d)
        cat = jnp.concatenate([core, xout], axis=-1)
        catq = _div_clamp_fp8(cat, proj_smooth)
        return jnp.einsum('bsi,oi->bso', catq, wproj) * (proj_in_scale * proj_w_scale)

    def _L0_ffn_ref(hidden_states, Wg, W1, W2, W3, bias):
        import jax, jax.numpy as jnp
        import numpy as np
        B, S, H = (2, 256, 256)
        FFN = 128
        E = 8
        TOP_K = 2
        bsz, seq_len, hidden_dim = hidden_states.shape
        x = hidden_states.reshape(-1, hidden_dim)
        router_logits = x @ Wg.T
        routing_weights = jax.nn.sigmoid(router_logits.astype(jnp.float32))
        scores = routing_weights + bias
        _, top_k_index = jax.lax.top_k(scores, TOP_K)
        top_k_weights = jnp.take_along_axis(routing_weights, top_k_index, axis=1)
        top_k_weights = top_k_weights / top_k_weights.sum(axis=-1, keepdims=True)
        top_k_weights = top_k_weights.astype(x.dtype)
        one_hot = jax.nn.one_hot(top_k_index, Wg.shape[0], dtype=x.dtype)
        expert_w = jnp.einsum('tk,tke->te', top_k_weights, one_hot)
        h1 = jnp.einsum('th,efh->tef', x, W1)
        h3 = jnp.einsum('th,efh->tef', x, W3)
        g = jax.nn.silu(h1) * h3 * expert_w[:, :, None]
        out = jnp.einsum('tef,ehf->th', g, W2)
        return out.reshape(bsz, seq_len, hidden_dim)

    def _L1_xattn_ref(x, context, Wq, Wk, Wv):
        import jax, jax.numpy as jnp
        import numpy as np
        DIM = 256
        NHEADS = 32
        HEAD_DIM = DIM // NHEADS
        EPS = 1e-06

        def _rmsnorm(t):
            return t * jax.lax.rsqrt(jnp.mean(t * t, axis=-1, keepdims=True) + EPS)
        b, n, _ = x.shape
        m = context.shape[1]
        q = x @ Wq.T
        k_raw = context @ Wk.T
        v_raw = context @ Wv.T
        q = q.reshape(b, n, NHEADS, HEAD_DIM).transpose(0, 2, 1, 3)
        kv = jnp.concatenate([k_raw, v_raw], axis=-1)
        kv = kv.reshape(b, m, NHEADS, HEAD_DIM, 2)
        k = kv[..., 0].transpose(0, 2, 1, 3)
        v = kv[..., 1].transpose(0, 2, 1, 3)
        q = _rmsnorm(q)
        k = _rmsnorm(k)
        scale = HEAD_DIM ** (-0.5)
        scores = jnp.einsum('bhnd,bhmd->bhnm', q, k) * scale
        attn = jax.nn.softmax(scores, axis=-1)
        out = jnp.einsum('bhnm,bhmd->bhnd', attn, v)
        return out.transpose(0, 2, 1, 3).reshape(b, n, NHEADS * HEAD_DIM)

    def _L1_ffn_ref(input, pweight, nweight, exps, bexps, mask_weight, scale, pbias, nbias, biasscale):
        import jax, jax.numpy as jnp
        import numpy as np
        NBITS = 4
        OUT_F = 256
        IN_F = 256

        def _bit_ste(w, nbits):
            step = float(2 ** nbits - 1)
            w = jnp.clip(w, -1.0, 1.0)
            return jnp.round(jnp.abs(w) * step) / step * jnp.sign(w)
        temp = 1.0
        mask = jax.nn.sigmoid(mask_weight)
        soft = jax.nn.sigmoid(temp * pweight) - jax.nn.sigmoid(temp * nweight)
        weight = jnp.einsum('oin,n->oi', soft, exps * mask) * scale[0]
        bias_raw = jnp.einsum('on,n->o', pbias - nbias, bexps)
        bias = _bit_ste(bias_raw, NBITS) * biasscale[0]
        return jnp.einsum('bsi,oi->bso', input, weight) + bias
    x = x + jnp.tanh(g_xattn[0]) * _L0_xattn_ref(_layernorm(x, axis=-1), ctx_2048, L0_xattn_ln_w, L0_xattn_ln_b, L0_xattn_wq, L0_xattn_wq_scale, L0_xattn_q_in_scale, L0_xattn_wqx, L0_xattn_wqx_scale, L0_xattn_qx_in_scale, L0_xattn_wk, L0_xattn_wk_scale, L0_xattn_k_in_scale, L0_xattn_wv, L0_xattn_wv_scale, L0_xattn_v_in_scale, L0_xattn_w_kv_x, L0_xattn_qln_w, L0_xattn_qln_b, L0_xattn_kln_w, L0_xattn_kln_b, L0_xattn_qxln_w, L0_xattn_qxln_b, L0_xattn_kxln_w, L0_xattn_kxln_b, L0_xattn_wproj, L0_xattn_proj_w_scale, L0_xattn_proj_in_scale, L0_xattn_proj_smooth)
    x = x + jnp.tanh(g_ffn[0]) * _L0_ffn_ref(_layernorm(x, axis=-1), L0_ffn_Wg, L0_ffn_W1, L0_ffn_W2, L0_ffn_W3, L0_ffn_bias)
    x = x + jnp.tanh(g_xattn[1]) * _L1_xattn_ref(_layernorm(x, axis=-1), ctx_2048, L1_xattn_Wq, L1_xattn_Wk, L1_xattn_Wv)
    x = x + jnp.tanh(g_ffn[1]) * _L1_ffn_ref(_layernorm(x, axis=-1), L1_ffn_pweight, L1_ffn_nweight, L1_ffn_exps, L1_ffn_bexps, L1_ffn_mask_weight, L1_ffn_scale, L1_ffn_pbias, L1_ffn_nbias, L1_ffn_biasscale)
    return x

_drawn_inputs = setup_inputs


def setup_inputs(seed=0):
    import zlib

    import numpy as np

    out = dict(_drawn_inputs(seed))
    spreads = {'g_ffn': (-1.0, 0.6),
     'L0_xattn_ln_w': (1.0, 0.6),
     'L0_xattn_ln_b': (0.0, 0.331),
     'L0_xattn_q_in_scale': (0.05000000074505806, 0.6),
     'L0_xattn_qx_in_scale': (0.05000000074505806, 0.6),
     'L0_xattn_k_in_scale': (0.05000000074505806, 0.6),
     'L0_xattn_v_in_scale': (0.05000000074505806, 0.6),
     'L0_xattn_qln_w': (1.0, 0.6),
     'L0_xattn_qln_b': (0.0, 0.8),
     'L0_xattn_kln_w': (1.0, 0.6),
     'L0_xattn_kln_b': (0.0, 2.0),
     'L0_xattn_qxln_w': (1.0, 0.6),
     'L0_xattn_qxln_b': (0.0, 0.8),
     'L0_xattn_kxln_w': (1.0, 0.6),
     'L0_xattn_kxln_b': (0.0, 2.0),
     'L0_xattn_proj_smooth': (0.05000000074505806, 0.6),
     'L0_ffn_bias': (0.0, 0.8),
     'L1_ffn_mask_weight': (1.0, 0.6)}
    factors = {'L0_ffn_Wg': 8.0,
     'L0_ffn_W1': 8.0,
     'L0_ffn_W2': 8.0,
     'L0_ffn_W3': 8.0,
     'L1_ffn_bexps': 33.747,
     'L1_ffn_pbias': 30.856,
     'L1_ffn_nbias': 32.099,
     'L1_xattn_Wq': 5.397,
     'L1_ffn_pweight': 3.779,
     'L1_ffn_nweight': 3.791,
     'L1_ffn_exps': 3.955}
    for name, (base, spread) in spreads.items():
        noise = np.random.default_rng([zlib.crc32(name.encode()), seed]).standard_normal(out[name].shape)
        drawn = base * np.exp(spread * noise) if base else spread * noise
        out[name] = jnp.asarray(drawn.astype(out[name].dtype))
    for name, factor in factors.items():
        out[name] = (out[name] * factor).astype(out[name].dtype)
    return out
```

```python
from contextlib import ExitStack

import concourse.bass as bass
from concourse import mybir

F32 = mybir.dt.float32
BF16 = mybir.dt.bfloat16
I16 = mybir.dt.int16
ALU = mybir.AluOpType
ACT = mybir.ActivationFunctionType
AX = mybir.AxisListType

P = 128
B, S, H = 4, 256, 256
SC = 1601
IC = H // P
NT = B * S // P
TB = S // P
D = 128
G = 8
HPG = 2
NQ = TB * HPG
KT = (SC + P - 1) // P
TAIL = SC - (KT - 1) * P
NGB = G * B
WCOLS = 2 * HPG * D + 4 * D
CQ, CQX, CK, CV, CKX = 0, 256, 512, 640, 768
STAGE = 2 * IC * SC + 4 * IC * S
FF, NE = 128, 8
NH1, D1 = 32, 8
NBITS = 4
FP8_MAX = 448.0
EPS5, EPS6 = 1e-5, 1e-6
ROUND_F8 = 1.5 * 2.0 ** 20
ROUND_INT = 1.5 * 2.0 ** 23

COLS = ["ln_w", "ln_b", "s_q", "s_qx", "s_k", "s_v"]
DCOLS = ["qln_w", "qln_b", "qxln_w", "qxln_b", "kln_w", "kln_b", "kxln_w", "kxln_b"]
SCAL = ["wq", "wqx", "wk", "wv", "pw", "pin", "gx0", "gx1", "gf0", "gf1", "scale", "bscale"]


class Token:

    def __init__(self, sem, n, region, back=0):
        self.sem, self.n, self.region, self.back = sem, n, region, back


class Carry:

    def __init__(self, region, name):
        self.region, self.name = region, name


class Program:

    ENGINES = ("pe", "act", "dve", "pool", "sp")

    def __init__(self, nc, ctx):
        self.nc, self.ctx = nc, ctx
        self.queue = {e: [] for e in self.ENGINES}
        self.sems, self.regions = {}, []
        self.left = {}
        for e in self.ENGINES[:4]:
            self.sems[e] = ctx.enter_context(nc.semaphore("done_" + e))
        self.straight()

    def stream(self, name):
        self.sems[name] = self.ctx.enter_context(self.nc.semaphore("dma_" + name))
        return name

    def straight(self):
        self._region(1)

    def loop(self, trips):
        self._region(trips)

    def _region(self, trips):
        self.regions.append({"trips": trips, "count": {}, "left": {}, "back": False})
        self.left = {}
        for e in self.ENGINES:
            self.queue[e].append(("region", len(self.regions) - 1))

    def carry(self, *names):
        r = len(self.regions) - 1
        for name in names:
            self.left[name] = [Carry(r, name)]
        self.regions[r]["left"] = self.left

    def leave(self, name, *tokens):
        self.left[name] = list(tokens)

    def of(self, *names):
        return [t for name in names for t in self.left.get(name, [])]

    def step(self, engine, fn, after=(), sem=None, signal=True, lone=False):
        sem = sem or engine
        inc = 1 if sem in self.ENGINES else 16
        tok = None
        if signal:
            r = self.regions[-1]
            r["count"][sem] = r["count"].get(sem, 0) + inc
            tok = Token(sem, r["count"][sem], len(self.regions) - 1)
        self.queue[engine].append(("step", fn, [t for t in after if t is not None], (sem, inc) if signal else None, lone))
        return tok

    def pe(self, fn, after=(), signal=False):
        return self.step("pe", fn, after, signal=signal)

    def act(self, fn, after=()):
        return self.step("act", fn, after)

    def dve(self, fn, after=(), lone=False):
        return self.step("dve", fn, after, lone=lone)

    def pool(self, fn, after=(), lone=False):
        return self.step("pool", fn, after, lone=lone)

    def dma(self, stream, fn, after=()):
        return self.step("sp", fn, after, sem=stream)

    def _resolve(self, tok, out, back=0):
        if isinstance(tok, Carry):
            r = self.regions[tok.region]
            for t in r["left"][tok.name]:
                if isinstance(t, Carry) and t.name == tok.name:
                    raise ValueError("nothing is left under " + tok.name)
                self._resolve(t, out, back + 1)
        else:
            out.append(Token(tok.sem, tok.n, tok.region, tok.back + back))

    def emit(self):
        base = {s: 0 for s in self.sems}
        for r in self.regions:
            primed = r["trips"] > 1
            r["base"] = dict(base)
            r["prime"] = {s: (r["count"].get(s, 0) if primed else 0) for s in self.sems}
            for s in base:
                base[s] += r["prime"][s] + r["trips"] * r["count"].get(s, 0)
        self.total = base
        block = self.ctx.enter_context(self.nc.Block())
        for name, dec in (("sp", block.sync), ("pool", block.gpsimd), ("dve", block.vector),
                          ("act", block.scalar), ("pe", block.tensor)):
            dec(self._emitter(name))

    def _emitter(self, name):
        def run(e):
            items = self.queue[name]
            parts, cur = [], None
            for it in items:
                if it[0] == "region":
                    cur = (it[1], [])
                    parts.append(cur)
                else:
                    cur[1].append(it)
            for ri, steps in parts:
                r = self.regions[ri]
                if ri:
                    for s, v in r["base"].items():
                        if v:
                            e.wait_ge(self.sems[s], v)
                if r["trips"] > 1:
                    for s, v in r["prime"].items():
                        owner = s if s in self.ENGINES else "sp"
                        if owner == name and v:
                            e.sem_inc(self.sems[s], v)
                    if steps:
                        with e.Fori(0, r["trips"], 1) as i:
                            self._steps(e, name, ri, steps, i)
                else:
                    self._steps(e, name, ri, steps, 0)
            for s, v in self.total.items():
                if s not in self.ENGINES and name == "sp" and v:
                    e.wait_ge(self.sems[s], v)
        return run

    def _steps(self, e, e_name, ri, steps, i):
        r = self.regions[ri]
        seen = {}
        for _, fn, after, sig, lone in steps:
            need = {}
            for tok in after:
                got = []
                self._resolve(tok, got)
                for t in got:
                    if t.region == ri:
                        v = t.n - t.back * r["count"].get(t.sem, 0)
                        need[t.sem] = max(need.get(t.sem, -10 ** 9), v)
            waited = False
            for s, v in need.items():
                if v <= seen.get(s, -10 ** 9):
                    continue
                seen[s] = v
                first = r["base"][s] + r["prime"][s] + v
                per = r["count"].get(s, 0)
                e.wait_ge(self.sems[s], i * per + first if r["trips"] > 1 else first)
                waited = True
            if lone and waited and r["trips"] > 1:
                e.nop(nofuse=True)
            self.i = i
            ins = fn(e)
            if sig:
                ins.then_inc(self.sems[sig[0]], sig[1])


def tensors(nc, ctx):
    def sb(name, shape, dt):
        return ctx.enter_context(nc.sbuf_tensor(name, shape, dt))

    def ps(name, shape, dt):
        return ctx.enter_context(nc.psum_tensor(name, shape, dt))

    return sb, ps


def round_fp8(pr, y, e, m, t, after, on_pool):
    add = pr.pool if on_pool else pr.dve
    a = pr.dve(lambda v: v.tensor_scalar(e.bitcast(I16), y.bitcast(I16), 0x7F80, None, ALU.bitwise_and), after)
    b = add(lambda v: v.tensor_scalar(m, e, 2.0 ** -6, ROUND_F8, ALU.max, ALU.mult), [a], lone=True)
    c = add(lambda v: v.tensor_tensor(t, y, m, ALU.add), [b])
    return add(lambda v: v.tensor_tensor(y, t, m, ALU.subtract), [c])


def layernorm_rows(pr, ci, x, out, st, mv, rs, mhalf, eps, tiles, after):
    for t in range(tiles):
        a = pr.dve(lambda v, t=t: v.bn_stats(st[:, t, :], x[:, t, :]), after)
    for t in range(tiles):
        a = pr.dve(lambda v, t=t: v.bn_aggr(mv[:, t, :], st[:, t, :]), [a])
    b = pr.pool(lambda v: v.tensor_scalar(rs[:, 0:tiles], mv[:, 0:tiles, 1], eps, None, ALU.add), [a])
    b = pr.pool(lambda v: v.tensor_tensor(rs[:, 0:tiles], rs[:, 0:tiles], mhalf[:, 0:tiles], ALU.pow), [b])
    for t in range(tiles):
        c = pr.dve(lambda v, t=t: v.tensor_scalar(out[:, t, :], x[:, t, :], mv[:, t, 0:1], rs[:, t:t + 1],
                                                  ALU.subtract, ALU.mult), [b])
    return c


def build(nc, A, out):
    whole = ExitStack()
    with whole:
        pr = Program(nc, whole)
        for s in ("x", "in", "ctx0", "ctx1", "ctxs0", "ctxs1", "w0", "w1", "ws0", "ws1", "xq0", "xq1", "ld0", "ld1", "wp0",
                  "wp1", "out", "row", "rsm0", "rsm1"):
            pr.stream(s)
        sb, ps = tensors(nc, whole)
        w_split = nc.dram_tensor("w_split", (G, P, 2 * IC * WCOLS), BF16, kind="Internal").ap()
        stage_d = nc.dram_tensor("stage_d", (B, P, STAGE), BF16, kind="Internal").ap()
        rsm_d = nc.dram_tensor("rsm_d", (P, 2 * G * HPG), F32, kind="Internal").ap()

        x = sb("x", [P, NT, H], F32)
        ident = sb("ident", [P, P], F32)
        identb = sb("identb", [P, P], BF16)
        mhalf = sb("mhalf", [P, 64], F32)
        cols = sb("cols", [P, len(COLS) * IC], F32)
        dcols = sb("dcols", [P, len(DCOLS)], F32)
        scal = sb("scal", [P, len(SCAL)], F32)
        gate = sb("gate", [P, 4], F32)
        st = sb("st", [P, NT, 6], F32)
        mv = sb("mv", [P, NT, 2], F32)
        rs = sb("rs", [P, NT], F32)
        col = lambda n, ic: cols[:, COLS.index(n) * IC + ic:COLS.index(n) * IC + ic + 1]
        dcol = lambda n: dcols[:, DCOLS.index(n):DCOLS.index(n) + 1]
        sc = lambda n: scal[:, SCAL.index(n):SCAL.index(n) + 1]

        score = ps("score", [P, 4 * 512], F32)
        tb = [ps("tb0", [P, 512], F32), ps("tb1", [P, 512], F32)]
        pv = ps("pv", [P, 512], F32)
        pa = ps("pa", [P, 512], F32)

        k = dict(nc=nc, pr=pr, A=A, out=out, x=x, ident=ident, identb=identb, mhalf=mhalf, col=col, dcol=dcol, sc=sc,
                 gate=gate, st=st, mv=mv, rs=rs, score=score, tb=tb, pv=pv, pa=pa, cols=cols, dcols=dcols,
                 scal=scal, w_split=w_split, stage_d=stage_d, rsm_d=rsm_d, sb=sb)
        attn = ExitStack()
        with attn:
            catq = tensors(nc, attn)[0]("catq", [P, (NGB + 1) * 2 * NQ * P], BF16)
            k.update(catq=catq)
            with ExitStack() as c0:
                prologue(k, tensors(nc, c0)[0])
            with ExitStack() as c1:
                layer0_attention(k, tensors(nc, c1)[0])
            with ExitStack() as c2:
                layer0_projection(k, tensors(nc, c2)[0])
        for stage in (layer0_ffn, layer1_attention, layer1_ffn):
            with ExitStack() as c:
                stage(k, tensors(nc, c)[0])
        pr.dma("out", lambda e: e.dma_start(out.rearrange("(t p) d -> p t d", p=P), x[:, :, :]), pr.of("x"))
        pr.emit()


def prologue(k, sb):
    pr, A, x = k["pr"], k["A"], k["x"]
    ident, identb, mhalf = k["ident"], k["identb"], k["mhalf"]
    col, sc, score, tb = k["col"], k["sc"], k["score"], k["tb"]
    st, mv, rs = k["st"], k["mv"], k["rs"]
    ld_x = pr.dma("x", lambda e: e.dma_start(x[:, :, :], A["x"].rearrange("(t p) d -> p t d", p=P)))
    pr.dma("in", lambda e: e.dma_start(k["cols"][:, :], A["cols"]))
    pr.dma("in", lambda e: e.dma_start(k["dcols"][:, :], A["dcols"]))
    pr.dma("in", lambda e: e.dma_start(k["scal"][:, :], A["scal"].partition_broadcast(P)))
    smc = sb("smc", [P, 2 * G * HPG], F32)
    rsmc = sb("rsmc", [P, 2 * G * HPG], F32)
    ld = pr.dma("in", lambda e: e.dma_start(smc[:, :], A["smooth"]))

    z = pr.pool(lambda e: e.memset(ident[:, :], 0.0))
    i = pr.pool(lambda e: e.affine_select(out=ident[:, :], in_=ident[:, :], compare_op=ALU.not_equal, fill=1.0,
                                          base=0, pattern=[[-1, P]], channel_multiplier=1), [z])
    pr.pool(lambda e: e.memset(mhalf[:, :], -0.5))
    ib = pr.dve(lambda e: e.tensor_copy(identb[:, :], ident[:, :]), [i])

    r = pr.dve(lambda e: e.reciprocal(rsmc[:, :], smc[:, :]), [ld])
    pr.dma("row", lambda e: e.dma_start(k["rsm_d"], rsmc[:, :]), [r])

    gate = k["gate"]
    g = pr.act(lambda e: e.activation(gate[:, :], k["scal"][:, SCAL.index("gx0"):SCAL.index("gx0") + 4], ACT.Tanh), [ld])
    g = pr.dve(lambda e: e.tensor_scalar(gate[:, 0:1], gate[:, 0:1], sc("pw"), sc("pin"), ALU.mult, ALU.mult), [g])
    for n in (0, 1, 2, 3):
        pr.dve(lambda e, n=n: e.tensor_scalar(k["dcols"][:, n:n + 1], k["dcols"][:, n:n + 1], float(D) ** -0.5, None,
                                              ALU.mult), [ld])

    rin = sb("rin", [P, 4 * IC], F32)
    win = sb("win", [P, 4 * IC], F32)
    kinds = (("q", "wq", CQ, 256), ("qx", "wqx", CQX, 256), ("k", "wk", CK, 128), ("v", "wv", CV, 128))
    for n, (kind, ws, _, _) in enumerate(kinds):
        wr = pr.dve(lambda e, n=n, kind=kind, ws=ws: e.tensor_scalar(
            win[:, n * IC:(n + 1) * IC], k["cols"][:, COLS.index("s_" + kind) * IC:(COLS.index("s_" + kind) + 1) * IC],
            sc(ws), None, ALU.mult), [ld])
    rr = pr.dve(lambda e: e.reciprocal(rin[:, :], k["cols"][:, 2 * IC:6 * IC]), [ld])
    wf = [sb(f"wf{i}", [P, IC, WCOLS], F32) for i in range(2)]
    wo = [sb(f"wo{i}", [P, 2, IC, WCOLS], BF16) for i in range(2)]
    free_f, free_o = [[], []], [[], []]
    for g in range(G):
        p = g % 2
        l = pr.dma(f"w{p}", lambda e, g=g, p=p: e.dma_start(wf[p][:, :, :], A["w_all"][g]), free_f[p])
        his, los = [], []
        for ic in range(IC):
            for n, (_, _, c0, nc_) in enumerate(kinds + ((None, None, CKX, 256),)):
                src = lambda p=p, ic=ic, c0=c0, nc_=nc_: wf[p][:, ic, c0:c0 + nc_]
                dst = lambda part, p=p, ic=ic, c0=c0, nc_=nc_: wo[p][:, part, ic, c0:c0 + nc_]
                if n < 4:
                    s = lambda n=n, ic=ic: win[:, n * IC + ic:n * IC + ic + 1]
                    h = pr.act(lambda e, s=s, src=src, dst=dst: e.activation(dst(0), src(), ACT.Copy, scale=s()),
                               [l, wr] + free_o[p])
                    lo = pr.dve(lambda e, s=s, src=src, dst=dst: e.scalar_tensor_tensor(
                        dst(1), src(), s(), dst(0), ALU.mult, ALU.subtract), [h])
                else:
                    h = pr.act(lambda e, src=src, dst=dst: e.copy(dst(0), src()), [l] + free_o[p])
                    lo = pr.pool(lambda e, src=src, dst=dst: e.tensor_tensor(dst(1), src(), dst(0), ALU.subtract), [h])
                his.append(h)
                los.append(lo)
        free_f[p] = [his[-1]] + los
        s = pr.dma(f"ws{p}", lambda e, g=g, p=p: e.dma_start(
            k["w_split"][g], wo[p][:, :, :, :].rearrange("p a b c -> p (a b c)")), los + [his[-1]])
        free_o[p] = [s]

    cf = [sb(f"cf{i}", [P, SC], F32) for i in range(2)]
    co = [sb(f"co{i}", [P, 2, SC], BF16) for i in range(2)]
    free_f, free_o = [[], []], [[], []]
    half = SC // 2
    for b in range(B):
        for ic in range(IC):
            p = ic % 2
            l = pr.dma(f"ctx{p}", lambda e, b=b, p=p, ic=ic: e.dma_start(cf[p][:, :], A["ctxT"][:, ic, b, :]), free_f[p])
            h = pr.act(lambda e, p=p: e.copy(co[p][:, 0, :], cf[p][:, :]), [l] + free_o[p])
            l1 = pr.dve(lambda e, p=p: e.tensor_tensor(co[p][:, 1, 0:half], cf[p][:, 0:half], co[p][:, 0, 0:half],
                                                       ALU.subtract), [h])
            l2 = pr.pool(lambda e, p=p: e.tensor_tensor(co[p][:, 1, half:], cf[p][:, half:], co[p][:, 0, half:],
                                                        ALU.subtract), [h])
            free_f[p] = [l1, l2]
            s = pr.dma(f"ctxs{p}", lambda e, b=b, p=p, ic=ic: e.dma_start(
                k["stage_d"][b, :, 0:2 * IC * SC].rearrange("p (a i s) -> p a i s", a=2, i=IC)[:, :, ic, :],
                co[p][:, :, :]), [l1, l2, h])
            free_o[p] = [s]

    xn = sb("xn", [P, NT, H], F32)
    xw = sb("xw", [P, IC, NT * P], F32)
    a = layernorm_rows(pr, 0, x, xn, st, mv, rs, mhalf, EPS5, NT, [ld_x])
    a = layernorm_rows(pr, 0, xn, xn, st, mv, rs, mhalf, EPS5, NT, [a])
    for ic in range(IC):
        for q in range(2):
            bank = score[:, (2 * ic + q) * 512:(2 * ic + q + 1) * 512]
            for t in range(4):
                tt = pr.pe(lambda e, bank=bank, t=t, q=q, ic=ic: e.transpose(
                    bank[:, t * P:(t + 1) * P], xn[:, 4 * q + t, ic * P:(ic + 1) * P], ident[:, :]), [a, i, ib],
                    signal=(t == 3))
            w = pr.dve(lambda e, bank=bank, q=q, ic=ic: e.tensor_scalar(
                xw[:, ic, q * 512:(q + 1) * 512], bank, col("ln_w", ic), col("ln_b", ic), ALU.mult, ALU.add), [tt])
    y32 = sb("y32", [P, IC, NT * P], F32)
    xq = [sb(f"xq{i}", [P, IC, NT * P], BF16) for i in range(2)]
    ex = sb("ex", [P, IC, NT * P], BF16)
    m = sb("m", [P, IC, NT * P], F32)
    free = [[], []]
    for n in range(4):
        p = n % 2
        for ic in range(IC):
            w = pr.dve(lambda e, n=n, ic=ic: e.tensor_scalar(
                y32[:, ic, :], xw[:, ic, :], rin[:, n * IC + ic:n * IC + ic + 1], FP8_MAX, ALU.mult, ALU.min), [w, rr])
        w = pr.dve(lambda e, p=p: e.tensor_scalar(xq[p][:, :, :], y32[:, :, :], -FP8_MAX, None, ALU.max),
                   [w] + free[p])
        w = round_fp8(pr, xq[p][:, :, :], ex[:, :, :], m[:, :, :], y32[:, :, :], [w], False)
        for b in range(B):
            s = pr.dma(f"xq{p}", lambda e, n=n, b=b, p=p: e.dma_start(
                k["stage_d"][b, :, 2 * IC * SC + n * IC * S:2 * IC * SC + (n + 1) * IC * S].rearrange(
                    "p (i s) -> p i s", i=IC), xq[p][:, :, b * S:(b + 1) * S]), [w])
        free[p] = [s]
    for t in tb:
        pr.dve(lambda e, t=t: e.memset(t[:, :], 0.0))


def layer0_attention(k, sb):
    pr, A = k["pr"], k["A"]
    ident, identb, mhalf, dcol = k["ident"], k["identb"], k["mhalf"], k["dcol"]
    score, tb, pv, pa, catq = k["score"], k["tb"], k["pv"], k["pa"], k["catq"]
    rsm = [sb(f"rsm{i}", [P, 2 * HPG * D], F32) for i in range(2)]
    stage = [sb(f"stage{i}", [P, STAGE], BF16) for i in range(2)]
    wsb = [sb(f"wsb{i}", [P, 2, IC, WCOLS], BF16) for i in range(2)]
    QT = [sb(f"QT{i}", [P, 2, 2, NQ * P], BF16) for i in range(2)]
    KS = [sb(f"KS{i}", [P, 2, S], BF16) for i in range(2)]
    VS = [sb(f"VS{i}", [P, 2, TB, D], BF16) for i in range(2)]
    KX = [sb(f"KX{i}", [P, 2, SC], BF16) for i in range(2)]
    VX = [sb(f"VX{i}", [P, 2, KT, D], BF16) for i in range(2)]
    NP_ = SC + S
    P32 = [sb(f"P32_{i}", [P, NP_], F32) for i in range(2)]
    PT = [sb(f"PT{i}", [P, 2, 512], BF16) for i in range(2)]
    kn = [sb(f"kn{i}", [P, 512], F32) for i in range(2)]
    t32 = [sb(f"t32_{i}", [P, 512], F32) for i in range(2)]
    st, mv, rs = (sb("a_st", [P, 4, 6], F32), sb("a_mv", [P, 4, 2], F32), sb("a_rs", [P, 4], F32))
    mxp = [sb(f"mxp{i}", [P, 2], F32) for i in range(2)]
    nmx = [sb(f"nmx{i}", [P, 2], F32) for i in range(2)]
    sums = [sb(f"sums{i}", [P, 4], F32) for i in range(2)]
    rsum = [sb(f"rsum{i}", [P, 2], F32) for i in range(2)]
    Y = sb("Y", [P, 2, TB, HPG, D], F32)
    yq = sb("yq", [P, 2 * NQ * P], BF16)
    ye = sb("ye", [P, 2 * NQ * P], BF16)
    ym = sb("ym", [P, NQ * P], F32)
    yt = sb("yt", [P, NQ * P], F32)

    def ctx_op(p, part, ic, a, b):
        o = (part * IC + ic) * SC
        return stage[p][:, o + a:o + b]

    def xq_op(p, kind, ic, a, b):
        o = 2 * IC * SC + (kind * IC + ic) * S
        return stage[p][:, o + a:o + b]

    turn = {"tb": 0, "kn": 0, "t32": 0}

    def next_of(name, n=2):
        i = turn[name]
        turn[name] = (i + 1) % n
        return i

    def load(p, n):
        after = pr.of(f"A_done{p}")
        grp = (lambda: n(pr.i) // B % G)
        bat = (lambda: n(pr.i) % B)
        a = pr.dma(f"ld{p}", lambda e: e.dma_start(
            stage[p][:, :].rearrange("p (o c) -> p o c", o=1),
            k["stage_d"][bass.ds(bat(), 1), :, :].rearrange("o p c -> p o c")), after)
        b = pr.dma(f"ld{p}", lambda e: e.dma_start(
            wsb[p][:, :, :, :].rearrange("p a b c -> p (a b c)").rearrange("p (o c) -> p o c", o=1),
            k["w_split"][bass.ds(grp(), 1), :, :].rearrange("o p c -> p o c")), after)
        pr.leave(f"loaded{p}", a, b)

    def load_rsm(p, n):
        a = pr.dma(f"rsm{p}", lambda e: e.dma_start(
            rsm[p][:, :], k["rsm_d"].rearrange("(g c) f -> g (c f)", g=G)[
                bass.ds(n(pr.i) // B % G, 1), :].partition_broadcast(P)), pr.of(f"finished{p}"))
        pr.leave(f"rsm{p}", a)

    def normalise(p, blocks, stride, rows, ready, eps):
        s = ready
        for j in range(blocks):
            s = pr.dve(lambda e, j=j: e.bn_stats(st[0:rows, j, :], pa[0:rows, j * stride:j * stride + D]), [s])
        for j in range(blocks):
            s = pr.dve(lambda e, j=j: e.bn_aggr(mv[0:rows, j, :], st[0:rows, j, :]), [s], lone=True)
        r = pr.pool(lambda e: e.tensor_scalar(rs[0:rows, 0:blocks], mv[0:rows, 0:blocks, 1], eps, None, ALU.add), [s], lone=True)
        r = pr.pool(lambda e: e.tensor_tensor(rs[0:rows, 0:blocks], rs[0:rows, 0:blocks], mhalf[0:rows, 0:blocks],
                                              ALU.pow), [r])
        b = next_of("kn")
        for j in range(blocks):
            n = pr.dve(lambda e, j=j, b=b: e.tensor_scalar(
                kn[b][0:rows, j * D:(j + 1) * D], pa[0:rows, j * stride:j * stride + D], mv[0:rows, j, 0:1],
                rs[0:rows, j:j + 1], ALU.subtract, ALU.mult), [r] + pr.of(f"kn{b}"))
        return b, n

    def to_parts(b, blocks, rows, ready, w, bias, hi, lo, dst_free):
        t = next_of("tb")
        width = (blocks - 1) * P + rows
        for j in range(blocks):
            tt = pr.pe(lambda e, j=j: e.transpose(tb[t][:, j * P:j * P + rows], kn[b][0:rows, j * D:(j + 1) * D],
                                                  ident[0:rows, 0:rows]),
                       [ready] + pr.of(f"tb{t}"), signal=(j == blocks - 1))
        pr.leave(f"kn{b}", tt)
        c = next_of("t32")
        a = pr.dve(lambda e: e.tensor_scalar(t32[c][:, 0:width], tb[t][:, 0:width], dcol(w), dcol(bias),
                                             ALU.mult, ALU.add), [tt] + pr.of(f"t32{c}"))
        pr.leave(f"tb{t}", a)
        h = pr.pool(lambda e: e.tensor_copy(hi(), t32[c][:, 0:width]), [a] + dst_free, lone=True)
        l = pr.pool(lambda e: e.tensor_tensor(lo(), t32[c][:, 0:width], hi(), ALU.subtract), [h])
        pr.leave(f"t32{c}", l)
        return l

    def stage_a(p):
        outs = []
        for kind, c0 in ((0, CQ), (1, CQX)):
            for tt in range(TB):
                for n, (ic, part) in enumerate((i, j) for i in range(IC) for j in range(2)):
                    r = pr.pe(lambda e, tt=tt, ic=ic, part=part, n=n, kind=kind, c0=c0: e.matmul(
                        pa[:, tt * 256:(tt + 1) * 256], xq_op(p, kind, ic, tt * P, (tt + 1) * P),
                        wsb[p][:, part, ic, c0:c0 + 256], start=(n == 0), stop=(n == 3)),
                        pr.of("pa", f"loaded{p}"), signal=(tt == TB - 1 and n == 3))
            b, n = normalise(p, 4, D, P, r, EPS5)
            pr.leave("pa", n)
            yield
            w, bias = (("qln_w", "qln_b"), ("qxln_w", "qxln_b"))[kind]
            outs.append(to_parts(b, 4, P, n, w, bias, lambda kind=kind: QT[p][:, kind, 0, :],
                                 lambda kind=kind: QT[p][:, kind, 1, :], pr.of(f"QK_read{p}")))
            yield
        for kind, c0, at in ((2, CK, 0), (3, CV, 256)):
            for tt in range(TB):
                for n, (ic, part) in enumerate((i, j) for i in range(IC) for j in range(2)):
                    r = pr.pe(lambda e, tt=tt, ic=ic, part=part, n=n, kind=kind, c0=c0, at=at: e.matmul(
                        pa[:, at + tt * P:at + (tt + 1) * P], xq_op(p, kind, ic, tt * P, (tt + 1) * P),
                        wsb[p][:, part, ic, c0:c0 + D], start=(n == 0), stop=(n == 3)),
                        pr.of("pa"), signal=(kind == 3 and tt == TB - 1 and n == 3))
        vh = pr.act(lambda e: e.copy(VS[p][:, 0, :, :].rearrange("p a d -> p (a d)"), pa[:, 256:512]),
                    [r] + pr.of(f"V_read{p}"))
        vl = pr.dve(lambda e: e.tensor_tensor(VS[p][:, 1, :, :].rearrange("p a d -> p (a d)"), pa[:, 256:512],
                                              VS[p][:, 0, :, :].rearrange("p a d -> p (a d)"), ALU.subtract), [vh])
        b, n = normalise(p, 2, D, P, vl, EPS5)
        pr.leave("pa", n)
        outs += [vl]
        yield
        outs.append(to_parts(b, 2, P, n, "kln_w", "kln_b", lambda: KS[p][:, 0, :], lambda: KS[p][:, 1, :],
                             pr.of(f"QK_read{p}")))
        yield
        for c in range(0, KT, 2):
            tiles = [t for t in (c, c + 1) if t < KT]
            rows = P if c + 1 < KT else TAIL
            for s, t in enumerate(tiles):
                passes = [(ic, a, w) for ic in range(IC) for a, w in ((0, 0), (0, 1), (1, 0))]
                for n, (ic, a, w) in enumerate(passes):
                    r = pr.pe(lambda e, s=s, t=t, n=n, ic=ic, a=a, w=w, rows=rows: e.matmul(
                        pa[0:rows, s * 256:(s + 1) * 256], ctx_op(p, a, ic, t * P, t * P + rows),
                        wsb[p][:, w, ic, CKX:CKX + 256], start=(n == 0), stop=(n == 5)),
                        pr.of("pa"), signal=(t == tiles[-1] and n == 5))
            k2 = len(tiles)
            src = lambda rows=rows, k2=k2: pa[0:rows, 0:k2 * 256].rearrange("p (s c) -> p s c", s=k2)[:, :, D:2 * D]
            vdst = lambda part, rows=rows, k2=k2, c=c: VX[p][0:rows, part, c:c + k2, :]
            vh = pr.act(lambda e, src=src, vdst=vdst: e.copy(vdst(0), src()), [r] + pr.of(f"V_read{p}"))
            vl = pr.dve(lambda e, src=src, vdst=vdst: e.tensor_tensor(vdst(1), src(), vdst(0), ALU.subtract), [vh])
            outs.append(vl)
            b, n = normalise(p, k2, 256, rows, vl, EPS5)
            pr.leave("pa", n)
            yield
            at = c * P
            width = (k2 - 1) * P + rows
            outs.append(to_parts(b, k2, rows, n, "kxln_w", "kxln_b",
                                 lambda at=at, width=width: KX[p][:, 0, at:at + width],
                                 lambda at=at, width=width: KX[p][:, 1, at:at + width], pr.of(f"QK_read{p}")))
            yield
        pr.leave(f"A_done{p}", r)
        pr.leave(f"ready{p}", *outs)

    SELF0 = 3 * 512 + P
    BANKS = [[(1, 0, 512, 0)], [(1, 512, 1024, 512)], [(1, 1024, 1536, 1024)],
             [(1, 1536, SC, 1536), (0, 0, S, SELF0)]]
    SPLITX = 1024

    def scores(p, q, par, bank):
        free = {0: "expA", 1: "expA", 2: "expB", 3: "expS"}[bank]
        for kind, a, b, at in BANKS[bank]:
            keys = KX[p] if kind else KS[p]
            for n, (qp, kp) in enumerate(((0, 0), (0, 1), (1, 0))):
                last = (kind, n) == (BANKS[bank][-1][0], 2)
                t = pr.pe(lambda e, kind=kind, a=a, b=b, at=at, keys=keys, n=n, qp=qp, kp=kp: e.matmul(
                    score[:, at:at + b - a], QT[p][:, kind, qp, q * P:(q + 1) * P], keys[:, kp, a:b],
                    start=(n == 0), stop=(n == 2)), pr.of(free, f"ready{p}"), signal=last)
        pr.leave(f"bank{bank}", t)
        if bank == 3:
            pr.leave(f"QK_read{p}", t)

    def max_a(par):
        t = pr.dve(lambda e: e.tensor_reduce(mxp[par][:, 0:1], score[:, 0:SPLITX], AX.X, ALU.max),
                   pr.of("bank0", "bank1"))

    def max_b(par):
        pr.dve(lambda e: e.tensor_reduce(nmx[par][:, 1:2], score[:, SELF0:SELF0 + S], AX.X, ALU.max, negate=True),
               pr.of("bank3", f"exp{par}"))
        t = pr.dve(lambda e: e.tensor_reduce(mxp[par][:, 1:2], score[:, SPLITX:SC], AX.X, ALU.max), pr.of("bank2"))
        t = pr.dve(lambda e: e.tensor_reduce(nmx[par][:, 0:1], mxp[par][:, :], AX.X, ALU.max, negate=True), [t])
        pr.leave("negmax", t)

    def exps(par):
        w = pr.of("negmax", f"P_read{par}", f"sum_read{par}")
        a = pr.act(lambda e: e.activation(P32[par][:, 0:SPLITX], score[:, 0:SPLITX], ACT.Exp,
                                          bias=nmx[par][:, 0:1], accum_out=sums[par][:, 0:1]), w)
        b = pr.act(lambda e: e.activation(P32[par][:, SPLITX:SC], score[:, SPLITX:SC], ACT.Exp,
                                          bias=nmx[par][:, 0:1], accum_out=sums[par][:, 1:2]), w)
        c = pr.act(lambda e: e.activation(P32[par][:, SC:SC + S], score[:, SELF0:SELF0 + S], ACT.Exp,
                                          bias=nmx[par][:, 1:2], accum_out=sums[par][:, 2:3]), w)
        pr.leave("expA", a)
        pr.leave("expB", b)
        pr.leave("expS", c)
        pr.leave(f"exp{par}", a, b, c)

    CHUNKS = [(1, t, t * P, P if t < KT - 1 else TAIL) for t in range(KT)] + [(0, t, SC + t * P, P) for t in range(TB)]
    GROUPS = [CHUNKS[0:4], CHUNKS[4:8], CHUNKS[8:12], CHUNKS[12:15]]
    group = {}

    def turn_p(par, g):
        t = next_of("tb")
        chunks = GROUPS[g]
        for j, (_, _, at, keys) in enumerate(chunks):
            tt = pr.pe(lambda e, j=j, at=at, keys=keys: e.transpose(
                tb[t][0:keys, j * P:(j + 1) * P], P32[par][:, at:at + keys], ident[:, :]),
                pr.of(f"exp{par}", f"tb{t}"), signal=(j == len(chunks) - 1))
        if g == len(GROUPS) - 1:
            pr.leave(f"P_read{par}", tt)
        pt, w = g % 2, len(chunks) * P
        h = pr.act(lambda e: e.copy(PT[pt][:, 0, 0:w], tb[t][:, 0:w]), [tt] + pr.of(f"PT{pt}"))
        l = pr.dve(lambda e: e.tensor_tensor(PT[pt][:, 1, 0:w], tb[t][:, 0:w], PT[pt][:, 0, 0:w], ALU.subtract), [h])
        pr.leave(f"tb{t}", l)
        group[g] = l

    def times_v(vp, par, q, g):
        pt = g % 2
        for j, (kind, t, _, keys) in enumerate(GROUPS[g]):
            V = VX[vp] if kind else VS[vp]
            at = P if kind else 0
            lastt = KT - 1 if kind else TB - 1
            for n, (a, v) in enumerate(((0, 0), (0, 1), (1, 0))):
                m = pr.pe(lambda e, j=j, t=t, keys=keys, V=V, at=at, n=n, a=a, v=v, lastt=lastt: e.matmul(
                    pv[:, at:at + D], PT[pt][0:keys, a, j * P:(j + 1) * P], V[0:keys, v, t, :],
                    start=(t == 0 and n == 0), stop=(t == lastt and n == 2)),
                    [group[g]] + pr.of("pv"), signal=(j == len(GROUPS[g]) - 1 and n == 2))
        pr.leave(f"PT{pt}", m)
        if g == len(GROUPS) - 1:
            pr.leave("pv_full", m)
            pr.leave(f"V_read{vp}", m)

    def finish(vp, par, q):
        tt, h = q // HPG, q % HPG
        a = pr.dve(lambda e: e.tensor_tensor(sums[par][:, 3:4], sums[par][:, 0:1], sums[par][:, 1:2], ALU.add),
                   pr.of(f"exp{par}"))
        a = pr.dve(lambda e: e.reciprocal(rsum[par][:, :], sums[par][:, 2:4]), [a])
        pr.leave(f"sum_read{par}", a)
        for x_ in range(2):
            a = pr.dve(lambda e, x_=x_: e.scalar_tensor_tensor(
                Y[:, x_, tt, h, :], pv[:, x_ * P:(x_ + 1) * P], rsum[par][:, x_:x_ + 1],
                rsm[vp][:, (x_ * HPG + h) * D:(x_ * HPG + h + 1) * D], ALU.mult, ALU.mult),
                [a] + pr.of("pv_full", "Y_read", f"rsm{vp}"))
        pr.leave("pv", a)
        if q == NQ - 1:
            pr.leave("Y", a)
            pr.leave(f"finished{vp}", a)

    def quantise():
        a = pr.pool(lambda e: e.tensor_scalar(yq[:, :], Y[:, :, :, :, :].rearrange("p a b c d -> p (a b c d)"),
                                              FP8_MAX, -FP8_MAX, ALU.min, ALU.max), pr.of("Y", "yq_read"), lone=True)
        pr.leave("Y_read", a)
        for h in range(2):
            part = slice(h * NQ * P, (h + 1) * NQ * P)
            a = round_fp8(pr, yq[:, part], ye[:, part], ym[:, :], yt[:, :], [a], True)
        pr.leave("yq", a)

    def turn_y(slot):
        t = next_of("tb")
        bank = tb[t][:, :].bitcast(BF16)
        for j in range(2 * NQ):
            m = pr.pe(lambda e, j=j: e.transpose(bank[:, j * P:(j + 1) * P], yq[:, j * P:(j + 1) * P], identb[:, :]),
                      pr.of("yq", f"tb{t}"), signal=(j == 2 * NQ - 1))
        pr.leave("yq_read", m)
        c = pr.dve(lambda e: e.tensor_copy(catq[:, bass.ds(slot(pr.i) * (2 * NQ * P), 2 * NQ * P)], bank), [m])
        pr.leave(f"tb{t}", c)

    def advance(gen, n):
        for _ in range(n):
            next(gen, None)

    def block(kk, gen, slot, nxt):
        p, q, par = kk // NQ % 2, kk % NQ, kk % 2
        lk = (kk - 1) % (2 * NQ)
        lp, lq, lpar = lk // NQ, lk % NQ, lk % 2
        turn_p(lpar, 0)
        scores(p, q, par, 0)
        turn_p(lpar, 1)
        scores(p, q, par, 1)
        max_a(par)
        times_v(lp, lpar, lq, 0)
        advance(gen, 2)
        scores(p, q, par, 2)
        scores(p, q, par, 3)
        max_b(par)
        turn_p(lpar, 2)
        times_v(lp, lpar, lq, 1)
        turn_p(lpar, 3)
        exps(par)
        advance(gen, 2)
        times_v(lp, lpar, lq, 2)
        times_v(lp, lpar, lq, 3)
        finish(lp, lpar, lq)
        advance(gen, 1)
        if q == 0:
            quantise()
            load_rsm(lp, nxt)
        if q == 2:
            turn_y(slot)

    pr.straight()
    for t in P32[1:] + sums[1:]:
        pr.pool(lambda e, t=t: e.memset(t[:, :], 1.0))
    pr.pool(lambda e: e.memset(Y[:, :, :, :, :], 1.0))
    for t in (VX[1], VS[1]):
        pr.pool(lambda e, t=t: e.memset(t[:, :, :, :], 1.0))
    load(0, lambda i: 0)
    load(1, lambda i: 1)
    load_rsm(0, lambda i: 0)
    load_rsm(1, lambda i: 0)
    gen = stage_a(0)
    advance(gen, 99)

    def names():
        return (["Y", "Y_read", "pa", "pv", "pv_full", "expA", "expB", "expS", "negmax", "yq", "yq_read", "tb0", "tb1", "kn0", "kn1",
                 "t320", "t321", "PT0", "PT1"]
                + [f"{n}{p}" for p in range(2) for n in ("A_done", "loaded", "ready", "QK_read", "V_read", "exp",
                                                         "P_read", "sum_read", "rsm", "finished")])

    pr.loop(NGB // 2)
    pr.carry(*names())
    for half in range(2):
        if half == 0:
            load(0, lambda i: i * 2 + 2)
        gen = stage_a(1 - half)
        for q in range(NQ):
            block(half * NQ + q, gen, lambda i, half=half: i * 2 + half, lambda i, half=half: i * 2 + half + 1)
        advance(gen, 99)
        if half == 0:
            load(1, lambda i: i * 2 + 3)
    pr.straight()
    turn.update(tb=0)
    for g in range(4):
        turn_p(1, g)
        times_v(1, 1, NQ - 1, g)
    finish(1, 1, NQ - 1)
    quantise()
    turn_y(lambda i: NGB)


def layer0_projection(k, sb):
    pr, A, x, catq, gate = k["pr"], k["A"], k["x"], k["catq"], k["gate"]
    score = k["score"]
    NCH = 2 * G * HPG
    wf = [sb(f"wpf{i}", [P, 8, H], F32) for i in range(2)]
    wp = sb("wp", [P, 2, NCH, H], BF16)
    free = [[], []]
    pr.straight()
    los = []
    for c in range(0, NCH, 8):
        p = c // 8 % 2
        l = pr.dma(f"wp{p}", lambda e, c=c, p=p: e.dma_start(wf[p][:, :, :], A["wprojT"][:, c:c + 8, :]), free[p])
        h = pr.act(lambda e, c=c, p=p: e.copy(wp[:, 0, c:c + 8, :], wf[p][:, :, :]), [l])
        lo = pr.dve(lambda e, c=c, p=p: e.tensor_tensor(wp[:, 1, c:c + 8, :], wf[p][:, :, :], wp[:, 0, c:c + 8, :],
                                                        ALU.subtract), [h])
        free[p] = [lo]
        los.append(lo)
    done = [[], [], [], []]
    for t in range(NT):
        b, tt, bank = t // TB, t % TB, t % 4
        acc = score[:, bank * 512:bank * 512 + H]
        n = 0
        for g in range(G):
            for x_ in range(2):
                for h in range(HPG):
                    at = ((g * B + b + 1) * 2 * NQ + (x_ * TB + tt) * HPG + h) * P
                    chunk = (g * 2 + x_) * HPG + h
                    for part in range(2):
                        m = pr.pe(lambda e, acc=acc, at=at, chunk=chunk, part=part, n=n: e.matmul(
                            acc, catq[:, at:at + P], wp[:, part, chunk, :], start=(n == 0), stop=(n == 2 * NCH - 1)),
                            los[chunk // 8:chunk // 8 + 1] + done[bank], signal=(n == 2 * NCH - 1))
                        n += 1
        d = pr.dve(lambda e, acc=acc, t=t: e.scalar_tensor_tensor(x[:, t, :], acc, gate[:, 0:1], x[:, t, :],
                                                                  ALU.mult, ALU.add), [m])
        done[bank] = [d]
        pr.leave("x", d)


def split(pr, src, hi, lo, after, hi_free=()):
    h = pr.act(lambda e: e.copy(hi, src), list(after) + list(hi_free))
    return pr.dve(lambda e: e.tensor_tensor(lo, src, hi, ALU.subtract), [h])


def norm_transposed(k, sb, name, eps, want32=False):
    pr, x, ident, score = k["pr"], k["x"], k["ident"], k["score"]
    xn = sb(name + "_xn", [P, NT, H], F32)
    xT = sb(name + "_xT", [P, 2, IC, NT * P], BF16)
    x32 = sb(name + "_x32", [P, IC, NT * P], F32) if want32 else None
    a = layernorm_rows(pr, 0, x, xn, k["st"], k["mv"], k["rs"], k["mhalf"], eps, NT, [])
    outs = []
    for ic in range(IC):
        for q in range(2):
            bank = score[:, (2 * ic + q) * 512:(2 * ic + q + 1) * 512]
            cols = slice(q * 512, (q + 1) * 512)
            for t in range(4):
                tt = pr.pe(lambda e, bank=bank, t=t, q=q, ic=ic: e.transpose(
                    bank[:, t * P:(t + 1) * P], xn[:, 4 * q + t, ic * P:(ic + 1) * P], ident[:, :]), [a],
                    signal=(t == 3))
            w = split(pr, bank, xT[:, 0, ic, cols], xT[:, 1, ic, cols], [tt])
            if want32:
                w = pr.act(lambda e, bank=bank, ic=ic, cols=cols: e.copy(x32[:, ic, cols], bank), [w])
            outs.append(w)
    return xT, x32, outs


THREE = ((0, 0), (0, 1), (1, 0))


def layer0_ffn(k, sb):
    pr, A, x, gate, ident = k["pr"], k["A"], k["x"], k["gate"], k["ident"]
    score, tb, pv, pa = k["score"], k["tb"], k["pv"], k["pa"]
    pr.straight()
    wg = sb("wg", [P, IC, NE], F32)
    brow = sb("brow", [P, NE], F32)
    ld = pr.dma("in", lambda e: e.dma_start(wg[:, :, :], A["wgT"]))
    ld = pr.dma("in", lambda e: e.dma_start(brow[:, :], A["ffn_bias"].partition_broadcast(P)))
    w13f = [sb(f"w13f{i}", [P, IC, NE * FF], F32) for i in range(2)]
    w2f = sb("w2f", [P, NE, H], F32)
    w13 = sb("w13", [P, 2, 2, IC, NE * FF], BF16)
    w2 = sb("w2", [P, 2, NE, H], BF16)
    wr = []
    for i, n in enumerate(("w1T", "w3T")):
        l = pr.dma(f"w{i}", lambda e, i=i, n=n: e.dma_start(w13f[i][:, :, :], A[n]))
        wr.append(split(pr, w13f[i][:, :, :], w13[:, i, 0, :, :], w13[:, i, 1, :, :], [l]))
    l = pr.dma("ws0", lambda e: e.dma_start(w2f[:, :, :], A["w2T"]))
    w2r = split(pr, w2f[:, :, :], w2[:, 0, :, :], w2[:, 1, :, :], [l])
    xT, x32, ready = norm_transposed(k, sb, "f", EPS5, want32=True)

    lg = pv[:, 0:NT * NE]
    for t in range(NT):
        for ic in range(IC):
            m = pr.pe(lambda e, t=t, ic=ic: e.matmul(lg[:, t * NE:(t + 1) * NE], x32[:, ic, t * P:(t + 1) * P],
                                                     wg[:, ic, :], start=(ic == 0), stop=(ic == IC - 1)),
                      ready + [ld], signal=(t == NT - 1 and ic == IC - 1))
    small = lambda n: sb(n, [P, NT, NE], F32)
    ex, sig, s1, eq, key, oh, oh2, ew = (small("r_" + n) for n in ("ex", "sig", "s1", "eq", "key", "oh", "oh2", "ew"))
    rank = small("r_rank")
    mx = sb("r_mx", [P, NT], F32)
    for e_ in range(NE):
        rk = pr.pool(lambda e, e_=e_: e.memset(rank[:, :, e_:e_ + 1], float(NE - e_)))
    bc = lambda ap: ap.unsqueeze(2).broadcast_to([P, NT, NE])
    a = pr.act(lambda e: e.activation(ex[:, :, :].rearrange("p a b -> p (a b)"), lg, ACT.Exp, scale=-1.0), [m])
    a = pr.dve(lambda e: e.tensor_scalar(ex[:, :, :], ex[:, :, :], 1.0, None, ALU.add), [a])
    a = pr.dve(lambda e: e.reciprocal(sig[:, :, :], ex[:, :, :]), [a])
    a = pr.dve(lambda e: e.tensor_tensor(s1[:, :, :], sig[:, :, :],
                                         brow[:, :].unsqueeze(1).broadcast_to([P, NT, NE]), ALU.add), [a])
    for hot in (oh, oh2):
        a = pr.dve(lambda e: e.tensor_reduce(mx[:, :], s1[:, :, :], AX.X, ALU.max), [a])
        a = pr.dve(lambda e: e.tensor_tensor(eq[:, :, :], s1[:, :, :], bc(mx[:, :]), ALU.is_equal), [a])
        a = pr.dve(lambda e: e.tensor_tensor(key[:, :, :], eq[:, :, :], rank[:, :, :], ALU.mult), [a, rk])
        a = pr.dve(lambda e: e.tensor_reduce(mx[:, :], key[:, :, :], AX.X, ALU.max), [a])
        a = pr.dve(lambda e, hot=hot: e.tensor_tensor(hot[:, :, :], key[:, :, :], bc(mx[:, :]), ALU.is_equal), [a])
        if hot is oh:
            a = pr.dve(lambda e: e.scalar_tensor_tensor(s1[:, :, :], oh[:, :, :], -1e30, s1[:, :, :],
                                                        ALU.mult, ALU.add), [a])
    a = pr.dve(lambda e: e.tensor_tensor(oh[:, :, :], oh[:, :, :], oh2[:, :, :], ALU.add), [a])
    a = pr.dve(lambda e: e.tensor_tensor(oh[:, :, :], oh[:, :, :], sig[:, :, :], ALU.mult), [a])
    a = pr.dve(lambda e: e.tensor_reduce(mx[:, :], oh[:, :, :], AX.X, ALU.add), [a])
    a = pr.dve(lambda e: e.reciprocal(mx[:, :], mx[:, :]), [a])
    ewr = pr.dve(lambda e: e.scalar_tensor_tensor(ew[:, :, :], oh[:, :, :], 0.5, bc(mx[:, :]), ALU.mult, ALU.mult), [a])

    th = [sb(f"f_th{i}", [P, 512], F32) for i in range(2)]
    gg = [sb(f"f_g{i}", [P, 512], F32) for i in range(2)]
    gT = [sb(f"f_gT{i}", [P, 2, 512], BF16) for i in range(2)]
    EH = NE // 2
    pairs = [(t, hf) for t in range(NT) for hf in range(2)]
    state = {}

    def up(n):
        t, hf = pairs[n]
        i = n % 2
        free = pr.of(f"h{i}")
        toks = []
        for w in range(2):
            bank = score[:, (2 * i + w) * 512:(2 * i + w + 1) * 512]
            passes = [(ic, a, b) for ic in range(IC) for a, b in THREE]
            for s, (ic, a, b) in enumerate(passes):
                m = pr.pe(lambda e, bank=bank, w=w, ic=ic, a=a, b=b, s=s: e.matmul(
                    bank, xT[:, a, ic, t * P:(t + 1) * P], w13[:, w, b, ic, hf * 512:(hf + 1) * 512],
                    start=(s == 0), stop=(s == 5)), free + wr + ready, signal=(s == 5))
            toks.append(m)
        h1, h3 = (score[:, (2 * i + w) * 512:(2 * i + w + 1) * 512] for w in range(2))
        a = pr.act(lambda e: e.activation(th[i][:, :], h1, ACT.Tanh, scale=0.5), [toks[0]] + pr.of(f"th{i}"))
        a = pr.dve(lambda e: e.scalar_tensor_tensor(th[i][:, :], th[i][:, :], 1.0, h1, ALU.add, ALU.mult), [a])
        a = pr.dve(lambda e: e.tensor_tensor(th[i][:, :], th[i][:, :], h3, ALU.mult), [a, toks[1]])
        pr.leave(f"h{i}", a)
        w_ = ew[:, t, hf * EH:(hf + 1) * EH].unsqueeze(2).broadcast_to([P, EH, FF])
        a = pr.dve(lambda e: e.tensor_tensor(gg[i][:, :].rearrange("p (a b) -> p a b", a=EH),
                                             th[i][:, :].rearrange("p (a b) -> p a b", a=EH), w_, ALU.mult),
                   [a, ewr] + pr.of(f"gg{i}"))
        pr.leave(f"th{i}", a)
        state[n] = a

    def down(n):
        t, hf = pairs[n]
        i = n % 2
        for j in range(EH):
            m = pr.pe(lambda e, j=j: e.transpose(tb[i][:, j * P:(j + 1) * P], gg[i][:, j * FF:(j + 1) * FF], ident[:, :]),
                      [state[n]] + pr.of(f"tbf{i}"), signal=(j == EH - 1))
        pr.leave(f"gg{i}", m)
        s = split(pr, tb[i][:, :], gT[i][:, 0, :], gT[i][:, 1, :], [m], pr.of(f"gT{i}"))
        pr.leave(f"tbf{i}", s)
        acc = (pv, pa)[t % 2]
        for j in range(EH):
            for c, (a, b) in enumerate(THREE):
                first, last = (hf, j, c) == (0, 0, 0), (hf, j, c) == (1, EH - 1, 2)
                m = pr.pe(lambda e, j=j, a=a, b=b, first=first, last=last, acc=acc: e.matmul(
                    acc[:, 0:H], gT[i][:, a, j * P:(j + 1) * P], w2[:, b, hf * EH + j, :], start=first, stop=last),
                    [s, w2r, ewr] + pr.of(f"acc{t % 2}"), signal=(j == EH - 1 and c == 2))
        pr.leave(f"gT{i}", m)
        if hf == 1:
            d = pr.dve(lambda e, acc=acc, t=t: e.scalar_tensor_tensor(x[:, t, :], acc[:, 0:H], gate[:, 2:3], x[:, t, :],
                                                                      ALU.mult, ALU.add), [m])
            pr.leave(f"acc{t % 2}", d)
            pr.leave("x", d)

    up(0)
    for n in range(1, len(pairs)):
        up(n)
        down(n - 1)
    down(len(pairs) - 1)


def layer1_attention(k, sb):
    pr, A, x, gate, ident, identb = k["pr"], k["A"], k["x"], k["gate"], k["ident"], k["identb"]
    score, tb, pv, pa, mhalf = k["score"], k["tb"], k["pv"], k["pa"], k["mhalf"]
    HQ, R = NH1 // 4, 4 * D1
    VC = 16
    wf = sb("l1_wf", [P, IC, 3 * H], F32)
    w1 = sb("l1_w", [P, 2, IC, 3 * H], BF16)
    stg = [sb(f"l1_ctx{i}", [P, 2, IC, SC], BF16) for i in range(2)]
    QB = [sb(f"QB{i}", [P, HQ, 4, S], BF16) for i in range(2)]
    KT1 = [sb(f"KT1_{i}", [P, HQ, SC], BF16) for i in range(2)]
    V1 = [sb(f"V1_{i}", [P, KT, NH1, VC], F32) for i in range(2)]
    P1 = [sb(f"P1_{i}", [P, 4 * S], F32) for i in range(3)]
    xn = sb("l1_xn", [P, TB, H], F32)
    xT = sb("l1_xT", [P, 2, IC, P], BF16)
    st, mv, rs = sb("l1_st", [P, TB, 6], F32), sb("l1_mv", [P, TB, 2], F32), sb("l1_rs", [P, TB], F32)
    sq = sb("l1_sq", [P, H], F32)
    ss, rr = sb("l1_ss", [P, NH1], F32), sb("l1_rr", [P, NH1], F32)
    kn = sb("l1_kn", [P, H], F32)
    stack = [sb(f"l1_stack{i}", [P, NH1, 4, D1], BF16) for i in range(2)]
    OS = sb("l1_O", [P, S], F32)
    den = sb("l1_den", [P, TB, 4], F32)
    att = sb("l1_att", [P, TB, 4, D1], F32)

    pr.straight()
    l = pr.dma("w0", lambda e: e.dma_start(wf[:, :, :], A["l1_wT"]))
    split(pr, wf[:, :, :], w1[:, 0, :, :], w1[:, 1, :, :], [l])
    for i in range(2):
        z = pr.pool(lambda e, i=i: e.memset(QB[i][:, :, :, :], 0.0))
        z = pr.pool(lambda e, i=i: e.memset(V1[i][:, :, :, :], 0.0))
        pr.pool(lambda e, i=i: e.memset(V1[i][:, :, :, D1:D1 + 1], 1.0), [z])
    pr.dve(lambda e: e.memset(pv[:, :], 0.0))

    def load(p, n):
        a = pr.dma(f"ld{p}", lambda e: e.dma_start(
            stg[p][:, :, :, :].rearrange("p a b c -> p (a b c)").rearrange("p (o c) -> p o c", o=1),
            k["stage_d"][bass.ds(n(pr.i) % B, 1), :, 0:2 * IC * SC].rearrange("o p c -> p o c")), pr.of(f"prepared{p}"))
        pr.leave(f"loaded{p}", a)

    def rms_stack(bank, rows, ready, s, dup_hi_inner):
        a = pr.act(lambda e: e.activation(sq[0:rows, :], bank, ACT.Square), [ready])
        a = pr.dve(lambda e: e.tensor_reduce(ss[0:rows, :], sq[0:rows, :].rearrange("p (h d) -> p h d", d=D1),
                                             AX.X, ALU.add), [a])
        a = pr.pool(lambda e: e.tensor_scalar(rr[0:rows, :], ss[0:rows, :], 1.0 / D1, EPS6, ALU.mult, ALU.add), [a], lone=True)
        a = pr.pool(lambda e: e.tensor_tensor(rr[0:rows, :], rr[0:rows, :], mhalf[0:rows, 0:NH1], ALU.pow), [a])
        a = pr.dve(lambda e: e.tensor_tensor(kn[0:rows, :].rearrange("p (h d) -> p h d", d=D1),
                                             bank.rearrange("p (h d) -> p h d", d=D1),
                                             rr[0:rows, :].unsqueeze(2).broadcast_to([rows, NH1, D1]), ALU.mult),
                   [a] + pr.of("kn_read"))
        done = a
        src = kn[0:rows, :].rearrange("p (h d) -> p h d", d=D1)
        slots = ((0, 1), (2, 3)) if dup_hi_inner else ((0, 2), (1, 3))
        sl = lambda i: stack[s][0:rows, :, i, :]
        h = pr.pool(lambda e: e.tensor_copy(sl(slots[0][0]), src), [a] + pr.of(f"stack{s}"), lone=True)
        h2 = pr.pool(lambda e: e.tensor_copy(sl(slots[0][1]), src))
        lo = pr.pool(lambda e: e.tensor_tensor(sl(slots[1][0]), src, sl(slots[0][0]), ALU.subtract), [h])
        pr.leave("kn_read", lo)
        lo = pr.pool(lambda e: e.tensor_copy(sl(slots[1][1]), sl(slots[1][0])), [lo], lone=True)
        return done, lo

    def turn_stack(s, rows, ready):
        bank = tb[1][:, :].bitcast(BF16)
        st_ = stack[s][:, :, :, :].rearrange("p h s d -> p (h s d)")
        for q in range(HQ):
            m = pr.pe(lambda e, q=q: e.transpose(bank[:, q * P:q * P + rows], st_[0:rows, q * P:(q + 1) * P],
                                                 identb[0:rows, 0:rows]), [ready] + pr.of("tb1"), signal=(q == HQ - 1))
        pr.leave(f"stack{s}", m)
        return bank.rearrange("p (q t) -> p q t", q=HQ)[:, :, 0:rows], m

    def prepare(p, n):
        outs = []
        for t in range(TB):
            a = pr.dve(lambda e, t=t: e.bn_stats(st[:, t, :], x[:, bass.ds(n(pr.i) % B * TB + t, 1), :].rearrange(
                "p o d -> p (o d)")), pr.of("x"))
        for t in range(TB):
            a = pr.dve(lambda e, t=t: e.bn_aggr(mv[:, t, :], st[:, t, :]), [a], lone=True)
        a = pr.pool(lambda e: e.tensor_scalar(rs[:, :], mv[:, :, 1], EPS5, None, ALU.add), [a], lone=True)
        a = pr.pool(lambda e: e.tensor_tensor(rs[:, :], rs[:, :], mhalf[:, 0:TB], ALU.pow), [a])
        for t in range(TB):
            xr = pr.dve(lambda e, t=t: e.tensor_scalar(
                xn[:, t, :], x[:, bass.ds(n(pr.i) % B * TB + t, 1), :].rearrange("p o d -> p (o d)"),
                mv[:, t, 0:1], rs[:, t:t + 1], ALU.subtract, ALU.mult), [a] + pr.of("xn_read"))
        yield
        for t in range(TB):
            for ic in range(IC):
                m = pr.pe(lambda e, t=t, ic=ic: e.transpose(tb[0][:, ic * P:(ic + 1) * P],
                                                            xn[:, t, ic * P:(ic + 1) * P], ident[:, :]),
                          [xr] + pr.of("tb0"), signal=(ic == IC - 1))
            pr.leave("xn_read", m)
            s = split(pr, tb[0][:, 0:IC * P], xT[:, 0, :, :].rearrange("p i t -> p (i t)"),
                      xT[:, 1, :, :].rearrange("p i t -> p (i t)"), [m], pr.of("xT_read"))
            pr.leave("tb0", s)
            passes = [(ic, a, b) for ic in range(IC) for a, b in THREE]
            for c, (ic, a, b) in enumerate(passes):
                m = pr.pe(lambda e, ic=ic, a=a, b=b, c=c: e.matmul(pa[:, 0:H], xT[:, a, ic, :], w1[:, b, ic, 0:H],
                                                                   start=(c == 0), stop=(c == 5)),
                          [s] + pr.of("pa"), signal=(c == 5))
            pr.leave("xT_read", m)
            done, lo = rms_stack(pa[:, 0:H], P, m, t % 2, False)
            pr.leave("pa", done)
            yield
            bank, m = turn_stack(t % 2, P, lo)
            for j in range(4):
                c = pr.dve(lambda e, j=j, t=t, bank=bank: e.tensor_copy(
                    QB[p][j * R:(j + 1) * R, :, j, t * P:(t + 1) * P], bank[j * R:(j + 1) * R, :, :]),
                    [m] + pr.of(f"QK_read{p}"))
            pr.leave("tb1", c)
            outs.append(c)
            yield
        for t in range(KT):
            rows = P if t < KT - 1 else TAIL
            passes = [(ic, a, b) for ic in range(IC) for a, b in THREE]
            for c, (ic, a, b) in enumerate(passes):
                m = pr.pe(lambda e, t=t, rows=rows, ic=ic, a=a, b=b, c=c: e.matmul(
                    pa[0:rows, :], stg[p][:, a, ic, t * P:t * P + rows], w1[:, b, ic, H:3 * H],
                    start=(c == 0), stop=(c == 5)), pr.of("pa", f"loaded{p}"), signal=(c == 5))
            v = pr.act(lambda e, t=t, rows=rows: e.copy(
                V1[p][0:rows, t, :, 0:D1], pa[0:rows, H:2 * H].rearrange("p (h d) -> p h d", d=D1)),
                [m] + pr.of(f"V_read{p}"))
            outs.append(v)
            done, lo = rms_stack(pa[0:rows, 0:H], rows, v, t % 2, True)
            pr.leave("pa", done)
            if t == KT - 1:
                pr.leave(f"prepared{p}", m)
            yield
            bank, m = turn_stack(t % 2, rows, lo)
            c = pr.dve(lambda e, t=t, rows=rows, bank=bank: e.tensor_copy(KT1[p][:, :, t * P:t * P + rows], bank),
                       [m] + pr.of(f"QK_read{p}"))
            pr.leave("tb1", c)
            outs.append(c)
            yield
        pr.leave(f"ready{p}", *outs)

    def advance(gen, n):
        for _ in range(n):
            next(gen, None)

    def attend(p, n, gen):
        steps = [(hq, t) for hq in range(HQ) for t in range(KT)]
        exps = {}

        def first(i):
            hq, t = steps[i]
            rows = P if t < KT - 1 else TAIL
            d = i % 2
            for h in range(2):
                m = pr.pe(lambda e, h=h: e.matmul(
                    score[0:rows, (2 * d + h) * 512:(2 * d + h + 1) * 512], KT1[p][:, hq, t * P:t * P + rows],
                    QB[p][:, hq, 2 * h:2 * h + 2, :], start=True, stop=True),
                    pr.of(f"s{d}", f"ready{p}"), signal=(h == 1))
            if i == len(steps) - 1:
                pr.leave(f"QK_read{p}", m)
            b = i % 3
            a = pr.act(lambda e: e.activation(P1[b][0:rows, :], score[0:rows, d * 1024:(d + 1) * 1024], ACT.Exp,
                                              scale=float(D1) ** -0.5), [m] + pr.of(f"P{b}"))
            pr.leave(f"s{d}", a)
            exps[i] = a

        def second(i):
            hq, t = steps[i]
            rows = P if t < KT - 1 else TAIL
            b = i % 3
            for j in range(4):
                m = pr.pe(lambda e, j=j: e.matmul(
                    pv[j * R:j * R + VC, 0:S], V1[p][0:rows, t, 4 * hq + j, :], P1[b][0:rows, j * S:(j + 1) * S],
                    start=(t == 0), stop=(t == KT - 1), skip_group_check=True),
                    [exps[i]] + pr.of("pv"), signal=(j == 3))
            pr.leave(f"P{b}", m)
            if i == len(steps) - 1:
                pr.leave(f"V_read{p}", m)
            if t == KT - 1:
                c = pr.dve(lambda e: e.tensor_copy(OS[:, :], pv[:, 0:S]), [m] + pr.of("OS"))
                pr.leave("pv", c)
                for tt in range(TB):
                    m = pr.pe(lambda e, tt=tt: e.transpose(tb[0][:, tt * P:(tt + 1) * P], OS[:, tt * P:(tt + 1) * P],
                                                           ident[:, :]), [c] + pr.of("tb0"), signal=(tt == TB - 1))
                pr.leave("OS", m)
                o = tb[0][:, 0:TB * P].rearrange("p (t h c) -> p t h c", t=TB, h=4)
                r = pr.dve(lambda e: e.reciprocal(den[:, :, :], o[:, :, :, D1]), [m])
                r = pr.dve(lambda e: e.tensor_tensor(att[:, :, :, :], o[:, :, :, 0:D1],
                                                     den[:, :, :].unsqueeze(3).broadcast_to([P, TB, 4, D1]),
                                                     ALU.mult), [r])
                pr.leave("tb0", r)

                def xs():
                    return x[:, bass.ds(n(pr.i) % B * TB, TB), hq * R:(hq + 1) * R]
                r = pr.dve(lambda e: e.scalar_tensor_tensor(
                    xs(), att[:, :, :, :].rearrange("p t h d -> p t (h d)"), gate[:, 1:2], xs(), ALU.mult, ALU.add), [r])
                pr.leave("x", r)

        first(0)
        for i in range(len(steps)):
            if i + 1 < len(steps):
                first(i + 1)
            if i % 3 == 1:
                advance(gen, 1)
            second(i)
        advance(gen, 99)

    pr.straight()
    load(0, lambda i: 0)
    load(1, lambda i: 1)
    advance(prepare(0, lambda i: 0), 99)
    pr.loop(B // 2)
    pr.carry(*(["x", "xn_read", "xT_read", "tb0", "tb1", "pa", "pv", "kn_read", "stack0", "stack1", "s0", "s1", "P0",
                "P1", "P2", "OS"]
               + [f"{n}{p}" for p in range(2) for n in ("loaded", "prepared", "QK_read", "V_read", "ready")]))
    load(0, lambda i: 2 * i + 2)
    attend(0, lambda i: 2 * i, prepare(1, lambda i: 2 * i + 1))
    load(1, lambda i: 2 * i + 3)
    attend(1, lambda i: 2 * i + 1, prepare(0, lambda i: 2 * i + 2))


def layer1_ffn(k, sb):
    pr, A, x, gate, sc = k["pr"], k["A"], k["x"], k["gate"], k["sc"]
    score = k["score"]
    pr.straight()
    pw, nw = (sb(n, [P, IC, H, NBITS], F32) for n in ("b_pw", "b_nw"))
    pb, nb = (sb(n, [P, H, NBITS], F32) for n in ("b_pb", "b_nb"))
    bits = sb("b_bits", [P, 3, NBITS], F32)
    wT32 = sb("b_w32", [P, IC, H], F32)
    wT = sb("b_w", [P, 2, IC, H], BF16)
    coef = sb("b_coef", [P, NBITS], F32)
    bias = sb("b_bias", [P, H], F32)
    l1 = pr.dma("w0", lambda e: e.dma_start(pw[:, :, :, :], A["pweight"]))
    l2 = pr.dma("w1", lambda e: e.dma_start(nw[:, :, :, :], A["nweight"]))
    pr.dma("in", lambda e: e.dma_start(pb[:, :, :].rearrange("p a b -> p (a b)"), A["pbias"].partition_broadcast(P)))
    pr.dma("in", lambda e: e.dma_start(nb[:, :, :].rearrange("p a b -> p (a b)"), A["nbias"].partition_broadcast(P)))
    l3 = pr.dma("in", lambda e: e.dma_start(bits[:, :, :].rearrange("p a b -> p (a b)"),
                                            A["bits"].partition_broadcast(P)))
    flat = lambda t: t[:, :, :, :].rearrange("p a b c -> p (a b c)")
    t1 = pr.act(lambda e: e.activation(flat(pw), flat(pw), ACT.Tanh, scale=0.5), [l1])
    t2 = pr.act(lambda e: e.activation(flat(nw), flat(nw), ACT.Tanh, scale=0.5), [l2])
    c = pr.act(lambda e: e.activation(coef[:, :], bits[:, 2, :], ACT.Exp, scale=-1.0), [l3])
    c = pr.dve(lambda e: e.tensor_scalar(coef[:, :], coef[:, :], 1.0, None, ALU.add), [c])
    c = pr.dve(lambda e: e.reciprocal(coef[:, :], coef[:, :]), [c])
    c = pr.dve(lambda e: e.tensor_tensor(coef[:, :], coef[:, :], bits[:, 0, :], ALU.mult), [c])
    c = pr.dve(lambda e: e.tensor_scalar(coef[:, :], coef[:, :], sc("scale"), 0.5, ALU.mult, ALU.mult), [c])
    d = pr.dve(lambda e: e.tensor_tensor(flat(pw), flat(pw), flat(nw), ALU.subtract), [t1, t2])
    pv3 = pw[:, :, :, :].rearrange("p a b c -> p (a b) c")
    d = pr.dve(lambda e: e.tensor_tensor(pv3, pv3, coef[:, :].unsqueeze(1).broadcast_to([P, IC * H, NBITS]),
                                         ALU.mult), [d, c])
    d = pr.dve(lambda e: e.tensor_reduce(wT32[:, :, :].rearrange("p a b -> p (a b)"), pv3, AX.X, ALU.add), [d])
    wr = split(pr, wT32[:, :, :], wT[:, 0, :, :], wT[:, 1, :, :], [d])
    b = pr.dve(lambda e: e.tensor_tensor(pb[:, :, :], pb[:, :, :], nb[:, :, :], ALU.subtract), [l3])
    b = pr.dve(lambda e: e.tensor_tensor(pb[:, :, :], pb[:, :, :],
                                         bits[:, 1, :].unsqueeze(1).broadcast_to([P, H, NBITS]), ALU.mult), [b])
    b = pr.dve(lambda e: e.tensor_reduce(bias[:, :], pb[:, :, :], AX.X, ALU.add), [b])
    step = float(2 ** NBITS - 1)
    b = pr.dve(lambda e: e.tensor_scalar(bias[:, :], bias[:, :], 1.0, -1.0, ALU.min, ALU.max), [b])
    b = pr.dve(lambda e: e.tensor_scalar(bias[:, :], bias[:, :], step, ROUND_INT, ALU.mult, ALU.add), [b])
    b = pr.dve(lambda e: e.tensor_scalar(bias[:, :], bias[:, :], ROUND_INT, 1.0 / step, ALU.subtract, ALU.mult), [b])
    b = pr.dve(lambda e: e.tensor_scalar(bias[:, :], bias[:, :], sc("bscale"), gate[:, 3:4], ALU.mult, ALU.mult), [b])
    xT, _, ready = norm_transposed(k, sb, "g", EPS5)
    done = pr.of()
    passes = [(ic, a, c_) for ic in range(IC) for a, c_ in THREE]
    free = {i: list(ready) for i in range(4)}
    for t in range(NT):
        i = t % 4
        bank = score[:, i * 512:i * 512 + H]
        for n, (ic, a, w) in enumerate(passes):
            m = pr.pe(lambda e, t=t, ic=ic, a=a, w=w, n=n, bank=bank: e.matmul(
                bank, xT[:, a, ic, t * P:(t + 1) * P], wT[:, w, ic, :], start=(n == 0), stop=(n == 5)),
                free[i] + [wr], signal=(n == 5))
        d = pr.dve(lambda e, t=t, bank=bank: e.scalar_tensor_tensor(x[:, t, :], bank, gate[:, 3:4], x[:, t, :],
                                                                    ALU.mult, ALU.add), [m])
        free[i] = [d]
        d = pr.dve(lambda e, t=t: e.tensor_tensor(x[:, t, :], x[:, t, :], bias[:, :], ALU.add), [d, b])
    pr.leave("x", d)


def kernel(**inputs):
    import numpy as np
    import concourse.bacc as bacc
    from concourse.bass_utils import run_bass_kernel_spmd

    nc = bacc.Bacc("TRN2", target_bir_lowering=False, num_devices=1)
    arrays, A = {}, {}
    for name, a in layout(np, inputs).items():
        arrays["in_" + name] = a
        A[name] = nc.dram_tensor("in_" + name, a.shape, mybir.dt.from_np(a.dtype), kind="ExternalInput").ap()
    out = nc.dram_tensor("out_0", (B * S, H), F32, kind="ExternalOutput").ap()
    build(nc, A, out)
    r = run_bass_kernel_spmd(nc, [arrays], core_ids=[0])
    return np.asarray(r.results[0]["out_0"]).reshape(B, S, H)


def layout(np, v):
    a = {n: np.ascontiguousarray(np.asarray(z)) for n, z in v.items()}
    l0 = lambda n: a["L0_xattn_" + n]

    def chunked(w):
        return w.reshape(w.shape[0] // P, P, -1).transpose(1, 0, 2)

    out = {}
    out["x"] = a["x"].reshape(B * S, H)
    out["ctxT"] = np.ascontiguousarray(chunked(a["ctx_2048"].reshape(B * SC, H).T).reshape(P, IC, B, SC))
    wt = {n: l0(n).T for n in ("wq", "wqx", "wk", "wv")}
    kv = l0("w_kv_x").T
    groups = []
    for g in range(G):
        s2, s1 = slice(g * HPG * D, (g + 1) * HPG * D), slice(g * D, (g + 1) * D)
        groups.append(chunked(np.concatenate(
            [wt["wq"][:, s2], wt["wqx"][:, s2], wt["wk"][:, s1], wt["wv"][:, s1], kv[:, s1],
             kv[:, G * D + g * D:G * D + (g + 1) * D]], axis=1)))
    out["w_all"] = np.ascontiguousarray(np.stack(groups))
    names = ["ln_w", "ln_b", "q_in_scale", "qx_in_scale", "k_in_scale", "v_in_scale"]
    out["cols"] = np.ascontiguousarray(np.concatenate([l0(n).reshape(IC, P).T for n in names], axis=1))
    out["dcols"] = np.ascontiguousarray(np.stack([l0(n) for n in DCOLS], axis=1))
    out["scal"] = np.concatenate([z.reshape(-1) for z in (
        l0("wq_scale"), l0("wqx_scale"), l0("wk_scale"), l0("wv_scale"), l0("proj_w_scale"), l0("proj_in_scale"),
        a["g_xattn"], a["g_ffn"], a["L1_ffn_scale"], a["L1_ffn_biasscale"])])
    fe = lambda z: z.reshape(2, G, HPG, D, -1).transpose(1, 0, 2, 3, 4).reshape(2 * G * HPG * D, -1)
    out["smooth"] = np.ascontiguousarray(fe(l0("proj_smooth")).reshape(P, 2 * G * HPG))
    out["wprojT"] = np.ascontiguousarray(fe(l0("wproj").T).reshape(2 * G * HPG, P, H).transpose(1, 0, 2))
    f = lambda n: a["L0_ffn_" + n]
    out["wgT"] = np.ascontiguousarray(chunked(f("Wg").T))
    out["w1T"] = np.ascontiguousarray(chunked(f("W1").reshape(NE * FF, H).T))
    out["w3T"] = np.ascontiguousarray(chunked(f("W3").reshape(NE * FF, H).T))
    out["w2T"] = np.ascontiguousarray(f("W2").transpose(2, 0, 1))
    out["ffn_bias"] = f("bias")
    kv1 = np.concatenate([a["L1_xattn_Wk"], a["L1_xattn_Wv"]], axis=0)
    out["l1_wT"] = np.ascontiguousarray(chunked(np.concatenate([a["L1_xattn_Wq"], kv1[0::2], kv1[1::2]], axis=0).T))
    for n in ("pweight", "nweight"):
        out[n] = np.ascontiguousarray(a["L1_ffn_" + n].transpose(1, 0, 2).reshape(IC, P, H, NBITS).transpose(1, 0, 2, 3))
    for n in ("pbias", "nbias"):
        out[n] = a["L1_ffn_" + n].reshape(-1)
    out["bits"] = np.concatenate([a["L1_ffn_exps"], a["L1_ffn_bexps"], a["L1_ffn_mask_weight"]])
    return out
```

```python
from contextlib import ExitStack

import concourse.bass as bass
from concourse import mybir

F32 = mybir.dt.float32
BF16 = mybir.dt.bfloat16
I16 = mybir.dt.int16
ALU = mybir.AluOpType
ACT = mybir.ActivationFunctionType
AX = mybir.AxisListType

P = 128
B, S, H = 4, 256, 256
SC = 1601
IC = H // P
NT = B * S // P
TB = S // P
D = 128
G = 8
HPG = 2
NQ = TB * HPG
KT = (SC + P - 1) // P
TAIL = SC - (KT - 1) * P
NGB = G * B
WCOLS = 2 * HPG * D + 4 * D
CQ, CQX, CK, CV, CKX = 0, 256, 512, 640, 768
STAGE = 2 * IC * SC + 4 * IC * S
FF, NE = 128, 8
NH1, D1 = 32, 8
NBITS = 4
FP8_MAX = 448.0
EPS5, EPS6 = 1e-5, 1e-6
ROUND_F8 = 1.5 * 2.0 ** 20
ROUND_INT = 1.5 * 2.0 ** 23

COLS = ["ln_w", "ln_b", "s_q", "s_qx", "s_k", "s_v"]
DCOLS = ["qln_w", "qln_b", "qxln_w", "qxln_b", "kln_w", "kln_b", "kxln_w", "kxln_b"]
SCAL = ["wq", "wqx", "wk", "wv", "pw", "pin", "gx0", "gx1", "gf0", "gf1", "scale", "bscale"]


class Token:

    def __init__(self, sem, n, region, back=0):
        self.sem, self.n, self.region, self.back = sem, n, region, back


class Carry:

    def __init__(self, region, name):
        self.region, self.name = region, name


class Program:

    ENGINES = ("pe", "act", "dve", "pool", "sp")

    def __init__(self, nc, ctx):
        self.nc, self.ctx = nc, ctx
        self.queue = {e: [] for e in self.ENGINES}
        self.sems, self.regions = {}, []
        self.left = {}
        for e in self.ENGINES[:4]:
            self.sems[e] = ctx.enter_context(nc.semaphore("done_" + e))
        self.straight()

    def stream(self, name):
        self.sems[name] = self.ctx.enter_context(self.nc.semaphore("dma_" + name))
        return name

    def straight(self):
        self._region(1)

    def loop(self, trips):
        self._region(trips)

    def _region(self, trips):
        self.regions.append({"trips": trips, "count": {}, "left": {}, "back": False})
        self.left = {}
        for e in self.ENGINES:
            self.queue[e].append(("region", len(self.regions) - 1))

    def carry(self, *names):
        r = len(self.regions) - 1
        for name in names:
            self.left[name] = [Carry(r, name)]
        self.regions[r]["left"] = self.left

    def leave(self, name, *tokens):
        self.left[name] = list(tokens)

    def of(self, *names):
        return [t for name in names for t in self.left.get(name, [])]

    def step(self, engine, fn, after=(), sem=None, signal=True, lone=False):
        sem = sem or engine
        inc = 1 if sem in self.ENGINES else 16
        tok = None
        if signal:
            r = self.regions[-1]
            r["count"][sem] = r["count"].get(sem, 0) + inc
            tok = Token(sem, r["count"][sem], len(self.regions) - 1)
        self.queue[engine].append(("step", fn, [t for t in after if t is not None], (sem, inc) if signal else None, lone))
        return tok

    def pe(self, fn, after=(), signal=False):
        return self.step("pe", fn, after, signal=signal)

    def act(self, fn, after=()):
        return self.step("act", fn, after)

    def dve(self, fn, after=(), lone=False):
        return self.step("dve", fn, after, lone=lone)

    def pool(self, fn, after=(), lone=False):
        return self.step("pool", fn, after, lone=lone)

    def dma(self, stream, fn, after=()):
        return self.step("sp", fn, after, sem=stream)

    def _resolve(self, tok, out, back=0):
        if isinstance(tok, Carry):
            r = self.regions[tok.region]
            for t in r["left"][tok.name]:
                if isinstance(t, Carry) and t.name == tok.name:
                    raise ValueError("nothing is left under " + tok.name)
                self._resolve(t, out, back + 1)
        else:
            out.append(Token(tok.sem, tok.n, tok.region, tok.back + back))

    def emit(self):
        base = {s: 0 for s in self.sems}
        for r in self.regions:
            primed = r["trips"] > 1
            r["base"] = dict(base)
            r["prime"] = {s: (r["count"].get(s, 0) if primed else 0) for s in self.sems}
            for s in base:
                base[s] += r["prime"][s] + r["trips"] * r["count"].get(s, 0)
        self.total = base
        block = self.ctx.enter_context(self.nc.Block())
        for name, dec in (("sp", block.sync), ("pool", block.gpsimd), ("dve", block.vector),
                          ("act", block.scalar), ("pe", block.tensor)):
            dec(self._emitter(name))

    def _emitter(self, name):
        def run(e):
            items = self.queue[name]
            parts, cur = [], None
            for it in items:
                if it[0] == "region":
                    cur = (it[1], [])
                    parts.append(cur)
                else:
                    cur[1].append(it)
            for ri, steps in parts:
                r = self.regions[ri]
                if ri:
                    for s, v in r["base"].items():
                        if v:
                            e.wait_ge(self.sems[s], v)
                if r["trips"] > 1:
                    for s, v in r["prime"].items():
                        owner = s if s in self.ENGINES else "sp"
                        if owner == name and v:
                            e.sem_inc(self.sems[s], v)
                    if steps:
                        with e.Fori(0, r["trips"], 1) as i:
                            self._steps(e, name, ri, steps, i)
                else:
                    self._steps(e, name, ri, steps, 0)
            for s, v in self.total.items():
                if s not in self.ENGINES and name == "sp" and v:
                    e.wait_ge(self.sems[s], v)
        return run

    def _steps(self, e, e_name, ri, steps, i):
        r = self.regions[ri]
        seen = {}
        for _, fn, after, sig, lone in steps:
            need = {}
            for tok in after:
                got = []
                self._resolve(tok, got)
                for t in got:
                    if t.region == ri:
                        v = t.n - t.back * r["count"].get(t.sem, 0)
                        need[t.sem] = max(need.get(t.sem, -10 ** 9), v)
            waited = False
            for s, v in need.items():
                if v <= seen.get(s, -10 ** 9):
                    continue
                seen[s] = v
                first = r["base"][s] + r["prime"][s] + v
                per = r["count"].get(s, 0)
                e.wait_ge(self.sems[s], i * per + first if r["trips"] > 1 else first)
                waited = True
            if lone and waited and r["trips"] > 1:
                e.nop(nofuse=True)
            self.i = i
            ins = fn(e)
            if sig:
                ins.then_inc(self.sems[sig[0]], sig[1])


def tensors(nc, ctx):
    def sb(name, shape, dt):
        return ctx.enter_context(nc.sbuf_tensor(name, shape, dt))

    def ps(name, shape, dt):
        return ctx.enter_context(nc.psum_tensor(name, shape, dt))

    return sb, ps


def round_fp8(pr, y, e, m, t, after, on_pool):
    add = pr.pool if on_pool else pr.dve
    a = pr.dve(lambda v: v.tensor_scalar(e.bitcast(I16), y.bitcast(I16), 0x7F80, None, ALU.bitwise_and), after)
    b = add(lambda v: v.tensor_scalar(m, e, 2.0 ** -6, ROUND_F8, ALU.max, ALU.mult), [a], lone=True)
    c = add(lambda v: v.tensor_tensor(t, y, m, ALU.add), [b])
    return add(lambda v: v.tensor_tensor(y, t, m, ALU.subtract), [c])


def layernorm_rows(pr, ci, x, out, st, mv, rs, mhalf, eps, tiles, after):
    for t in range(tiles):
        a = pr.dve(lambda v, t=t: v.bn_stats(st[:, t, :], x[:, t, :]), after)
    for t in range(tiles):
        a = pr.dve(lambda v, t=t: v.bn_aggr(mv[:, t, :], st[:, t, :]), [a])
    b = pr.pool(lambda v: v.tensor_scalar(rs[:, 0:tiles], mv[:, 0:tiles, 1], eps, None, ALU.add), [a])
    b = pr.pool(lambda v: v.tensor_tensor(rs[:, 0:tiles], rs[:, 0:tiles], mhalf[:, 0:tiles], ALU.pow), [b])
    for t in range(tiles):
        c = pr.dve(lambda v, t=t: v.tensor_scalar(out[:, t, :], x[:, t, :], mv[:, t, 0:1], rs[:, t:t + 1],
                                                  ALU.subtract, ALU.mult), [b])
    return c


def build(nc, A, out):
    whole = ExitStack()
    with whole:
        pr = Program(nc, whole)
        for s in ("x", "in", "ctx0", "ctx1", "ctxs0", "ctxs1", "w0", "w1", "ws0", "ws1", "xq0", "xq1", "ld0", "ld1", "wp0",
                  "wp1", "out", "row", "rsm0", "rsm1"):
            pr.stream(s)
        sb, ps = tensors(nc, whole)
        w_split = nc.dram_tensor("w_split", (G, P, 2 * IC * WCOLS), BF16, kind="Internal").ap()
        stage_d = nc.dram_tensor("stage_d", (B, P, STAGE), BF16, kind="Internal").ap()
        rsm_d = nc.dram_tensor("rsm_d", (P, 2 * G * HPG), F32, kind="Internal").ap()

        x = sb("x", [P, NT, H], F32)
        ident = sb("ident", [P, P], F32)
        identb = sb("identb", [P, P], BF16)
        mhalf = sb("mhalf", [P, 64], F32)
        cols = sb("cols", [P, len(COLS) * IC], F32)
        dcols = sb("dcols", [P, len(DCOLS)], F32)
        scal = sb("scal", [P, len(SCAL)], F32)
        gate = sb("gate", [P, 4], F32)
        st = sb("st", [P, NT, 6], F32)
        mv = sb("mv", [P, NT, 2], F32)
        rs = sb("rs", [P, NT], F32)
        col = lambda n, ic: cols[:, COLS.index(n) * IC + ic:COLS.index(n) * IC + ic + 1]
        dcol = lambda n: dcols[:, DCOLS.index(n):DCOLS.index(n) + 1]
        sc = lambda n: scal[:, SCAL.index(n):SCAL.index(n) + 1]

        score = ps("score", [P, 4 * 512], F32)
        tb = [ps("tb0", [P, 512], F32), ps("tb1", [P, 512], F32)]
        pv = ps("pv", [P, 512], F32)
        pa = ps("pa", [P, 512], F32)

        k = dict(nc=nc, pr=pr, A=A, out=out, x=x, ident=ident, identb=identb, mhalf=mhalf, col=col, dcol=dcol, sc=sc,
                 gate=gate, st=st, mv=mv, rs=rs, score=score, tb=tb, pv=pv, pa=pa, cols=cols, dcols=dcols,
                 scal=scal, w_split=w_split, stage_d=stage_d, rsm_d=rsm_d, sb=sb)
        attn = ExitStack()
        with attn:
            catq = tensors(nc, attn)[0]("catq", [P, (NGB + 1) * 2 * NQ * P], BF16)
            k.update(catq=catq)
            with ExitStack() as c0:
                prologue(k, tensors(nc, c0)[0])
            with ExitStack() as c1:
                layer0_attention(k, tensors(nc, c1)[0])
            with ExitStack() as c2:
                layer0_projection(k, tensors(nc, c2)[0])
        for stage in (layer0_ffn, layer1_attention, layer1_ffn):
            with ExitStack() as c:
                stage(k, tensors(nc, c)[0])
        pr.dma("out", lambda e: e.dma_start(out.rearrange("(t p) d -> p t d", p=P), x[:, :, :]), pr.of("x"))
        pr.emit()


def prologue(k, sb):
    pr, A, x = k["pr"], k["A"], k["x"]
    ident, identb, mhalf = k["ident"], k["identb"], k["mhalf"]
    col, sc, score, tb = k["col"], k["sc"], k["score"], k["tb"]
    st, mv, rs = k["st"], k["mv"], k["rs"]
    ld_x = pr.dma("x", lambda e: e.dma_start(x[:, :, :], A["x"].rearrange("(t p) d -> p t d", p=P)))
    pr.dma("in", lambda e: e.dma_start(k["cols"][:, :], A["cols"]))
    pr.dma("in", lambda e: e.dma_start(k["dcols"][:, :], A["dcols"]))
    pr.dma("in", lambda e: e.dma_start(k["scal"][:, :], A["scal"].partition_broadcast(P)))
    smc = sb("smc", [P, 2 * G * HPG], F32)
    rsmc = sb("rsmc", [P, 2 * G * HPG], F32)
    ld = pr.dma("in", lambda e: e.dma_start(smc[:, :], A["smooth"]))

    z = pr.pool(lambda e: e.memset(ident[:, :], 0.0))
    i = pr.pool(lambda e: e.affine_select(out=ident[:, :], in_=ident[:, :], compare_op=ALU.not_equal, fill=1.0,
                                          base=0, pattern=[[-1, P]], channel_multiplier=1), [z])
    pr.pool(lambda e: e.memset(mhalf[:, :], -0.5))
    ib = pr.dve(lambda e: e.tensor_copy(identb[:, :], ident[:, :]), [i])

    r = pr.dve(lambda e: e.reciprocal(rsmc[:, :], smc[:, :]), [ld])
    pr.dma("row", lambda e: e.dma_start(k["rsm_d"], rsmc[:, :]), [r])

    gate = k["gate"]
    g = pr.act(lambda e: e.activation(gate[:, :], k["scal"][:, SCAL.index("gx0"):SCAL.index("gx0") + 4], ACT.Tanh), [ld])
    g = pr.dve(lambda e: e.tensor_scalar(gate[:, 0:1], gate[:, 0:1], sc("pw"), sc("pin"), ALU.mult, ALU.mult), [g])
    for n in (0, 1, 2, 3):
        pr.dve(lambda e, n=n: e.tensor_scalar(k["dcols"][:, n:n + 1], k["dcols"][:, n:n + 1], float(D) ** -0.5, None,
                                              ALU.mult), [ld])

    rin = sb("rin", [P, 4 * IC], F32)
    win = sb("win", [P, 4 * IC], F32)
    kinds = (("q", "wq", CQ, 256), ("qx", "wqx", CQX, 256), ("k", "wk", CK, 128), ("v", "wv", CV, 128))
    for n, (kind, ws, _, _) in enumerate(kinds):
        wr = pr.dve(lambda e, n=n, kind=kind, ws=ws: e.tensor_scalar(
            win[:, n * IC:(n + 1) * IC], k["cols"][:, COLS.index("s_" + kind) * IC:(COLS.index("s_" + kind) + 1) * IC],
            sc(ws), None, ALU.mult), [ld])
    rr = pr.dve(lambda e: e.reciprocal(rin[:, :], k["cols"][:, 2 * IC:6 * IC]), [ld])
    def x_norms():
        a = layernorm_rows(pr, 0, x, xn, st, mv, rs, mhalf, EPS5, NT, [ld_x])
        a = layernorm_rows(pr, 0, xn, xn, st, mv, rs, mhalf, EPS5, NT, [a])
        for ic in range(IC):
            for q in range(2):
                bank = score[:, (2 * ic + q) * 512:(2 * ic + q + 1) * 512]
                for t in range(4):
                    tt = pr.pe(lambda e, bank=bank, t=t, q=q, ic=ic: e.transpose(
                        bank[:, t * P:(t + 1) * P], xn[:, 4 * q + t, ic * P:(ic + 1) * P], ident[:, :]), [a, i, ib],
                        signal=(t == 3))
                w = pr.dve(lambda e, bank=bank, q=q, ic=ic: e.tensor_scalar(
                    xw[:, ic, q * 512:(q + 1) * 512], bank, col("ln_w", ic), col("ln_b", ic), ALU.mult, ALU.add), [tt])
        return w

    def quantised_input(n, w):
        p = n % 2
        for ic in range(IC):
            y = pr.act(lambda e, ic=ic: e.activation(xq[p][:, ic, :], xw[:, ic, :], ACT.Copy,
                                                     scale=rin[:, n * IC + ic:n * IC + ic + 1]), [w, rr] + free_q[p])
        y = pr.dve(lambda e: e.tensor_scalar(xq[p][:, :, :], xq[p][:, :, :], FP8_MAX, -FP8_MAX, ALU.min, ALU.max), [y])
        y = round_fp8(pr, xq[p][:, :, :], ex[:, :, :], m[:, :, :], y32[:, :, :], [y], False)

        def store(b):
            return pr.dma(f"xq{p}", lambda e: e.dma_start(
                k["stage_d"][b, :, 2 * IC * SC + n * IC * S:2 * IC * SC + (n + 1) * IC * S].rearrange(
                    "p (i s) -> p i s", i=IC), xq[p][:, :, b * S:(b + 1) * S]), [y])
        free_q[p] = [y]

        def stores():
            for b in range(B):
                s = store(b)
            free_q[p] = [s]
        return stores

    def weight_load(g):
        p = g % 2
        return pr.dma(f"w{p}", lambda e: e.dma_start(wf[p][:, :, :], A["w_all"][g]), free_f[p])

    def weight_parts(g, l):
        p = g % 2
        his, los = [], []
        for ic in range(IC):
            for n, (_, _, c0, nc_) in enumerate(kinds + ((None, None, CKX, 256),)):
                src = lambda ic=ic, c0=c0, nc_=nc_: wf[p][:, ic, c0:c0 + nc_]
                dst = lambda part, ic=ic, c0=c0, nc_=nc_: wo[p][:, part, ic, c0:c0 + nc_]
                if n < 4:
                    s = lambda n=n, ic=ic: win[:, n * IC + ic:n * IC + ic + 1]
                    h = pr.act(lambda e, s=s, src=src, dst=dst: e.activation(dst(0), src(), ACT.Copy, scale=s()),
                               [l, wr] + free_o[p])
                    lo = pr.dve(lambda e, s=s, src=src, dst=dst: e.scalar_tensor_tensor(
                        dst(1), src(), s(), dst(0), ALU.mult, ALU.subtract), [h])
                else:
                    h = pr.act(lambda e, src=src, dst=dst: e.copy(dst(0), src()), [l] + free_o[p])
                    lo = pr.pool(lambda e, src=src, dst=dst: e.tensor_tensor(dst(1), src(), dst(0), ALU.subtract), [h])
                his.append(h)
                los.append(lo)
        free_f[p] = [his[-1]] + los
        return los + [his[-1]]

    def weight_store(g, done):
        p = g % 2
        free_o[p] = [pr.dma(f"ws{p}", lambda e: e.dma_start(
            k["w_split"][g], wo[p][:, :, :, :].rearrange("p a b c -> p (a b c)")), done)]

    def context_load(c):
        p, b, ic = c % 2, c // IC, c % IC
        return pr.dma(f"ctx{p}", lambda e: e.dma_start(cf[p][:, :], A["ctxT"][:, ic, b, :]), free_cf[p])

    def context_parts(l, c):
        p = c % 2
        half = 1024
        h = pr.act(lambda e: e.copy(co[p][:, 0, :], cf[p][:, :]), [l] + free_co[p])
        l1 = pr.dve(lambda e: e.tensor_tensor(co[p][:, 1, 0:half], cf[p][:, 0:half], co[p][:, 0, 0:half],
                                              ALU.subtract), [h])
        l2 = pr.pool(lambda e: e.tensor_tensor(co[p][:, 1, half:], cf[p][:, half:], co[p][:, 0, half:],
                                               ALU.subtract), [h])
        free_cf[p] = [l1, l2]
        return [h, l1, l2]

    def context_store(c, done):
        p, b, ic = c % 2, c // IC, c % IC
        free_co[p] = [pr.dma(f"ctxs{p}", lambda e: e.dma_start(
            k["stage_d"][b, :, 0:2 * IC * SC].rearrange("p (a i s) -> p a i s", a=2, i=IC)[:, :, ic, :],
            co[p][:, :, :]), done)]

    wf = [sb(f"wf{i}", [P, IC, WCOLS], F32) for i in range(2)]
    wo = [sb(f"wo{i}", [P, 2, IC, WCOLS], BF16) for i in range(2)]
    cf = [sb(f"cf{i}", [P, SC], F32) for i in range(2)]
    co = [sb(f"co{i}", [P, 2, SC], BF16) for i in range(2)]
    xn = sb("xn", [P, NT, H], F32)
    xw = sb("xw", [P, IC, NT * P], F32)
    y32 = sb("y32", [P, IC, NT * P], F32)
    xq = [sb(f"xq{i}", [P, IC, NT * P], BF16) for i in range(2)]
    ex = sb("ex", [P, IC, NT * P], BF16)
    m = sb("m", [P, IC, NT * P], F32)
    free_f, free_o, free_cf, free_co, free_q = ([[], []] for _ in range(5))
    wl = {g: weight_load(g) for g in range(2)}
    cl = {c: context_load(c) for c in range(2)}
    xw_done = x_norms()
    for g in range(G):
        wd = weight_parts(g, wl[g])
        if g + 2 < G:
            wl[g + 2] = weight_load(g + 2)
        weight_store(g, wd)
        c = g
        cd = context_parts(cl[c], c)
        if c + 2 < B * IC:
            cl[c + 2] = context_load(c + 2)
        context_store(c, cd)
        if g % 2 == 1:
            quantised_input(g // 2, xw_done)()
    for t in tb:
        pr.dve(lambda e, t=t: e.memset(t[:, :], 0.0))


def layer0_attention(k, sb):
    pr, A = k["pr"], k["A"]
    ident, identb, mhalf, dcol = k["ident"], k["identb"], k["mhalf"], k["dcol"]
    score, tb, pv, pa, catq = k["score"], k["tb"], k["pv"], k["pa"], k["catq"]
    rsm = [sb(f"rsm{i}", [P, 2 * HPG * D], F32) for i in range(2)]
    stage = [sb(f"stage{i}", [P, STAGE], BF16) for i in range(2)]
    wsb = [sb(f"wsb{i}", [P, 2, IC, WCOLS], BF16) for i in range(2)]
    QT = [sb(f"QT{i}", [P, 2, 2, NQ * P], BF16) for i in range(2)]
    KS = [sb(f"KS{i}", [P, 2, S], BF16) for i in range(2)]
    VS = [sb(f"VS{i}", [P, 2, TB, D], BF16) for i in range(2)]
    KX = [sb(f"KX{i}", [P, 2, SC], BF16) for i in range(2)]
    VX = [sb(f"VX{i}", [P, 2, KT, D], BF16) for i in range(2)]
    NP_ = SC + S
    P32 = [sb(f"P32_{i}", [P, NP_], F32) for i in range(2)]
    PT = [sb(f"PT{i}", [P, 2, 512], BF16) for i in range(2)]
    kn = [sb(f"kn{i}", [P, 512], F32) for i in range(3)]
    t32 = [sb(f"t32_{i}", [P, 512], F32) for i in range(2)]
    st, mv, rs, nm = ([sb(f"a_{n}{i}", [P, *w], F32) for i in range(3)]
                      for n, w in (("st", (4, 6)), ("mv", (4, 2)), ("rs", (4,)), ("nm", (4,))))
    mxp = [sb(f"mxp{i}", [P, 2], F32) for i in range(2)]
    nmx = [sb(f"nmx{i}", [P, 2], F32) for i in range(2)]
    sums = [sb(f"sums{i}", [P, 4], F32) for i in range(2)]
    rsum = [sb(f"rsum{i}", [P, 2], F32) for i in range(2)]
    yq = sb("yq", [P, 2, NQ, P], BF16)
    ye = sb("ye", [P, 2, P], BF16)
    ym, yt = sb("ym", [P, 2, P], F32), sb("yt", [P, 2, P], F32)

    def ctx_op(p, part, ic, a, b):
        o = (part * IC + ic) * SC
        return stage[p][:, o + a:o + b]

    def xq_op(p, kind, ic, a, b):
        o = 2 * IC * SC + (kind * IC + ic) * S
        return stage[p][:, o + a:o + b]

    turn = {"tb": 0, "kn": 0, "t32": 0}

    def next_of(name, n=2):
        i = turn[name]
        turn[name] = (i + 1) % n
        return i

    def load(p, n):
        after = pr.of(f"A_done{p}")
        grp = (lambda: n(pr.i) // B % G)
        bat = (lambda: n(pr.i) % B)
        a = pr.dma(f"ld{p}", lambda e: e.dma_start(
            stage[p][:, :].rearrange("p (o c) -> p o c", o=1),
            k["stage_d"][bass.ds(bat(), 1), :, :].rearrange("o p c -> p o c")), after)
        b = pr.dma(f"ld{p}", lambda e: e.dma_start(
            wsb[p][:, :, :, :].rearrange("p a b c -> p (a b c)").rearrange("p (o c) -> p o c", o=1),
            k["w_split"][bass.ds(grp(), 1), :, :].rearrange("o p c -> p o c")), after)
        pr.leave(f"loaded{p}", a, b)

    def load_rsm(p, n):
        a = pr.dma(f"rsm{p}", lambda e: e.dma_start(
            rsm[p][:, :], k["rsm_d"].rearrange("(g c) f -> g (c f)", g=G)[
                bass.ds(n(pr.i) // B % G, 1), :].partition_broadcast(P)), pr.of(f"finished{p}"))
        pr.leave(f"rsm{p}", a)

    def normalise_start(b, blocks, rows, ready, eps):
        s = ready
        for j in range(blocks):
            s = pr.dve(lambda e, j=j: e.bn_stats(st[b][0:rows, j, :], kn[b][0:rows, j * D:(j + 1) * D]), [s])
        for j in range(blocks):
            s = pr.dve(lambda e, j=j: e.bn_aggr(mv[b][0:rows, j, :], st[b][0:rows, j, :]), [s], lone=True)
        v = lambda a: a[b][0:rows, 0:blocks]
        r = pr.pool(lambda e: e.tensor_scalar(v(rs), mv[b][0:rows, 0:blocks, 1], eps, None, ALU.add), [s], lone=True)
        r = pr.pool(lambda e: e.tensor_tensor(v(rs), v(rs), mhalf[0:rows, 0:blocks], ALU.pow), [r])
        r = pr.pool(lambda e: e.tensor_tensor(v(nm), mv[b][0:rows, 0:blocks, 0], v(rs), ALU.mult), [r])
        return pr.pool(lambda e: e.tensor_scalar(v(nm), v(nm), -1.0, None, ALU.mult), [r], lone=True)

    def normalise_end(b, blocks, rows, ready):
        for j in range(blocks):
            n = pr.act(lambda e, j=j: e.activation(
                kn[b][0:rows, j * D:(j + 1) * D], kn[b][0:rows, j * D:(j + 1) * D], ACT.Identity,
                bias=nm[b][0:rows, j:j + 1], scale=rs[b][0:rows, j:j + 1]), [ready])
        return n

    def to_parts(b, blocks, rows, ready, w, bias, hi, lo, dst_free):
        t = next_of("tb")
        width = (blocks - 1) * P + rows
        for j in range(blocks):
            tt = pr.pe(lambda e, j=j: e.transpose(tb[t][:, j * P:j * P + rows], kn[b][0:rows, j * D:(j + 1) * D],
                                                  ident[0:rows, 0:rows]),
                       [ready] + pr.of(f"tb{t}"), signal=(j == blocks - 1))
        pr.leave(f"kn{b}", tt)
        c = next_of("t32")
        pr.act(lambda e: e.activation(t32[c][:, 0:width], tb[t][:, 0:width], ACT.Identity, scale=dcol(w),
                                      bias=dcol(bias)), [tt] + pr.of(f"t32{c}"))
        h = pr.act(lambda e: e.activation(hi(), tb[t][:, 0:width], ACT.Identity, scale=dcol(w), bias=dcol(bias)),
                   dst_free)
        pr.leave(f"tb{t}", h)
        l = pr.pool(lambda e: e.tensor_tensor(lo(), t32[c][:, 0:width], hi(), ALU.subtract), [h])
        pr.leave(f"t32{c}", l)
        return l

    def stage_a(p):
        def product(dst, kind, tt, c0, width):
            for n, (ic, part) in enumerate((i, j) for i in range(IC) for j in range(2)):
                r = pr.pe(lambda e, ic=ic, part=part, n=n: e.matmul(
                    dst, xq_op(p, kind, ic, tt * P, (tt + 1) * P), wsb[p][:, part, ic, c0:c0 + width],
                    start=(n == 0), stop=(n == 3)), pr.of("pa", f"loaded{p}"), signal=(n == 3))
            return r

        def values(src, dst, r):
            vh = pr.act(lambda e: e.copy(dst(0), src), [r] + pr.of(f"V_read{p}"))
            return pr.dve(lambda e: e.tensor_tensor(dst(1), src, dst(0), ALU.subtract), [vh])

        def keep(src, blocks, rows, r):
            b = next_of("kn", 3)
            dst = kn[b][0:rows, 0:blocks * D].rearrange("p (s d) -> p s d", s=blocks)
            c = pr.act(lambda e: e.copy(dst, src), [r] + pr.of(f"kn{b}"))
            return b, c

        def queries(kind):
            w, c0 = (("qln", CQ), ("qxln", CQX))[kind]
            for tt in range(TB):
                r = product(pa[:, tt * 256:(tt + 1) * 256], kind, tt, c0, 256)
            b, c = keep(pa[:, :].rearrange("p (s d) -> p s d", s=4), 4, P, r)
            pr.leave("pa", c)
            return (b, 4, P, c, w, lambda part: QT[p][:, kind, part, :])

        def self_kv():
            for tt in range(TB):
                product(pa[:, tt * P:(tt + 1) * P], 2, tt, CK, D)
                r = product(pa[:, 256 + tt * P:256 + (tt + 1) * P], 3, tt, CV, D)
            b, c = keep(pa[:, 0:256].rearrange("p (s d) -> p s d", s=2), 2, P, r)
            v = values(pa[:, 256:512].rearrange("p (s d) -> p s d", s=2), lambda part: VS[p][:, part, :, :], r)
            pr.leave("pa", c, v)
            vals.append(v)
            return (b, 2, P, c, "kln", lambda part: KS[p][:, part, :])

        def context_kv(c0):
            k2 = min(2, KT - c0)
            rows = P if c0 + 1 < KT else TAIL
            for s in range(k2):
                t = c0 + s
                for n, (ic, a, w) in enumerate((ic, a, w) for ic in range(IC) for a, w in THREE):
                    r = pr.pe(lambda e, s=s, t=t, n=n, ic=ic, a=a, w=w: e.matmul(
                        pa[0:rows, s * 256:(s + 1) * 256], ctx_op(p, a, ic, t * P, t * P + rows),
                        wsb[p][:, w, ic, CKX:CKX + 256], start=(n == 0), stop=(n == 5)),
                        pr.of("pa", f"loaded{p}"), signal=(s == k2 - 1 and n == 5))
            bank = pa[0:rows, 0:k2 * 256].rearrange("p (s c) -> p s c", s=k2)
            b, c = keep(bank[:, :, 0:D], k2, rows, r)
            v = values(bank[:, :, D:2 * D], lambda part: VX[p][0:rows, part, c0:c0 + k2, :], r)
            pr.leave("pa", c, v)
            vals.append(v)
            if c0 + k2 >= KT:
                pr.leave(f"A_done{p}", r)
            at, width = c0 * P, (k2 - 1) * P + rows
            return (b, k2, rows, c, "kxln", lambda part: KX[p][:, part, at:at + width])

        vals = []
        chunks = [lambda: queries(0), lambda: queries(1), self_kv] + [
            lambda c0=c0: context_kv(c0) for c0 in range(0, KT, 2)]
        needs = {len(chunks) - 1 - i: bank for bank, i in ((0, 5), (1, 3), (2, 1), (3, 0))}
        info, normed, parts = {}, {}, []
        for j in range(len(chunks) + 2):
            if j >= 2:
                b, blocks, rows, r, _, _ = info[j - 2]
                normed[j - 2] = normalise_end(b, blocks, rows, r)
            yield
            if j < len(chunks):
                b, blocks, rows, r, w, dst = chunks[j]()
                info[j] = (b, blocks, rows, normalise_start(b, blocks, rows, r, EPS5), w, dst)
            if j >= 2:
                b, blocks, rows, _, w, dst = info[j - 2]
                parts.append(to_parts(b, blocks, rows, normed[j - 2], w + "_w", w + "_b", lambda dst=dst: dst(0),
                                      lambda dst=dst: dst(1), pr.of(f"QK_read{p}")))
                if j - 2 in needs:
                    pr.leave(f"ready{p}_{needs[j - 2]}", *parts)
            if j == len(chunks) + 1:
                pr.leave(f"values{p}", *vals)
            yield

    SELF0 = 3 * 512 + P
    BANKS = [[(1, 0, 512, 0)], [(1, 512, 1024, 512)], [(1, 1024, 1536, 1024)],
             [(1, 1536, SC, 1536), (0, 0, S, SELF0)]]
    SPLITX = 1024

    def scores(p, q, par, bank):
        free = {0: "expA", 1: "expA", 2: "expB", 3: "expS"}[bank]
        for kind, a, b, at in BANKS[bank]:
            keys = KX[p] if kind else KS[p]
            for n, (qp, kp) in enumerate(((0, 0), (0, 1), (1, 0))):
                last = (kind, n) == (BANKS[bank][-1][0], 2)
                t = pr.pe(lambda e, kind=kind, a=a, b=b, at=at, keys=keys, n=n, qp=qp, kp=kp: e.matmul(
                    score[:, at:at + b - a], QT[p][:, kind, qp, q * P:(q + 1) * P], keys[:, kp, a:b],
                    start=(n == 0), stop=(n == 2)), pr.of(free, f"ready{p}_{bank}"), signal=last)
        pr.leave(f"bank{bank}", t)
        if bank == 3:
            pr.leave(f"QK_read{p}", t)

    def max_a(par):
        t = pr.dve(lambda e: e.tensor_reduce(mxp[par][:, 0:1], score[:, 0:SPLITX], AX.X, ALU.max),
                   pr.of("bank0", "bank1"))

    def max_b(par):
        pr.dve(lambda e: e.tensor_reduce(nmx[par][:, 1:2], score[:, SELF0:SELF0 + S], AX.X, ALU.max, negate=True),
               pr.of("bank3", f"exp{par}"))
        t = pr.dve(lambda e: e.tensor_reduce(mxp[par][:, 1:2], score[:, SPLITX:SC], AX.X, ALU.max), pr.of("bank2"))
        t = pr.dve(lambda e: e.tensor_reduce(nmx[par][:, 0:1], mxp[par][:, :], AX.X, ALU.max, negate=True), [t])
        pr.leave("negmax", t)

    def exps(par):
        w = pr.of("negmax", f"P_read{par}", f"sum_read{par}")
        a = pr.act(lambda e: e.activation(P32[par][:, 0:SPLITX], score[:, 0:SPLITX], ACT.Exp,
                                          bias=nmx[par][:, 0:1], accum_out=sums[par][:, 0:1]), w)
        b = pr.act(lambda e: e.activation(P32[par][:, SPLITX:SC], score[:, SPLITX:SC], ACT.Exp,
                                          bias=nmx[par][:, 0:1], accum_out=sums[par][:, 1:2]), w)
        c = pr.act(lambda e: e.activation(P32[par][:, SC:SC + S], score[:, SELF0:SELF0 + S], ACT.Exp,
                                          bias=nmx[par][:, 1:2], accum_out=sums[par][:, 2:3]), w)
        pr.leave("expA", a)
        pr.leave("expB", b)
        pr.leave("expS", c)
        pr.leave(f"exp{par}", a, b, c)

    CHUNKS = [(1, t, t * P, P if t < KT - 1 else TAIL) for t in range(KT)] + [(0, t, SC + t * P, P) for t in range(TB)]
    GROUPS = [CHUNKS[0:4], CHUNKS[4:8], CHUNKS[8:12], CHUNKS[12:15]]
    group = {}

    def turn_p(par, g):
        t = next_of("tb")
        chunks = GROUPS[g]
        for j, (_, _, at, keys) in enumerate(chunks):
            tt = pr.pe(lambda e, j=j, at=at, keys=keys: e.transpose(
                tb[t][0:keys, j * P:(j + 1) * P], P32[par][:, at:at + keys], ident[:, :]),
                pr.of(f"exp{par}", f"tb{t}"), signal=(j == len(chunks) - 1))
        if g == len(GROUPS) - 1:
            pr.leave(f"P_read{par}", tt)
        pt, w = g % 2, len(chunks) * P
        h = pr.act(lambda e: e.copy(PT[pt][:, 0, 0:w], tb[t][:, 0:w]), [tt] + pr.of(f"PT{pt}"))
        l = pr.dve(lambda e: e.tensor_tensor(PT[pt][:, 1, 0:w], tb[t][:, 0:w], PT[pt][:, 0, 0:w], ALU.subtract), [h])
        pr.leave(f"tb{t}", l)
        group[g] = l

    def times_v(vp, par, q, g):
        pt = g % 2
        for j, (kind, t, _, keys) in enumerate(GROUPS[g]):
            V = VX[vp] if kind else VS[vp]
            at = P if kind else 0
            lastt = KT - 1 if kind else TB - 1
            for n, (a, v) in enumerate(((0, 0), (0, 1), (1, 0))):
                m = pr.pe(lambda e, j=j, t=t, keys=keys, V=V, at=at, n=n, a=a, v=v, lastt=lastt: e.matmul(
                    pv[:, at:at + D], PT[pt][0:keys, a, j * P:(j + 1) * P], V[0:keys, v, t, :],
                    start=(t == 0 and n == 0), stop=(t == lastt and n == 2)),
                    [group[g]] + pr.of("pv", f"values{vp}"), signal=(j == len(GROUPS[g]) - 1 and n == 2))
        pr.leave(f"PT{pt}", m)
        if g == len(GROUPS) - 1:
            pr.leave("pv_full", m)
            pr.leave(f"V_read{vp}", m)

    def finish(vp, par, q):
        h = q % HPG
        a = pr.dve(lambda e: e.tensor_tensor(sums[par][:, 3:4], sums[par][:, 0:1], sums[par][:, 1:2], ALU.add),
                   pr.of(f"exp{par}"))
        a = pr.dve(lambda e: e.reciprocal(rsum[par][:, :], sums[par][:, 2:4]), [a])
        pr.leave(f"sum_read{par}", a)
        y = yq[:, :, q, :]
        for x_ in range(2):
            a = pr.dve(lambda e, x_=x_: e.scalar_tensor_tensor(
                yq[:, x_, q, :], pv[:, x_ * P:(x_ + 1) * P], rsum[par][:, x_:x_ + 1],
                rsm[vp][:, (x_ * HPG + h) * D:(x_ * HPG + h + 1) * D], ALU.mult, ALU.mult),
                [a] + pr.of("pv_full", f"rsm{vp}", "yq_read"))
        pr.leave("pv", a)
        if q == NQ - 1:
            pr.leave(f"finished{vp}", a)
        c = pr.dve(lambda e: e.tensor_scalar(y, y, FP8_MAX, -FP8_MAX, ALU.min, ALU.max), [a])
        pr.leave("yq", round_fp8(pr, y, ye[:, :, :], ym[:, :, :], yt[:, :, :], [c], True))

    def turn_y(slot):
        t = next_of("tb")
        bank = tb[t][:, :].bitcast(BF16)
        for j in range(2 * NQ):
            m = pr.pe(lambda e, j=j: e.transpose(bank[:, j * P:(j + 1) * P], yq[:, j // NQ, j % NQ, :], identb[:, :]),
                      pr.of("yq", f"tb{t}"), signal=(j == 2 * NQ - 1))
        pr.leave("yq_read", m)
        c = pr.dve(lambda e: e.tensor_copy(catq[:, bass.ds(slot(pr.i) * (2 * NQ * P), 2 * NQ * P)], bank), [m])
        pr.leave(f"tb{t}", c)

    def block(kk, gen, slot, nxt):
        p, q, par = kk // NQ % 2, kk % NQ, kk % 2
        lk = (kk - 1) % (2 * NQ)
        lp, lq, lpar = lk // NQ, lk % NQ, lk % 2
        turn_p(lpar, 0)
        scores(p, q, par, 0)
        turn_p(lpar, 1)
        scores(p, q, par, 1)
        max_a(par)
        next(gen, None)
        next(gen, None)
        times_v(lp, lpar, lq, 0)
        scores(p, q, par, 2)
        scores(p, q, par, 3)
        max_b(par)
        next(gen, None)
        turn_p(lpar, 2)
        times_v(lp, lpar, lq, 1)
        turn_p(lpar, 3)
        exps(par)
        next(gen, None)
        if q == 1:
            turn_y(slot)
        times_v(lp, lpar, lq, 2)
        times_v(lp, lpar, lq, 3)
        finish(lp, lpar, lq)
        next(gen, None)
        next(gen, None)
        if q == 0:
            load_rsm(lp, nxt)

    pr.straight()
    for t in P32[1:] + sums[1:]:
        pr.pool(lambda e, t=t: e.memset(t[:, :], 1.0))
    pr.pool(lambda e: e.memset(yq[:, :, :, :], 1.0))
    for t in (VX[1], VS[1]):
        pr.pool(lambda e, t=t: e.memset(t[:, :, :, :], 1.0))
    load(0, lambda i: 0)
    load(1, lambda i: 1)
    load_rsm(0, lambda i: 0)
    load_rsm(1, lambda i: 0)
    for _ in stage_a(0):
        pass

    def names():
        return (["pa", "pv", "pv_full", "expA", "expB", "expS", "negmax", "yq", "yq_read", "tb0", "tb1", "kn0", "kn1",
                 "kn2", "t320", "t321", "PT0", "PT1"]
                + [f"{n}{p}" for p in range(2) for n in ("A_done", "loaded", "values", "QK_read", "V_read", "exp",
                                                         "P_read", "sum_read", "rsm", "finished")]
                + [f"ready{p}_{bank}" for p in range(2) for bank in range(4)])

    pr.loop(NGB // 2)
    pr.carry(*names())
    for half in range(2):
        if half == 0:
            load(0, lambda i: i * 2 + 2)
        gen = stage_a(1 - half)
        for q in range(NQ):
            block(half * NQ + q, gen, lambda i, half=half: i * 2 + half, lambda i, half=half: i * 2 + half + 1)
        for _ in gen:
            pass
        if half == 0:
            load(1, lambda i: i * 2 + 3)
    pr.straight()
    turn.update(tb=0)
    for g in range(4):
        turn_p(1, g)
        times_v(1, 1, NQ - 1, g)
    finish(1, 1, NQ - 1)
    turn_y(lambda i: NGB)


def layer0_projection(k, sb):
    pr, A, x, catq, gate = k["pr"], k["A"], k["x"], k["catq"], k["gate"]
    score = k["score"]
    NCH = 2 * G * HPG
    wf = [sb(f"wpf{i}", [P, 8, H], F32) for i in range(2)]
    wp = sb("wp", [P, 2, NCH, H], BF16)
    free = [[], []]
    pr.straight()
    los = []
    for c in range(0, NCH, 8):
        p = c // 8 % 2
        l = pr.dma(f"wp{p}", lambda e, c=c, p=p: e.dma_start(wf[p][:, :, :], A["wprojT"][:, c:c + 8, :]), free[p])
        h = pr.act(lambda e, c=c, p=p: e.copy(wp[:, 0, c:c + 8, :], wf[p][:, :, :]), [l])
        lo = pr.dve(lambda e, c=c, p=p: e.tensor_tensor(wp[:, 1, c:c + 8, :], wf[p][:, :, :], wp[:, 0, c:c + 8, :],
                                                        ALU.subtract), [h])
        free[p] = [lo]
        los.append(lo)
    done = [[], [], [], []]
    for t in range(NT):
        b, tt, bank = t // TB, t % TB, t % 4
        acc = score[:, bank * 512:bank * 512 + H]
        n = 0
        for g in range(G):
            for x_ in range(2):
                for h in range(HPG):
                    at = ((g * B + b + 1) * 2 * NQ + (x_ * TB + tt) * HPG + h) * P
                    chunk = (g * 2 + x_) * HPG + h
                    for part in range(2):
                        m = pr.pe(lambda e, acc=acc, at=at, chunk=chunk, part=part, n=n: e.matmul(
                            acc, catq[:, at:at + P], wp[:, part, chunk, :], start=(n == 0), stop=(n == 2 * NCH - 1)),
                            los[chunk // 8:chunk // 8 + 1] + done[bank], signal=(n == 2 * NCH - 1))
                        n += 1
        d = pr.dve(lambda e, acc=acc, t=t: e.scalar_tensor_tensor(x[:, t, :], acc, gate[:, 0:1], x[:, t, :],
                                                                  ALU.mult, ALU.add), [m])
        done[bank] = [d]
        pr.leave("x", d)


def split(pr, src, hi, lo, after, hi_free=()):
    h = pr.act(lambda e: e.copy(hi, src), list(after) + list(hi_free))
    return pr.dve(lambda e: e.tensor_tensor(lo, src, hi, ALU.subtract), [h])


def norm_transposed(k, sb, name, eps, want32=False):
    pr, x, ident, score = k["pr"], k["x"], k["ident"], k["score"]
    xn = sb(name + "_xn", [P, NT, H], F32)
    xT = sb(name + "_xT", [P, 2, IC, NT * P], BF16)
    x32 = sb(name + "_x32", [P, IC, NT * P], F32) if want32 else None
    a = layernorm_rows(pr, 0, x, xn, k["st"], k["mv"], k["rs"], k["mhalf"], eps, NT, [])
    outs = []
    for ic in range(IC):
        for q in range(2):
            bank = score[:, (2 * ic + q) * 512:(2 * ic + q + 1) * 512]
            cols = slice(q * 512, (q + 1) * 512)
            for t in range(4):
                tt = pr.pe(lambda e, bank=bank, t=t, q=q, ic=ic: e.transpose(
                    bank[:, t * P:(t + 1) * P], xn[:, 4 * q + t, ic * P:(ic + 1) * P], ident[:, :]), [a],
                    signal=(t == 3))
            w = split(pr, bank, xT[:, 0, ic, cols], xT[:, 1, ic, cols], [tt])
            if want32:
                w = pr.act(lambda e, bank=bank, ic=ic, cols=cols: e.copy(x32[:, ic, cols], bank), [w])
            outs.append(w)
    return xT, x32, outs


THREE = ((0, 0), (0, 1), (1, 0))


def layer0_ffn(k, sb):
    pr, A, x, gate, ident = k["pr"], k["A"], k["x"], k["gate"], k["ident"]
    score, tb, pv, pa = k["score"], k["tb"], k["pv"], k["pa"]
    pr.straight()
    wg = sb("wg", [P, IC, NE], F32)
    brow = sb("brow", [P, NE], F32)
    ld = pr.dma("in", lambda e: e.dma_start(wg[:, :, :], A["wgT"]))
    ld = pr.dma("in", lambda e: e.dma_start(brow[:, :], A["ffn_bias"].partition_broadcast(P)))
    w13f = [sb(f"w13f{i}", [P, IC, NE * FF], F32) for i in range(2)]
    w2f = sb("w2f", [P, NE, H], F32)
    w13 = sb("w13", [P, 2, 2, IC, NE * FF], BF16)
    w2 = sb("w2", [P, 2, NE, H], BF16)
    wr = []
    for i, n in enumerate(("w1T", "w3T")):
        l = pr.dma(f"w{i}", lambda e, i=i, n=n: e.dma_start(w13f[i][:, :, :], A[n]))
        wr.append(split(pr, w13f[i][:, :, :], w13[:, i, 0, :, :], w13[:, i, 1, :, :], [l]))
    l = pr.dma("ws0", lambda e: e.dma_start(w2f[:, :, :], A["w2T"]))
    w2r = split(pr, w2f[:, :, :], w2[:, 0, :, :], w2[:, 1, :, :], [l])
    xT, x32, ready = norm_transposed(k, sb, "f", EPS5, want32=True)

    lg = pv[:, 0:NT * NE]
    for t in range(NT):
        for ic in range(IC):
            m = pr.pe(lambda e, t=t, ic=ic: e.matmul(lg[:, t * NE:(t + 1) * NE], x32[:, ic, t * P:(t + 1) * P],
                                                     wg[:, ic, :], start=(ic == 0), stop=(ic == IC - 1)),
                      ready + [ld], signal=(t == NT - 1 and ic == IC - 1))
    small = lambda n: sb(n, [P, NT, NE], F32)
    ex, sig, s1, eq, key, oh, oh2, ew = (small("r_" + n) for n in ("ex", "sig", "s1", "eq", "key", "oh", "oh2", "ew"))
    rank = small("r_rank")
    mx = sb("r_mx", [P, NT], F32)
    for e_ in range(NE):
        rk = pr.pool(lambda e, e_=e_: e.memset(rank[:, :, e_:e_ + 1], float(NE - e_)))
    bc = lambda ap: ap.unsqueeze(2).broadcast_to([P, NT, NE])
    a = pr.act(lambda e: e.activation(ex[:, :, :].rearrange("p a b -> p (a b)"), lg, ACT.Exp, scale=-1.0), [m])
    a = pr.dve(lambda e: e.tensor_scalar(ex[:, :, :], ex[:, :, :], 1.0, None, ALU.add), [a])
    a = pr.dve(lambda e: e.reciprocal(sig[:, :, :], ex[:, :, :]), [a])
    a = pr.dve(lambda e: e.tensor_tensor(s1[:, :, :], sig[:, :, :],
                                         brow[:, :].unsqueeze(1).broadcast_to([P, NT, NE]), ALU.add), [a])
    for hot in (oh, oh2):
        a = pr.dve(lambda e: e.tensor_reduce(mx[:, :], s1[:, :, :], AX.X, ALU.max), [a])
        a = pr.dve(lambda e: e.tensor_tensor(eq[:, :, :], s1[:, :, :], bc(mx[:, :]), ALU.is_equal), [a])
        a = pr.dve(lambda e: e.tensor_tensor(key[:, :, :], eq[:, :, :], rank[:, :, :], ALU.mult), [a, rk])
        a = pr.dve(lambda e: e.tensor_reduce(mx[:, :], key[:, :, :], AX.X, ALU.max), [a])
        a = pr.dve(lambda e, hot=hot: e.tensor_tensor(hot[:, :, :], key[:, :, :], bc(mx[:, :]), ALU.is_equal), [a])
        if hot is oh:
            a = pr.dve(lambda e: e.scalar_tensor_tensor(s1[:, :, :], oh[:, :, :], -1e30, s1[:, :, :],
                                                        ALU.mult, ALU.add), [a])
    a = pr.dve(lambda e: e.tensor_tensor(oh[:, :, :], oh[:, :, :], oh2[:, :, :], ALU.add), [a])
    a = pr.dve(lambda e: e.tensor_tensor(oh[:, :, :], oh[:, :, :], sig[:, :, :], ALU.mult), [a])
    a = pr.dve(lambda e: e.tensor_reduce(mx[:, :], oh[:, :, :], AX.X, ALU.add), [a])
    a = pr.dve(lambda e: e.reciprocal(mx[:, :], mx[:, :]), [a])
    ewr = pr.dve(lambda e: e.scalar_tensor_tensor(ew[:, :, :], oh[:, :, :], 0.5, bc(mx[:, :]), ALU.mult, ALU.mult), [a])

    th = [sb(f"f_th{i}", [P, 512], F32) for i in range(2)]
    gg = [sb(f"f_g{i}", [P, 512], F32) for i in range(2)]
    gT = [sb(f"f_gT{i}", [P, 2, 512], BF16) for i in range(2)]
    EH = NE // 2
    pairs = [(t, hf) for t in range(NT) for hf in range(2)]
    state = {}

    def up(n):
        t, hf = pairs[n]
        i = n % 2
        free = pr.of(f"h{i}")
        toks = []
        for w in range(2):
            bank = score[:, (2 * i + w) * 512:(2 * i + w + 1) * 512]
            passes = [(ic, a, b) for ic in range(IC) for a, b in THREE]
            for s, (ic, a, b) in enumerate(passes):
                m = pr.pe(lambda e, bank=bank, w=w, ic=ic, a=a, b=b, s=s: e.matmul(
                    bank, xT[:, a, ic, t * P:(t + 1) * P], w13[:, w, b, ic, hf * 512:(hf + 1) * 512],
                    start=(s == 0), stop=(s == 5)), free + wr + ready, signal=(s == 5))
            toks.append(m)
        h1, h3 = (score[:, (2 * i + w) * 512:(2 * i + w + 1) * 512] for w in range(2))
        a = pr.act(lambda e: e.activation(th[i][:, :], h1, ACT.Tanh, scale=0.5), [toks[0]] + pr.of(f"th{i}"))
        a = pr.dve(lambda e: e.scalar_tensor_tensor(th[i][:, :], th[i][:, :], 1.0, h1, ALU.add, ALU.mult), [a])
        a = pr.dve(lambda e: e.tensor_tensor(th[i][:, :], th[i][:, :], h3, ALU.mult), [a, toks[1]])
        pr.leave(f"h{i}", a)
        w_ = ew[:, t, hf * EH:(hf + 1) * EH].unsqueeze(2).broadcast_to([P, EH, FF])
        a = pr.dve(lambda e: e.tensor_tensor(gg[i][:, :].rearrange("p (a b) -> p a b", a=EH),
                                             th[i][:, :].rearrange("p (a b) -> p a b", a=EH), w_, ALU.mult),
                   [a, ewr] + pr.of(f"gg{i}"))
        pr.leave(f"th{i}", a)
        state[n] = a

    def down(n):
        t, hf = pairs[n]
        i = n % 2
        for j in range(EH):
            m = pr.pe(lambda e, j=j: e.transpose(tb[i][:, j * P:(j + 1) * P], gg[i][:, j * FF:(j + 1) * FF], ident[:, :]),
                      [state[n]] + pr.of(f"tbf{i}"), signal=(j == EH - 1))
        pr.leave(f"gg{i}", m)
        s = split(pr, tb[i][:, :], gT[i][:, 0, :], gT[i][:, 1, :], [m], pr.of(f"gT{i}"))
        pr.leave(f"tbf{i}", s)
        acc = (pv, pa)[t % 2]
        for j in range(EH):
            for c, (a, b) in enumerate(THREE):
                first, last = (hf, j, c) == (0, 0, 0), (hf, j, c) == (1, EH - 1, 2)
                m = pr.pe(lambda e, j=j, a=a, b=b, first=first, last=last, acc=acc: e.matmul(
                    acc[:, 0:H], gT[i][:, a, j * P:(j + 1) * P], w2[:, b, hf * EH + j, :], start=first, stop=last),
                    [s, w2r, ewr] + pr.of(f"acc{t % 2}"), signal=(j == EH - 1 and c == 2))
        pr.leave(f"gT{i}", m)
        if hf == 1:
            d = pr.dve(lambda e, acc=acc, t=t: e.scalar_tensor_tensor(x[:, t, :], acc[:, 0:H], gate[:, 2:3], x[:, t, :],
                                                                      ALU.mult, ALU.add), [m])
            pr.leave(f"acc{t % 2}", d)
            pr.leave("x", d)

    up(0)
    for n in range(1, len(pairs)):
        up(n)
        down(n - 1)
    down(len(pairs) - 1)


def layer1_attention(k, sb):
    pr, A, x, gate, ident, identb = k["pr"], k["A"], k["x"], k["gate"], k["ident"], k["identb"]
    score, tb, pv, pa, mhalf = k["score"], k["tb"], k["pv"], k["pa"], k["mhalf"]
    HQ, R = NH1 // 4, 4 * D1
    VC = 16
    wf = sb("l1_wf", [P, IC, 3 * H], F32)
    w1 = sb("l1_w", [P, 2, IC, 3 * H], BF16)
    stg = [sb(f"l1_ctx{i}", [P, 2, IC, SC], BF16) for i in range(2)]
    QB = [sb(f"QB{i}", [P, HQ, 4, S], BF16) for i in range(2)]
    KT1 = [sb(f"KT1_{i}", [P, HQ, SC], BF16) for i in range(2)]
    V1 = [sb(f"V1_{i}", [P, KT, NH1, VC], F32) for i in range(2)]
    P1 = [sb(f"P1_{i}", [P, 4 * S], F32) for i in range(3)]
    xn = sb("l1_xn", [P, TB, H], F32)
    xT = sb("l1_xT", [P, 2, IC, P], BF16)
    st, mv, rs = sb("l1_st", [P, TB, 6], F32), sb("l1_mv", [P, TB, 2], F32), sb("l1_rs", [P, TB], F32)
    sq = sb("l1_sq", [P, H], F32)
    ss, rr, kn = ([sb(f"l1_{n}{i}", [P, w], F32) for i in range(3)] for n, w in (("ss", NH1), ("rr", NH1), ("kn", H)))
    stack = [sb(f"l1_stack{i}", [P, NH1, 4, D1], BF16) for i in range(2)]
    OS = [sb(f"l1_O{i}", [P, S], F32) for i in range(2)]
    den = sb("l1_den", [P, TB, 4], F32)
    att = sb("l1_att", [P, TB, 4, D1], F32)

    pr.straight()
    l = pr.dma("w0", lambda e: e.dma_start(wf[:, :, :], A["l1_wT"]))
    split(pr, wf[:, :, :], w1[:, 0, :, :], w1[:, 1, :, :], [l])
    for i in range(2):
        z = pr.pool(lambda e, i=i: e.memset(QB[i][:, :, :, :], 0.0))
        z = pr.pool(lambda e, i=i: e.memset(V1[i][:, :, :, :], 0.0))
        pr.pool(lambda e, i=i: e.memset(V1[i][:, :, :, D1:D1 + 1], 1.0), [z])
    pr.dve(lambda e: e.memset(pv[:, :], 0.0))

    def load(p, n):
        a = pr.dma(f"ld{p}", lambda e: e.dma_start(
            stg[p][:, :, :, :].rearrange("p a b c -> p (a b c)").rearrange("p (o c) -> p o c", o=1),
            k["stage_d"][bass.ds(n(pr.i) % B, 1), :, 0:2 * IC * SC].rearrange("o p c -> p o c")), pr.of(f"prepared{p}"))
        pr.leave(f"loaded{p}", a)

    def rms_start(c, bank, rows, ready):
        b = c % 3
        k_ = pr.act(lambda e: e.copy(kn[b][0:rows, :], bank), [ready] + pr.of(f"kn{b}"))
        a = pr.dve(lambda e: e.tensor_tensor(sq[0:rows, :], kn[b][0:rows, :], kn[b][0:rows, :], ALU.mult), [k_])
        a = pr.dve(lambda e: e.tensor_reduce(ss[b][0:rows, :], sq[0:rows, :].rearrange("p (h d) -> p h d", d=D1),
                                             AX.X, ALU.add), [a])
        a = pr.pool(lambda e: e.tensor_scalar(rr[b][0:rows, :], ss[b][0:rows, :], 1.0 / D1, EPS6, ALU.mult, ALU.add),
                    [a], lone=True)
        return k_, pr.pool(lambda e: e.tensor_tensor(rr[b][0:rows, :], rr[b][0:rows, :], mhalf[0:rows, 0:NH1],
                                                     ALU.pow), [a])

    def rms_stack(c, rows, ready, keys):
        b, s = c % 3, c % 2
        heads = kn[b][0:rows, :].rearrange("p (h d) -> p h d", d=D1)
        a = pr.dve(lambda e: e.tensor_tensor(heads, heads, rr[b][0:rows, :].unsqueeze(2).broadcast_to(
            [rows, NH1, D1]), ALU.mult), [ready])
        twice = heads.unsqueeze(2).broadcast_to([rows, NH1, 2, D1])
        part = lambda i: stack[s][0:rows, :, 2 * i:2 * i + 2, :] if keys else stack[s][0:rows, :, i::2, :]
        a = pr.dve(lambda e: e.tensor_copy(part(0), twice), [a] + pr.of(f"stack{s}"))
        a = pr.dve(lambda e: e.tensor_tensor(part(1), twice, part(0), ALU.subtract), [a])
        pr.leave(f"kn{b}", a)
        return a

    def turn_stack(c, rows, ready):
        s = c % 2
        bank = tb[1][:, :].bitcast(BF16)
        st_ = stack[s][:, :, :, :].rearrange("p h s d -> p (h s d)")
        for q in range(HQ):
            m = pr.pe(lambda e, q=q: e.transpose(bank[:, q * P:q * P + rows], st_[0:rows, q * P:(q + 1) * P],
                                                 identb[0:rows, 0:rows]), [ready] + pr.of("tb1"), signal=(q == HQ - 1))
        pr.leave(f"stack{s}", m)
        return bank.rearrange("p (q t) -> p q t", q=HQ)[:, :, 0:rows], m

    def prepare(p, n):
        outs, made, stacked, norm = [], {}, {}, {}
        xrow = lambda t: x[:, bass.ds(n(pr.i) % B * TB + t, 1), :].rearrange("p o d -> p (o d)")

        def norm_start():
            for t in range(TB):
                a = pr.dve(lambda e, t=t: e.bn_stats(st[:, t, :], xrow(t)), pr.of("x"))
            for t in range(TB):
                a = pr.dve(lambda e, t=t: e.bn_aggr(mv[:, t, :], st[:, t, :]), [a], lone=True)
            a = pr.pool(lambda e: e.tensor_scalar(rs[:, :], mv[:, :, 1], EPS5, None, ALU.add), [a], lone=True)
            norm["rs"] = pr.pool(lambda e: e.tensor_tensor(rs[:, :], rs[:, :], mhalf[:, 0:TB], ALU.pow), [a])

        def norm_end():
            for t in range(TB):
                norm["x"] = pr.dve(lambda e, t=t: e.tensor_scalar(
                    xn[:, t, :], xrow(t), mv[:, t, 0:1], rs[:, t:t + 1], ALU.subtract, ALU.mult),
                    [norm["rs"]] + pr.of("xn_read"))

        def turn_x(t):
            for ic in range(IC):
                m = pr.pe(lambda e, ic=ic: e.transpose(tb[0][:, ic * P:(ic + 1) * P], xn[:, t, ic * P:(ic + 1) * P],
                                                       ident[:, :]), [norm["x"]] + pr.of("tb0"), signal=(ic == IC - 1))
            pr.leave("xn_read", m)
            s = split(pr, tb[0][:, 0:IC * P], xT[:, 0, :, :].rearrange("p i t -> p (i t)"),
                      xT[:, 1, :, :].rearrange("p i t -> p (i t)"), [m], pr.of("xT_read"))
            pr.leave("tb0", s)
            norm["xT"] = s

        def query_product(t):
            for i, (ic, a, b) in enumerate((ic, a, b) for ic in range(IC) for a, b in THREE):
                m = pr.pe(lambda e, ic=ic, a=a, b=b, i=i: e.matmul(
                    pa[:, 0:H], xT[:, a, ic, :], w1[:, b, ic, 0:H], start=(i == 0), stop=(i == 5)),
                    [norm["xT"]] + pr.of("pa"), signal=(i == 5))
            pr.leave("xT_read", m)
            read, made[t] = rms_start(t, pa[:, 0:H], P, m)
            pr.leave("pa", read)

        def key_product(c):
            t, rows = c - TB, P if c - TB < KT - 1 else TAIL
            for i, (ic, a, b) in enumerate((ic, a, b) for ic in range(IC) for a, b in THREE):
                m = pr.pe(lambda e, ic=ic, a=a, b=b, i=i: e.matmul(
                    pa[0:rows, :], stg[p][:, a, ic, t * P:t * P + rows], w1[:, b, ic, H:3 * H],
                    start=(i == 0), stop=(i == 5)), pr.of("pa", f"loaded{p}"), signal=(i == 5))
            read, made[c] = rms_start(c, pa[0:rows, 0:H], rows, m)
            v = pr.act(lambda e: e.copy(V1[p][0:rows, t, :, 0:D1], pa[0:rows, H:2 * H].rearrange(
                "p (h d) -> p h d", d=D1)), [m] + pr.of(f"V_read{p}"))
            outs.append(v)
            pr.leave("pa", read, v)
            if t == KT - 1:
                pr.leave(f"prepared{p}", m)

        def finish(c):
            rows = TAIL if c == chunks - 1 else P
            bank, m = turn_stack(c, rows, stacked[c])
            if c < TB:
                for j in range(4):
                    r = pr.dve(lambda e, j=j: e.tensor_copy(
                        QB[p][j * R:(j + 1) * R, :, j, c * P:(c + 1) * P], bank[j * R:(j + 1) * R, :, :]),
                        [m] + pr.of(f"QK_read{p}"))
            else:
                at = (c - TB) * P
                r = pr.dve(lambda e: e.tensor_copy(KT1[p][:, :, at:at + rows], bank), [m] + pr.of(f"QK_read{p}"))
            pr.leave("tb1", r)
            outs.append(r)

        def stack_up(c):
            stacked[c] = rms_stack(c, TAIL if c == chunks - 1 else P, made[c], c >= TB)

        chunks = TB + KT
        at = lambda c: 4 + 3 * c
        work = [[] for _ in range(at(chunks - 1) + 6)]
        work[0].append(norm_start)
        work[1].append(norm_end)
        for c in range(chunks):
            if c < TB:
                work[at(c) - 1].append(lambda c=c: turn_x(c))
            work[at(c)].append(lambda c=c: query_product(c) if c < TB else key_product(c))
            work[at(c) + 4].append(lambda c=c: stack_up(c))
            work[at(c) + 5].append(lambda c=c: finish(c))
        for pieces in work:
            for piece in pieces:
                piece()
            yield
        pr.leave(f"ready{p}", *outs)

    def attend(p, n, gen):
        steps = [(hq, t) for hq in range(HQ) for t in range(KT)]
        exps, copied = {}, {}

        def first(i):
            hq, t = steps[i]
            rows = P if t < KT - 1 else TAIL
            d = i % 2
            for h in range(2):
                m = pr.pe(lambda e, h=h: e.matmul(
                    score[0:rows, (2 * d + h) * 512:(2 * d + h + 1) * 512], KT1[p][:, hq, t * P:t * P + rows],
                    QB[p][:, hq, 2 * h:2 * h + 2, :], start=True, stop=True),
                    pr.of(f"s{d}", f"ready{p}"), signal=(h == 1))
            if i == len(steps) - 1:
                pr.leave(f"QK_read{p}", m)
            b = i % 3
            a = pr.act(lambda e: e.activation(P1[b][0:rows, :], score[0:rows, d * 1024:(d + 1) * 1024], ACT.Exp,
                                              scale=float(D1) ** -0.5), [m] + pr.of(f"P{b}"))
            pr.leave(f"s{d}", a)
            exps[i] = a

        def second(i):
            hq, t = steps[i]
            rows = P if t < KT - 1 else TAIL
            b, o = i % 3, hq % 2
            for j in range(4):
                m = pr.pe(lambda e, j=j: e.matmul(
                    pv[j * R:j * R + VC, 0:S], V1[p][0:rows, t, 4 * hq + j, :],
                    P1[b][0:rows, j * S:(j + 1) * S], start=(t == 0), stop=(t == KT - 1), skip_group_check=True),
                    [exps[i]] + pr.of("pv"), signal=(j == 3))
            pr.leave(f"P{b}", m)
            if i == len(steps) - 1:
                pr.leave(f"V_read{p}", m)
            if t == KT - 1:
                c = pr.dve(lambda e: e.tensor_copy(OS[o][:, :], pv[:, 0:S]), [m] + pr.of(f"OS{o}"))
                pr.leave("pv", c)
                copied[hq] = c

        def third(hq):
            o = hq % 2
            for tt in range(TB):
                m = pr.pe(lambda e, tt=tt: e.transpose(tb[0][:, tt * P:(tt + 1) * P], OS[o][:, tt * P:(tt + 1) * P],
                                                       ident[:, :]), [copied[hq]] + pr.of("tb0"), signal=(tt == TB - 1))
            pr.leave(f"OS{o}", m)
            v = tb[0][:, 0:TB * P].rearrange("p (t h c) -> p t h c", t=TB, h=4)
            r = pr.dve(lambda e: e.reciprocal(den[:, :, :], v[:, :, :, D1]), [m])
            r = pr.dve(lambda e: e.tensor_tensor(att[:, :, :, :], v[:, :, :, 0:D1],
                                                 den[:, :, :].unsqueeze(3).broadcast_to([P, TB, 4, D1]),
                                                 ALU.mult), [r])
            pr.leave("tb0", r)

            def xs():
                return x[:, bass.ds(n(pr.i) % B * TB, TB), hq * R:(hq + 1) * R]
            r = pr.dve(lambda e: e.scalar_tensor_tensor(
                xs(), att[:, :, :, :].rearrange("p t h d -> p t (h d)"), gate[:, 1:2], xs(), ALU.mult, ALU.add), [r])
            pr.leave("x", r)

        first(0)
        for i in range(len(steps)):
            if i + 1 < len(steps):
                first(i + 1)
            if i % 2 == 1:
                next(gen, None)
            second(i)
            hq, t = steps[i]
            if hq and t == 1:
                third(hq - 1)
        for _ in gen:
            pass
        third(HQ - 1)

    pr.straight()
    load(0, lambda i: 0)
    load(1, lambda i: 1)
    for _ in prepare(0, lambda i: 0):
        pass
    pr.loop(B // 2)
    pr.carry(*(["x", "xn_read", "xT_read", "tb0", "tb1", "pa", "pv", "kn0", "kn1", "kn2", "stack0",
                "stack1", "s0", "s1", "P0", "P1", "P2", "OS0", "OS1"]
               + [f"{n}{p}" for p in range(2) for n in ("loaded", "prepared", "QK_read", "V_read", "ready")]))
    load(0, lambda i: 2 * i + 2)
    attend(0, lambda i: 2 * i, prepare(1, lambda i: 2 * i + 1))
    load(1, lambda i: 2 * i + 3)
    attend(1, lambda i: 2 * i + 1, prepare(0, lambda i: 2 * i + 2))


def layer1_ffn(k, sb):
    pr, A, x, gate, sc = k["pr"], k["A"], k["x"], k["gate"], k["sc"]
    score = k["score"]
    pr.straight()
    pw, nw = (sb(n, [P, IC, H, NBITS], F32) for n in ("b_pw", "b_nw"))
    pb, nb = (sb(n, [P, H, NBITS], F32) for n in ("b_pb", "b_nb"))
    bits = sb("b_bits", [P, 3, NBITS], F32)
    wT32 = sb("b_w32", [P, IC, H], F32)
    wT = sb("b_w", [P, 2, IC, H], BF16)
    coef = sb("b_coef", [P, NBITS], F32)
    bias = sb("b_bias", [P, H], F32)
    l1 = pr.dma("w0", lambda e: e.dma_start(pw[:, :, :, :], A["pweight"]))
    l2 = pr.dma("w1", lambda e: e.dma_start(nw[:, :, :, :], A["nweight"]))
    pr.dma("in", lambda e: e.dma_start(pb[:, :, :].rearrange("p a b -> p (a b)"), A["pbias"].partition_broadcast(P)))
    pr.dma("in", lambda e: e.dma_start(nb[:, :, :].rearrange("p a b -> p (a b)"), A["nbias"].partition_broadcast(P)))
    l3 = pr.dma("in", lambda e: e.dma_start(bits[:, :, :].rearrange("p a b -> p (a b)"),
                                            A["bits"].partition_broadcast(P)))
    flat = lambda t: t[:, :, :, :].rearrange("p a b c -> p (a b c)")
    t1 = pr.act(lambda e: e.activation(flat(pw), flat(pw), ACT.Tanh, scale=0.5), [l1])
    t2 = pr.act(lambda e: e.activation(flat(nw), flat(nw), ACT.Tanh, scale=0.5), [l2])
    c = pr.act(lambda e: e.activation(coef[:, :], bits[:, 2, :], ACT.Exp, scale=-1.0), [l3])
    c = pr.dve(lambda e: e.tensor_scalar(coef[:, :], coef[:, :], 1.0, None, ALU.add), [c])
    c = pr.dve(lambda e: e.reciprocal(coef[:, :], coef[:, :]), [c])
    c = pr.dve(lambda e: e.tensor_tensor(coef[:, :], coef[:, :], bits[:, 0, :], ALU.mult), [c])
    c = pr.dve(lambda e: e.tensor_scalar(coef[:, :], coef[:, :], sc("scale"), 0.5, ALU.mult, ALU.mult), [c])
    d = pr.dve(lambda e: e.tensor_tensor(flat(pw), flat(pw), flat(nw), ALU.subtract), [t1, t2])
    pv3 = pw[:, :, :, :].rearrange("p a b c -> p (a b) c")
    d = pr.dve(lambda e: e.tensor_tensor(pv3, pv3, coef[:, :].unsqueeze(1).broadcast_to([P, IC * H, NBITS]),
                                         ALU.mult), [d, c])
    d = pr.dve(lambda e: e.tensor_reduce(wT32[:, :, :].rearrange("p a b -> p (a b)"), pv3, AX.X, ALU.add), [d])
    wr = split(pr, wT32[:, :, :], wT[:, 0, :, :], wT[:, 1, :, :], [d])
    b = pr.dve(lambda e: e.tensor_tensor(pb[:, :, :], pb[:, :, :], nb[:, :, :], ALU.subtract), [l3])
    b = pr.dve(lambda e: e.tensor_tensor(pb[:, :, :], pb[:, :, :],
                                         bits[:, 1, :].unsqueeze(1).broadcast_to([P, H, NBITS]), ALU.mult), [b])
    b = pr.dve(lambda e: e.tensor_reduce(bias[:, :], pb[:, :, :], AX.X, ALU.add), [b])
    step = float(2 ** NBITS - 1)
    b = pr.dve(lambda e: e.tensor_scalar(bias[:, :], bias[:, :], 1.0, -1.0, ALU.min, ALU.max), [b])
    b = pr.dve(lambda e: e.tensor_scalar(bias[:, :], bias[:, :], step, ROUND_INT, ALU.mult, ALU.add), [b])
    b = pr.dve(lambda e: e.tensor_scalar(bias[:, :], bias[:, :], ROUND_INT, 1.0 / step, ALU.subtract, ALU.mult), [b])
    b = pr.dve(lambda e: e.tensor_scalar(bias[:, :], bias[:, :], sc("bscale"), gate[:, 3:4], ALU.mult, ALU.mult), [b])
    xT, _, ready = norm_transposed(k, sb, "g", EPS5)
    done = pr.of()
    passes = [(ic, a, c_) for ic in range(IC) for a, c_ in THREE]
    free = {i: list(ready) for i in range(4)}
    for t in range(NT):
        i = t % 4
        bank = score[:, i * 512:i * 512 + H]
        for n, (ic, a, w) in enumerate(passes):
            m = pr.pe(lambda e, t=t, ic=ic, a=a, w=w, n=n, bank=bank: e.matmul(
                bank, xT[:, a, ic, t * P:(t + 1) * P], wT[:, w, ic, :], start=(n == 0), stop=(n == 5)),
                free[i] + [wr], signal=(n == 5))
        d = pr.dve(lambda e, t=t, bank=bank: e.scalar_tensor_tensor(x[:, t, :], bank, gate[:, 3:4], x[:, t, :],
                                                                    ALU.mult, ALU.add), [m])
        free[i] = [d]
        d = pr.dve(lambda e, t=t: e.tensor_tensor(x[:, t, :], x[:, t, :], bias[:, :], ALU.add), [d, b])
    pr.leave("x", d)


def kernel(**inputs):
    import numpy as np
    import concourse.bacc as bacc
    from concourse.bass_utils import run_bass_kernel_spmd

    nc = bacc.Bacc("TRN2", target_bir_lowering=False, num_devices=1)
    arrays, A = {}, {}
    for name, a in layout(np, inputs).items():
        arrays["in_" + name] = a
        A[name] = nc.dram_tensor("in_" + name, a.shape, mybir.dt.from_np(a.dtype), kind="ExternalInput").ap()
    out = nc.dram_tensor("out_0", (B * S, H), F32, kind="ExternalOutput").ap()
    build(nc, A, out)
    r = run_bass_kernel_spmd(nc, [arrays], core_ids=[0])
    return np.asarray(r.results[0]["out_0"]).reshape(B, S, H)


def layout(np, v):
    a = {n: np.ascontiguousarray(np.asarray(z)) for n, z in v.items()}
    l0 = lambda n: a["L0_xattn_" + n]

    def chunked(w):
        return w.reshape(w.shape[0] // P, P, -1).transpose(1, 0, 2)

    out = {}
    out["x"] = a["x"].reshape(B * S, H)
    out["ctxT"] = np.ascontiguousarray(chunked(a["ctx_2048"].reshape(B * SC, H).T).reshape(P, IC, B, SC))
    wt = {n: l0(n).T for n in ("wq", "wqx", "wk", "wv")}
    kv = l0("w_kv_x").T
    groups = []
    for g in range(G):
        s2, s1 = slice(g * HPG * D, (g + 1) * HPG * D), slice(g * D, (g + 1) * D)
        groups.append(chunked(np.concatenate(
            [wt["wq"][:, s2], wt["wqx"][:, s2], wt["wk"][:, s1], wt["wv"][:, s1], kv[:, s1],
             kv[:, G * D + g * D:G * D + (g + 1) * D]], axis=1)))
    out["w_all"] = np.ascontiguousarray(np.stack(groups))
    names = ["ln_w", "ln_b", "q_in_scale", "qx_in_scale", "k_in_scale", "v_in_scale"]
    out["cols"] = np.ascontiguousarray(np.concatenate([l0(n).reshape(IC, P).T for n in names], axis=1))
    out["dcols"] = np.ascontiguousarray(np.stack([l0(n) for n in DCOLS], axis=1))
    out["scal"] = np.concatenate([z.reshape(-1) for z in (
        l0("wq_scale"), l0("wqx_scale"), l0("wk_scale"), l0("wv_scale"), l0("proj_w_scale"), l0("proj_in_scale"),
        a["g_xattn"], a["g_ffn"], a["L1_ffn_scale"], a["L1_ffn_biasscale"])])
    fe = lambda z: z.reshape(2, G, HPG, D, -1).transpose(1, 0, 2, 3, 4).reshape(2 * G * HPG * D, -1)
    out["smooth"] = np.ascontiguousarray(fe(l0("proj_smooth")).reshape(P, 2 * G * HPG))
    out["wprojT"] = np.ascontiguousarray(fe(l0("wproj").T).reshape(2 * G * HPG, P, H).transpose(1, 0, 2))
    f = lambda n: a["L0_ffn_" + n]
    out["wgT"] = np.ascontiguousarray(chunked(f("Wg").T))
    out["w1T"] = np.ascontiguousarray(chunked(f("W1").reshape(NE * FF, H).T))
    out["w3T"] = np.ascontiguousarray(chunked(f("W3").reshape(NE * FF, H).T))
    out["w2T"] = np.ascontiguousarray(f("W2").transpose(2, 0, 1))
    out["ffn_bias"] = f("bias")
    kv1 = np.concatenate([a["L1_xattn_Wk"], a["L1_xattn_Wv"]], axis=0)
    out["l1_wT"] = np.ascontiguousarray(chunked(np.concatenate([a["L1_xattn_Wq"], kv1[0::2], kv1[1::2]], axis=0).T))
    for n in ("pweight", "nweight"):
        out[n] = np.ascontiguousarray(a["L1_ffn_" + n].transpose(1, 0, 2).reshape(IC, P, H, NBITS).transpose(1, 0, 2, 3))
    for n in ("pbias", "nbias"):
        out[n] = a["L1_ffn_" + n].reshape(-1)
    out["bits"] = np.concatenate([a["L1_ffn_exps"], a["L1_ffn_bexps"], a["L1_ffn_mask_weight"]])
    return out
```

```python
from contextlib import ExitStack

import concourse.bass as bass
from concourse import mybir

F32 = mybir.dt.float32
BF16 = mybir.dt.bfloat16
I16 = mybir.dt.int16
ALU = mybir.AluOpType
ACT = mybir.ActivationFunctionType
AX = mybir.AxisListType

P = 128
B, S, H = 4, 256, 256
SC = 1601
IC = H // P
NT = B * S // P
TB = S // P
D = 128
G = 8
HPG = 2
NQ = TB * HPG
KT = (SC + P - 1) // P
TAIL = SC - (KT - 1) * P
NGB = G * B
WCOLS = 2 * HPG * D + 4 * D
CQ, CQX, CK, CV, CKX = 0, 256, 512, 640, 768
STAGE = 2 * IC * SC + 4 * IC * S
FF, NE = 128, 8
NH1, D1 = 32, 8
NBITS = 4
FP8_MAX = 448.0
EPS5, EPS6 = 1e-5, 1e-6
ROUND_F8 = 1.5 * 2.0 ** 20
ROUND_INT = 1.5 * 2.0 ** 23

COLS = ["ln_w", "ln_b", "s_q", "s_qx", "s_k", "s_v"]
DCOLS = ["qln_w", "qln_b", "qxln_w", "qxln_b", "kln_w", "kln_b", "kxln_w", "kxln_b"]
SCAL = ["wq", "wqx", "wk", "wv", "pw", "pin", "gx0", "gx1", "gf0", "gf1", "scale", "bscale"]


class Token:

    def __init__(self, sem, n, region, back=0):
        self.sem, self.n, self.region, self.back = sem, n, region, back


class Carry:

    def __init__(self, region, name):
        self.region, self.name = region, name


class Program:

    ENGINES = ("pe", "act", "dve", "pool", "sp")

    def __init__(self, nc, ctx):
        self.nc, self.ctx = nc, ctx
        self.queue = {e: [] for e in self.ENGINES}
        self.sems, self.regions = {}, []
        self.left = {}
        for e in self.ENGINES[:4]:
            self.sems[e] = ctx.enter_context(nc.semaphore("done_" + e))
        self.straight()

    def stream(self, name):
        self.sems[name] = self.ctx.enter_context(self.nc.semaphore("dma_" + name))
        return name

    def straight(self):
        self._region(1)

    def loop(self, trips):
        self._region(trips)

    def _region(self, trips):
        self.regions.append({"trips": trips, "count": {}, "left": {}, "back": False})
        self.left = {}
        for e in self.ENGINES:
            self.queue[e].append(("region", len(self.regions) - 1))

    def carry(self, *names):
        r = len(self.regions) - 1
        for name in names:
            self.left[name] = [Carry(r, name)]
        self.regions[r]["left"] = self.left

    def leave(self, name, *tokens):
        self.left[name] = list(tokens)

    def of(self, *names):
        return [t for name in names for t in self.left.get(name, [])]

    def step(self, engine, fn, after=(), sem=None, signal=True, lone=False):
        sem = sem or engine
        inc = 1 if sem in self.ENGINES else 16
        tok = None
        if signal:
            r = self.regions[-1]
            r["count"][sem] = r["count"].get(sem, 0) + inc
            tok = Token(sem, r["count"][sem], len(self.regions) - 1)
        self.queue[engine].append(("step", fn, [t for t in after if t is not None], (sem, inc) if signal else None, lone))
        return tok

    def pe(self, fn, after=(), signal=False):
        return self.step("pe", fn, after, signal=signal)

    def act(self, fn, after=()):
        return self.step("act", fn, after)

    def dve(self, fn, after=(), lone=False):
        return self.step("dve", fn, after, lone=lone)

    def pool(self, fn, after=(), lone=False):
        return self.step("pool", fn, after, lone=lone)

    def dma(self, stream, fn, after=()):
        return self.step("sp", fn, after, sem=stream)

    def _resolve(self, tok, out, back=0):
        if isinstance(tok, Carry):
            r = self.regions[tok.region]
            for t in r["left"][tok.name]:
                if isinstance(t, Carry) and t.name == tok.name:
                    raise ValueError("nothing is left under " + tok.name)
                self._resolve(t, out, back + 1)
        else:
            out.append(Token(tok.sem, tok.n, tok.region, tok.back + back))

    def emit(self):
        base = {s: 0 for s in self.sems}
        for r in self.regions:
            primed = r["trips"] > 1
            r["base"] = dict(base)
            r["prime"] = {s: (r["count"].get(s, 0) if primed else 0) for s in self.sems}
            for s in base:
                base[s] += r["prime"][s] + r["trips"] * r["count"].get(s, 0)
        self.total = base
        block = self.ctx.enter_context(self.nc.Block())
        for name, dec in (("sp", block.sync), ("pool", block.gpsimd), ("dve", block.vector),
                          ("act", block.scalar), ("pe", block.tensor)):
            dec(self._emitter(name))

    def _emitter(self, name):
        def run(e):
            items = self.queue[name]
            parts, cur = [], None
            for it in items:
                if it[0] == "region":
                    cur = (it[1], [])
                    parts.append(cur)
                else:
                    cur[1].append(it)
            for ri, steps in parts:
                r = self.regions[ri]
                if ri:
                    for s, v in r["base"].items():
                        if v:
                            e.wait_ge(self.sems[s], v)
                if r["trips"] > 1:
                    for s, v in r["prime"].items():
                        owner = s if s in self.ENGINES else "sp"
                        if owner == name and v:
                            e.sem_inc(self.sems[s], v)
                    if steps:
                        with e.Fori(0, r["trips"], 1) as i:
                            self._steps(e, ri, steps, i)
                else:
                    self._steps(e, ri, steps, 0)
            for s, v in self.total.items():
                if s not in self.ENGINES and name == "sp" and v:
                    e.wait_ge(self.sems[s], v)
        return run

    def _steps(self, e, ri, steps, i):
        r = self.regions[ri]
        seen = {}
        for _, fn, after, sig, lone in steps:
            need = {}
            for tok in after:
                got = []
                self._resolve(tok, got)
                for t in got:
                    if t.region == ri:
                        v = t.n - t.back * r["count"].get(t.sem, 0)
                        need[t.sem] = max(need.get(t.sem, -10 ** 9), v)
            waited = False
            for s, v in need.items():
                if v <= seen.get(s, -10 ** 9):
                    continue
                seen[s] = v
                first = r["base"][s] + r["prime"][s] + v
                per = r["count"].get(s, 0)
                e.wait_ge(self.sems[s], i * per + first if r["trips"] > 1 else first)
                waited = True
            if lone and waited and r["trips"] > 1:
                e.nop(nofuse=True)
            self.i = i
            ins = fn(e)
            if sig:
                ins.then_inc(self.sems[sig[0]], sig[1])


def tensors(nc, ctx):
    def sb(name, shape, dt):
        return ctx.enter_context(nc.sbuf_tensor(name, shape, dt))

    def ps(name, shape, dt):
        return ctx.enter_context(nc.psum_tensor(name, shape, dt))

    return sb, ps


def round_fp8(pr, y, e, m, t, after, on_pool):
    add = pr.pool if on_pool else pr.dve
    a = pr.dve(lambda v: v.tensor_scalar(e.bitcast(I16), y.bitcast(I16), 0x7F80, None, ALU.bitwise_and), after)
    b = add(lambda v: v.tensor_scalar(m, e, 2.0 ** -6, ROUND_F8, ALU.max, ALU.mult), [a], lone=True)
    c = add(lambda v: v.tensor_tensor(t, y, m, ALU.add), [b])
    return add(lambda v: v.tensor_tensor(y, t, m, ALU.subtract), [c])


def layernorm_rows(pr, x, out, st, mv, rs, mhalf, eps, tiles, after):
    for t in range(tiles):
        a = pr.dve(lambda v, t=t: v.bn_stats(st[:, t, :], x[:, t, :]), after)
    for t in range(tiles):
        a = pr.dve(lambda v, t=t: v.bn_aggr(mv[:, t, :], st[:, t, :]), [a])
    b = pr.pool(lambda v: v.tensor_scalar(rs[:, 0:tiles], mv[:, 0:tiles, 1], eps, None, ALU.add), [a])
    b = pr.pool(lambda v: v.tensor_tensor(rs[:, 0:tiles], rs[:, 0:tiles], mhalf[:, 0:tiles], ALU.pow), [b])
    for t in range(tiles):
        c = pr.dve(lambda v, t=t: v.tensor_scalar(out[:, t, :], x[:, t, :], mv[:, t, 0:1], rs[:, t:t + 1],
                                                  ALU.subtract, ALU.mult), [b])
    return c


def build(nc, A, out):
    whole = ExitStack()
    with whole:
        pr = Program(nc, whole)
        for s in ("x", "in", "ctx0", "ctx1", "ctxs0", "ctxs1", "w0", "w1", "ws0", "ws1", "xq0", "xq1", "ld0", "ld1", "wp0",
                  "wp1", "out", "row", "rsm0", "rsm1"):
            pr.stream(s)
        sb, ps = tensors(nc, whole)
        w_split = nc.dram_tensor("w_split", (G, P, 2 * IC * WCOLS), BF16, kind="Internal").ap()
        stage_d = nc.dram_tensor("stage_d", (B, P, STAGE), BF16, kind="Internal").ap()
        rsm_d = nc.dram_tensor("rsm_d", (P, 2 * G * HPG), F32, kind="Internal").ap()

        x = sb("x", [P, NT, H], F32)
        ident = sb("ident", [P, P], F32)
        identb = sb("identb", [P, P], BF16)
        mhalf = sb("mhalf", [P, 64], F32)
        cols = sb("cols", [P, len(COLS) * IC], F32)
        dcols = sb("dcols", [P, len(DCOLS)], F32)
        scal = sb("scal", [P, len(SCAL)], F32)
        gate = sb("gate", [P, 4], F32)
        st = sb("st", [P, NT, 6], F32)
        mv = sb("mv", [P, NT, 2], F32)
        rs = sb("rs", [P, NT], F32)
        l1_ffn_w = sb("l1_ffn_w", [P, 2, IC, H], BF16)
        l1_ffn_b = sb("l1_ffn_b", [P, H], F32)
        col = lambda n, ic: cols[:, COLS.index(n) * IC + ic:COLS.index(n) * IC + ic + 1]
        dcol = lambda n: dcols[:, DCOLS.index(n):DCOLS.index(n) + 1]
        sc = lambda n: scal[:, SCAL.index(n):SCAL.index(n) + 1]

        score = ps("score", [P, 4 * 512], F32)
        tb = [ps("tb0", [P, 512], F32), ps("tb1", [P, 512], F32)]
        pv = ps("pv", [P, 512], F32)
        pa = ps("pa", [P, 512], F32)

        k = dict(nc=nc, pr=pr, A=A, out=out, x=x, ident=ident, identb=identb, mhalf=mhalf, col=col, dcol=dcol, sc=sc,
                 gate=gate, st=st, mv=mv, rs=rs, score=score, tb=tb, pv=pv, pa=pa, cols=cols, dcols=dcols,
                 scal=scal, w_split=w_split, stage_d=stage_d, rsm_d=rsm_d, l1_ffn_w=l1_ffn_w, l1_ffn_b=l1_ffn_b)
        attn = ExitStack()
        with attn:
            catq = tensors(nc, attn)[0]("catq", [P, (NGB + 1) * 2 * NQ * P], BF16)
            k.update(catq=catq)
            with ExitStack() as c0:
                prologue(k, tensors(nc, c0)[0])
            with ExitStack() as c1:
                layer0_attention(k, tensors(nc, c1)[0])
            with ExitStack() as c2:
                layer0_projection(k, tensors(nc, c2)[0])
                layer0_ffn(k, tensors(nc, c2)[0])
        for stage in (layer1_attention, layer1_ffn):
            with ExitStack() as c:
                stage(k, tensors(nc, c)[0])
        pr.emit()


def prologue(k, sb):
    pr, A, x = k["pr"], k["A"], k["x"]
    ident, identb, mhalf = k["ident"], k["identb"], k["mhalf"]
    col, sc, score, tb = k["col"], k["sc"], k["score"], k["tb"]
    st, mv, rs = k["st"], k["mv"], k["rs"]
    ld_x = pr.dma("x", lambda e: e.dma_start(x[:, :, :], A["x"].rearrange("(t p) d -> p t d", p=P)))
    pr.dma("in", lambda e: e.dma_start(k["cols"][:, :], A["cols"]))
    pr.dma("in", lambda e: e.dma_start(k["dcols"][:, :], A["dcols"]))
    pr.dma("in", lambda e: e.dma_start(k["scal"][:, :], A["scal"].partition_broadcast(P)))
    smc = sb("smc", [P, 2 * G * HPG], F32)
    rsmc = sb("rsmc", [P, 2 * G * HPG], F32)
    ld = pr.dma("in", lambda e: e.dma_start(smc[:, :], A["smooth"]))

    z = pr.pool(lambda e: e.memset(ident[:, :], 0.0))
    i = pr.pool(lambda e: e.affine_select(out=ident[:, :], in_=ident[:, :], compare_op=ALU.not_equal, fill=1.0,
                                          base=0, pattern=[[-1, P]], channel_multiplier=1), [z])
    pr.pool(lambda e: e.memset(mhalf[:, :], -0.5))
    ib = pr.dve(lambda e: e.tensor_copy(identb[:, :], ident[:, :]), [i])

    r = pr.dve(lambda e: e.reciprocal(rsmc[:, :], smc[:, :]), [ld])
    pr.dma("row", lambda e: e.dma_start(k["rsm_d"], rsmc[:, :]), [r])

    gate = k["gate"]
    g = pr.act(lambda e: e.activation(gate[:, :], k["scal"][:, SCAL.index("gx0"):SCAL.index("gx0") + 4], ACT.Tanh), [ld])
    g = pr.dve(lambda e: e.tensor_scalar(gate[:, 0:1], gate[:, 0:1], sc("pw"), sc("pin"), ALU.mult, ALU.mult), [g])
    for n in (0, 1, 2, 3):
        pr.dve(lambda e, n=n: e.tensor_scalar(k["dcols"][:, n:n + 1], k["dcols"][:, n:n + 1], float(D) ** -0.5, None,
                                              ALU.mult), [ld])

    rin = sb("rin", [P, 4 * IC], F32)
    win = sb("win", [P, 4 * IC], F32)
    kinds = (("q", "wq", CQ, 256), ("qx", "wqx", CQX, 256), ("k", "wk", CK, 128), ("v", "wv", CV, 128))
    for n, (kind, ws, _, _) in enumerate(kinds):
        wr = pr.dve(lambda e, n=n, kind=kind, ws=ws: e.tensor_scalar(
            win[:, n * IC:(n + 1) * IC], k["cols"][:, COLS.index("s_" + kind) * IC:(COLS.index("s_" + kind) + 1) * IC],
            sc(ws), None, ALU.mult), [ld])
    rr = pr.dve(lambda e: e.reciprocal(rin[:, :], k["cols"][:, 2 * IC:6 * IC]), [ld])
    def x_norms():
        a = layernorm_rows(pr, x, xn, st, mv, rs, mhalf, EPS5, NT, [ld_x])
        a = layernorm_rows(pr, xn, xn, st, mv, rs, mhalf, EPS5, NT, [a])
        for ic in range(IC):
            for q in range(2):
                bank = score[:, (2 * ic + q) * 512:(2 * ic + q + 1) * 512]
                for t in range(4):
                    tt = pr.pe(lambda e, bank=bank, t=t, q=q, ic=ic: e.transpose(
                        bank[:, t * P:(t + 1) * P], xn[:, 4 * q + t, ic * P:(ic + 1) * P], ident[:, :]), [a, i, ib],
                        signal=(t == 3))
                w = pr.dve(lambda e, bank=bank, q=q, ic=ic: e.tensor_scalar(
                    xw[:, ic, q * 512:(q + 1) * 512], bank, col("ln_w", ic), col("ln_b", ic), ALU.mult, ALU.add), [tt])
        return w

    def quantised_input(n, w):
        p = n % 2
        for ic in range(IC):
            y = pr.act(lambda e, ic=ic: e.activation(xq[p][:, ic, :], xw[:, ic, :], ACT.Copy,
                                                     scale=rin[:, n * IC + ic:n * IC + ic + 1]), [w, rr] + free_q[p])
        y = pr.dve(lambda e: e.tensor_scalar(xq[p][:, :, :], xq[p][:, :, :], FP8_MAX, -FP8_MAX, ALU.min, ALU.max), [y])
        y = round_fp8(pr, xq[p][:, :, :], ex[:, :, :], m[:, :, :], y32[:, :, :], [y], False)

        def store(b):
            return pr.dma(f"xq{p}", lambda e: e.dma_start(
                k["stage_d"][b, :, 2 * IC * SC + n * IC * S:2 * IC * SC + (n + 1) * IC * S].rearrange(
                    "p (i s) -> p i s", i=IC), xq[p][:, :, b * S:(b + 1) * S]), [y])
        for b in range(B):
            s = store(b)
        free_q[p] = [s]

    def weight_load(g):
        p = g % 2
        return pr.dma(f"w{p}", lambda e: e.dma_start(wf[p][:, :, :], A["w_all"][g]), free_f[p])

    def weight_parts(g, l):
        p = g % 2
        his, los = [], []
        for ic in range(IC):
            for n, (_, _, c0, nc_) in enumerate(kinds + ((None, None, CKX, 256),)):
                src = lambda ic=ic, c0=c0, nc_=nc_: wf[p][:, ic, c0:c0 + nc_]
                dst = lambda part, ic=ic, c0=c0, nc_=nc_: wo[p][:, part, ic, c0:c0 + nc_]
                if n < 4:
                    s = lambda n=n, ic=ic: win[:, n * IC + ic:n * IC + ic + 1]
                    h = pr.act(lambda e, s=s, src=src, dst=dst: e.activation(dst(0), src(), ACT.Copy, scale=s()),
                               [l, wr] + free_o[p])
                    lo = pr.dve(lambda e, s=s, src=src, dst=dst: e.scalar_tensor_tensor(
                        dst(1), src(), s(), dst(0), ALU.mult, ALU.subtract), [h])
                else:
                    h = pr.act(lambda e, src=src, dst=dst: e.copy(dst(0), src()), [l] + free_o[p])
                    lo = pr.pool(lambda e, src=src, dst=dst: e.tensor_tensor(dst(1), src(), dst(0), ALU.subtract), [h])
                his.append(h)
                los.append(lo)
        free_f[p] = [his[-1]] + los
        return los + [his[-1]]

    def weight_store(g, done):
        p = g % 2
        free_o[p] = [pr.dma(f"ws{p}", lambda e: e.dma_start(
            k["w_split"][g], wo[p][:, :, :, :].rearrange("p a b c -> p (a b c)")), done)]

    def context_load(c):
        p, b, ic = c % 2, c // IC, c % IC
        return pr.dma(f"ctx{p}", lambda e: e.dma_start(cf[p][:, :], A["ctxT"][:, ic, b, :]), free_cf[p])

    def context_parts(l, c):
        p = c % 2
        half = 1024
        h = pr.act(lambda e: e.copy(co[p][:, 0, :], cf[p][:, :]), [l] + free_co[p])
        l1 = pr.dve(lambda e: e.tensor_tensor(co[p][:, 1, 0:half], cf[p][:, 0:half], co[p][:, 0, 0:half],
                                              ALU.subtract), [h])
        l2 = pr.pool(lambda e: e.tensor_tensor(co[p][:, 1, half:], cf[p][:, half:], co[p][:, 0, half:],
                                               ALU.subtract), [h])
        free_cf[p] = [l1, l2]
        return [h, l1, l2]

    def context_store(c, done):
        p, b, ic = c % 2, c // IC, c % IC
        free_co[p] = [pr.dma(f"ctxs{p}", lambda e: e.dma_start(
            k["stage_d"][b, :, 0:2 * IC * SC].rearrange("p (a i s) -> p a i s", a=2, i=IC)[:, :, ic, :],
            co[p][:, :, :]), done)]

    wf = [sb(f"wf{i}", [P, IC, WCOLS], F32) for i in range(2)]
    wo = [sb(f"wo{i}", [P, 2, IC, WCOLS], BF16) for i in range(2)]
    cf = [sb(f"cf{i}", [P, SC], F32) for i in range(2)]
    co = [sb(f"co{i}", [P, 2, SC], BF16) for i in range(2)]
    xn = sb("xn", [P, NT, H], F32)
    xw = sb("xw", [P, IC, NT * P], F32)
    y32 = sb("y32", [P, IC, NT * P], F32)
    xq = [sb(f"xq{i}", [P, IC, NT * P], BF16) for i in range(2)]
    ex = sb("ex", [P, IC, NT * P], BF16)
    m = sb("m", [P, IC, NT * P], F32)
    free_f, free_o, free_cf, free_co, free_q = ([[], []] for _ in range(5))
    wl = {g: weight_load(g) for g in range(2)}
    cl = {c: context_load(c) for c in range(2)}
    xw_done = x_norms()
    for g in range(G):
        wd = weight_parts(g, wl[g])
        if g + 2 < G:
            wl[g + 2] = weight_load(g + 2)
        weight_store(g, wd)
        c = g
        cd = context_parts(cl[c], c)
        if c + 2 < B * IC:
            cl[c + 2] = context_load(c + 2)
        context_store(c, cd)
        if g % 2 == 1:
            quantised_input(g // 2, xw_done)
    for t in tb:
        pr.dve(lambda e, t=t: e.memset(t[:, :], 0.0))


def layer0_attention(k, sb):
    pr, A = k["pr"], k["A"]
    ident, identb, mhalf, dcol = k["ident"], k["identb"], k["mhalf"], k["dcol"]
    score, tb, pv, pa, catq = k["score"], k["tb"], k["pv"], k["pa"], k["catq"]
    rsm = [sb(f"rsm{i}", [P, 2 * HPG * D], F32) for i in range(2)]
    stage = [sb(f"stage{i}", [P, STAGE], BF16) for i in range(2)]
    wsb = [sb(f"wsb{i}", [P, 2, IC, WCOLS], BF16) for i in range(2)]
    QT = [sb(f"QT{i}", [P, 2, 2, NQ * P], BF16) for i in range(2)]
    KS = [sb(f"KS{i}", [P, 2, S], BF16) for i in range(2)]
    VS = [sb(f"VS{i}", [P, 2, TB, D], BF16) for i in range(2)]
    KX = [sb(f"KX{i}", [P, 2, SC], BF16) for i in range(2)]
    VX = [sb(f"VX{i}", [P, 2, KT, D], BF16) for i in range(2)]
    NP_ = SC + S
    P32 = [sb(f"P32_{i}", [P, NP_], F32) for i in range(2)]
    PT = [sb(f"PT{i}", [P, 2, 512], BF16) for i in range(2)]
    kn = [sb(f"kn{i}", [P, 512], F32) for i in range(3)]
    t32 = [sb(f"t32_{i}", [P, 512], F32) for i in range(2)]
    st, mv, rs, nm = ([sb(f"a_{n}{i}", [P, *w], F32) for i in range(3)]
                      for n, w in (("st", (4, 6)), ("mv", (4, 2)), ("rs", (4,)), ("nm", (4,))))
    mxp = [sb(f"mxp{i}", [P, 2], F32) for i in range(2)]
    nmx = [sb(f"nmx{i}", [P, 2], F32) for i in range(2)]
    sums = [sb(f"sums{i}", [P, 2], F32) for i in range(2)]
    rsum = [sb(f"rsum{i}", [P, 2], F32) for i in range(2)]
    yq = sb("yq", [P, 2, NQ, P], BF16)
    ye = sb("ye", [P, 2, P], BF16)
    ym, yt = sb("ym", [P, 2, P], F32), sb("yt", [P, 2, P], F32)

    def ctx_op(p, part, ic, a, b):
        o = (part * IC + ic) * SC
        return stage[p][:, o + a:o + b]

    def xq_op(p, kind, ic, a, b):
        o = 2 * IC * SC + (kind * IC + ic) * S
        return stage[p][:, o + a:o + b]

    turn = {"tb": 0, "kn": 0, "t32": 0}

    def next_of(name, n=2):
        i = turn[name]
        turn[name] = (i + 1) % n
        return i

    def load(p, n):
        after = pr.of(f"A_done{p}")
        grp = (lambda: n(pr.i) // B % G)
        bat = (lambda: n(pr.i) % B)
        a = pr.dma(f"ld{p}", lambda e: e.dma_start(
            stage[p][:, :].rearrange("p (o c) -> p o c", o=1),
            k["stage_d"][bass.ds(bat(), 1), :, :].rearrange("o p c -> p o c")), after)
        b = pr.dma(f"ld{p}", lambda e: e.dma_start(
            wsb[p][:, :, :, :].rearrange("p a b c -> p (a b c)").rearrange("p (o c) -> p o c", o=1),
            k["w_split"][bass.ds(grp(), 1), :, :].rearrange("o p c -> p o c")), after)
        pr.leave(f"loaded{p}", a, b)

    def load_rsm(p, n):
        a = pr.dma(f"rsm{p}", lambda e: e.dma_start(
            rsm[p][:, :], k["rsm_d"].rearrange("(g c) f -> g (c f)", g=G)[
                bass.ds(n(pr.i) // B % G, 1), :].partition_broadcast(P)), pr.of(f"finished{p}"))
        pr.leave(f"rsm{p}", a)

    def normalise_start(b, blocks, stride, rows, ready, eps):
        s = ready
        for j in range(blocks):
            s = pr.dve(lambda e, j=j: e.bn_stats(st[b][0:rows, j, :], kn[b][0:rows, j * stride:j * stride + D]), [s])
        for j in range(blocks):
            s = pr.dve(lambda e, j=j: e.bn_aggr(mv[b][0:rows, j, :], st[b][0:rows, j, :]), [s], lone=True)
        v = lambda a: a[b][0:rows, 0:blocks]
        r = pr.pool(lambda e: e.tensor_scalar(v(rs), mv[b][0:rows, 0:blocks, 1], eps, None, ALU.add), [s], lone=True)
        r = pr.pool(lambda e: e.tensor_tensor(v(rs), v(rs), mhalf[0:rows, 0:blocks], ALU.pow), [r])
        r = pr.pool(lambda e: e.tensor_tensor(v(nm), mv[b][0:rows, 0:blocks, 0], v(rs), ALU.mult), [r])
        return pr.pool(lambda e: e.tensor_scalar(v(nm), v(nm), -1.0, None, ALU.mult), [r], lone=True)

    def normalise_end(b, blocks, stride, rows, ready):
        for j in range(blocks):
            n = pr.act(lambda e, j=j: e.activation(
                kn[b][0:rows, j * stride:j * stride + D], kn[b][0:rows, j * stride:j * stride + D], ACT.Identity,
                bias=nm[b][0:rows, j:j + 1], scale=rs[b][0:rows, j:j + 1]), [ready])
        return n

    def to_parts(b, blocks, stride, rows, ready, w, bias, hi, lo, dst_free, beside_exps):
        t = next_of("tb")
        width = (blocks - 1) * P + rows
        for j in range(blocks):
            tt = pr.pe(lambda e, j=j: e.transpose(tb[t][:, j * P:j * P + rows], kn[b][0:rows, j * stride:j * stride + D],
                                                  ident[0:rows, 0:rows]),
                       [ready] + pr.of(f"tb{t}"), signal=(j == blocks - 1))
        pr.leave(f"kn{b}", tt, *pr.of(f"kv{b}"))
        c = next_of("t32")
        bank, t32_free = tb[t][:, 0:width], pr.of(f"t32{c}")
        if not beside_exps:
            pr.act(lambda e: e.activation(t32[c][:, 0:width], bank, ACT.Identity, scale=dcol(w), bias=dcol(bias)),
                   [tt] + t32_free)
        a = pr.act(lambda e: e.activation(hi(), bank, ACT.Identity, scale=dcol(w), bias=dcol(bias)), [tt] + dst_free)
        if beside_exps:
            a = pr.dve(lambda e: e.tensor_scalar(t32[c][:, 0:width], bank, dcol(w), dcol(bias), ALU.mult, ALU.add),
                       [a] + t32_free)
        pr.leave(f"tb{t}", a)
        l = pr.pool(lambda e: e.tensor_tensor(lo(), t32[c][:, 0:width], hi(), ALU.subtract), [a])
        pr.leave(f"t32{c}", l)
        return l

    def stage_a(p):
        def product(dst, kind, tt, c0, width):
            for n, (ic, part) in enumerate((i, j) for i in range(IC) for j in range(2)):
                r = pr.pe(lambda e, ic=ic, part=part, n=n: e.matmul(
                    dst, xq_op(p, kind, ic, tt * P, (tt + 1) * P), wsb[p][:, part, ic, c0:c0 + width],
                    start=(n == 0), stop=(n == 3)), pr.of("pa", f"loaded{p}"), signal=(n == 3))
            return r

        def keep(blocks, rows, r):
            b = next_of("kn", 3)
            src, dst, after = pa[0:rows, 0:blocks * D], kn[b][0:rows, 0:blocks * D], [r] + pr.of(f"kn{b}")
            if beside_exps:
                c = pr.dve(lambda e: e.tensor_copy(dst, src), after)
            else:
                c = pr.act(lambda e: e.copy(dst, src), after)
            pr.leave("pa", c)
            pr.leave(f"kv{b}")
            return b, c

        def values(b, src, dst, c):
            vh = pr.dve(lambda e: e.tensor_copy(dst(0), src), [c] + pr.of(f"V_read{p}"))
            vl = pr.pool(lambda e: e.tensor_tensor(dst(1), src, dst(0), ALU.subtract), [vh])
            pr.leave(f"kv{b}", vl)
            vals.append(vl)

        def queries(kind):
            w, c0 = (("qln", CQ), ("qxln", CQX))[kind]
            for tt in range(TB):
                r = product(pa[:, tt * 256:(tt + 1) * 256], kind, tt, c0, 256)
            b, c = keep(4, P, r)
            return (b, 4, D, P, c, w, lambda part: QT[p][:, kind, part, :])

        def self_kv():
            for tt in range(TB):
                product(pa[:, tt * P:(tt + 1) * P], 2, tt, CK, D)
                r = product(pa[:, 256 + tt * P:256 + (tt + 1) * P], 3, tt, CV, D)
            b, c = keep(4, P, r)
            values(b, kn[b][:, 256:512].rearrange("p (s d) -> p s d", s=2), lambda part: VS[p][:, part, :, :], c)
            return (b, 2, D, P, c, "kln", lambda part: KS[p][:, part, :])

        def context_kv(c0):
            k2 = min(2, KT - c0)
            rows = P if c0 + 1 < KT else TAIL
            for s in range(k2):
                t = c0 + s
                for n, (ic, a, w) in enumerate((ic, a, w) for ic in range(IC) for a, w in THREE):
                    r = pr.pe(lambda e, s=s, t=t, n=n, ic=ic, a=a, w=w: e.matmul(
                        pa[0:rows, s * 256:(s + 1) * 256], ctx_op(p, a, ic, t * P, t * P + rows),
                        wsb[p][:, w, ic, CKX:CKX + 256], start=(n == 0), stop=(n == 5)),
                        pr.of("pa", f"loaded{p}"), signal=(s == k2 - 1 and n == 5))
            b, c = keep(2 * k2, rows, r)
            values(b, kn[b][0:rows, 0:k2 * 256].rearrange("p (s c) -> p s c", s=k2)[:, :, D:2 * D],
                   lambda part: VX[p][0:rows, part, c0:c0 + k2, :], c)
            if c0 + k2 >= KT:
                pr.leave(f"A_done{p}", r)
            at, width = c0 * P, (k2 - 1) * P + rows
            return (b, k2, 2 * D, rows, c, "kxln", lambda part: KX[p][:, part, at:at + width])

        vals = []
        chunks = [lambda: queries(0), lambda: queries(1), self_kv] + [
            lambda c0=c0: context_kv(c0) for c0 in range(0, KT, 2)]
        needs = {len(chunks) - 1 - i: bank for bank, i in ((0, 5), (1, 3), (2, 1), (3, 0))}
        info, normed, parts = {}, {}, []
        for j in range(len(chunks) + 2):
            beside_exps = j % 3 == 1
            if j >= 2:
                b, blocks, stride, rows, r, _, _ = info[j - 2]
                normed[j - 2] = normalise_end(b, blocks, stride, rows, r)
            yield
            if j < len(chunks):
                b, blocks, stride, rows, r, w, dst = chunks[j]()
                info[j] = (b, blocks, stride, rows, normalise_start(b, blocks, stride, rows, r, EPS5), w, dst)
            if j >= 2:
                b, blocks, stride, rows, _, w, dst = info[j - 2]
                parts.append(to_parts(b, blocks, stride, rows, normed[j - 2], w + "_w", w + "_b", lambda dst=dst: dst(0),
                                      lambda dst=dst: dst(1), pr.of(f"QK_read{p}"), beside_exps))
                if j - 2 in needs:
                    pr.leave(f"ready{p}_{needs[j - 2]}", *parts)
            if j == len(chunks) + 1:
                pr.leave(f"values{p}", *vals)
            yield

    SELF0 = 3 * 512 + P
    BANKS = [[(1, 0, 512, 0)], [(1, 512, 1024, 512)], [(1, 1024, 1536, 1024)],
             [(1, 1536, SC, 1536), (0, 0, S, SELF0)]]
    SPLITX = 1024

    def scores(p, q, bank):
        free = "expS" if bank == 3 else "expX"
        for kind, a, b, at in BANKS[bank]:
            keys = KX[p] if kind else KS[p]
            for n, (qp, kp) in enumerate(((0, 0), (0, 1), (1, 0))):
                last = (kind, n) == (BANKS[bank][-1][0], 2)
                t = pr.pe(lambda e, kind=kind, a=a, b=b, at=at, keys=keys, n=n, qp=qp, kp=kp: e.matmul(
                    score[:, at:at + b - a], QT[p][:, kind, qp, q * P:(q + 1) * P], keys[:, kp, a:b],
                    start=(n == 0), stop=(n == 2)), pr.of(free, f"ready{p}_{bank}"), signal=last)
        pr.leave(f"bank{bank}", t)
        if bank == 3:
            pr.leave(f"QK_read{p}", t)

    def max_a(par):
        t = pr.dve(lambda e: e.tensor_reduce(mxp[par][:, 0:1], score[:, 0:SPLITX], AX.X, ALU.max),
                   pr.of("bank0", "bank1"))

    def max_b(par):
        pr.dve(lambda e: e.tensor_reduce(nmx[par][:, 1:2], score[:, SELF0:SELF0 + S], AX.X, ALU.max, negate=True),
               pr.of("bank3", f"exp{par}"))
        t = pr.dve(lambda e: e.tensor_reduce(mxp[par][:, 1:2], score[:, SPLITX:SC], AX.X, ALU.max), pr.of("bank2"))
        t = pr.dve(lambda e: e.tensor_reduce(nmx[par][:, 0:1], mxp[par][:, :], AX.X, ALU.max, negate=True), [t])
        pr.leave("negmax", t)

    def exps(par):
        w = pr.of("negmax", f"P_read{par}", f"sum_read{par}")
        a = pr.act(lambda e: e.activation(P32[par][:, 0:SC], score[:, 0:SC], ACT.Exp,
                                          bias=nmx[par][:, 0:1], accum_out=sums[par][:, 1:2]), w)
        c = pr.act(lambda e: e.activation(P32[par][:, SC:SC + S], score[:, SELF0:SELF0 + S], ACT.Exp,
                                          bias=nmx[par][:, 1:2], accum_out=sums[par][:, 0:1]), w)
        pr.leave("expX", a)
        pr.leave("expS", c)
        pr.leave(f"exp{par}", a, c)

    CHUNKS = [(1, t, t * P, P if t < KT - 1 else TAIL) for t in range(KT)] + [(0, t, SC + t * P, P) for t in range(TB)]
    GROUPS = [CHUNKS[0:4], CHUNKS[4:8], CHUNKS[8:12], CHUNKS[12:15]]
    group = {}

    def turn_p(par, g):
        t = next_of("tb")
        chunks = GROUPS[g]
        for j, (_, _, at, keys) in enumerate(chunks):
            tt = pr.pe(lambda e, j=j, at=at, keys=keys: e.transpose(
                tb[t][0:keys, j * P:(j + 1) * P], P32[par][:, at:at + keys], ident[:, :]),
                pr.of(f"exp{par}", f"tb{t}"), signal=(j == len(chunks) - 1))
        if g == len(GROUPS) - 1:
            pr.leave(f"P_read{par}", tt)
        pt, w = g % 2, len(chunks) * P
        h = pr.act(lambda e: e.copy(PT[pt][:, 0, 0:w], tb[t][:, 0:w]), [tt] + pr.of(f"PT{pt}"))
        l = pr.dve(lambda e: e.tensor_tensor(PT[pt][:, 1, 0:w], tb[t][:, 0:w], PT[pt][:, 0, 0:w], ALU.subtract), [h])
        pr.leave(f"tb{t}", l)
        group[g] = l

    def times_v(vp, g):
        pt = g % 2
        for j, (kind, t, _, keys) in enumerate(GROUPS[g]):
            V = VX[vp] if kind else VS[vp]
            at = P if kind else 0
            lastt = KT - 1 if kind else TB - 1
            for n, (a, v) in enumerate(((0, 0), (0, 1), (1, 0))):
                m = pr.pe(lambda e, j=j, t=t, keys=keys, V=V, at=at, n=n, a=a, v=v, lastt=lastt: e.matmul(
                    pv[:, at:at + D], PT[pt][0:keys, a, j * P:(j + 1) * P], V[0:keys, v, t, :],
                    start=(t == 0 and n == 0), stop=(t == lastt and n == 2)),
                    [group[g]] + pr.of("pv", f"values{vp}"), signal=(j == len(GROUPS[g]) - 1 and n == 2))
        pr.leave(f"PT{pt}", m)
        if g == len(GROUPS) - 1:
            pr.leave("pv_full", m)
            pr.leave(f"V_read{vp}", m)

    def finish(vp, par, q):
        h = q % HPG
        a = pr.dve(lambda e: e.reciprocal(rsum[par][:, :], sums[par][:, :]), pr.of(f"exp{par}"))
        pr.leave(f"sum_read{par}", a)
        y = yq[:, :, q, :]
        for x_ in range(2):
            a = pr.dve(lambda e, x_=x_: e.scalar_tensor_tensor(
                yq[:, x_, q, :], pv[:, x_ * P:(x_ + 1) * P], rsum[par][:, x_:x_ + 1],
                rsm[vp][:, (x_ * HPG + h) * D:(x_ * HPG + h + 1) * D], ALU.mult, ALU.mult),
                [a] + pr.of("pv_full", f"rsm{vp}", "yq_read"))
        pr.leave("pv", a)
        if q == NQ - 1:
            pr.leave(f"finished{vp}", a)
        c = pr.dve(lambda e: e.tensor_scalar(y, y, FP8_MAX, -FP8_MAX, ALU.min, ALU.max), [a])
        pr.leave("clipped", c)

    def quantise(q):
        pr.leave("yq", round_fp8(pr, yq[:, :, q, :], ye[:, :, :], ym[:, :, :], yt[:, :, :], pr.of("clipped", "yq"), True))

    def turn_y(slot):
        t = next_of("tb")
        bank = tb[t][:, :].bitcast(BF16)
        for j in range(2 * NQ):
            m = pr.pe(lambda e, j=j: e.transpose(bank[:, j * P:(j + 1) * P], yq[:, j // NQ, j % NQ, :], identb[:, :]),
                      pr.of("yq", f"tb{t}"), signal=(j == 2 * NQ - 1))
        pr.leave("yq_read", m)
        c = pr.dve(lambda e: e.tensor_copy(catq[:, bass.ds(slot(pr.i) * (2 * NQ * P), 2 * NQ * P)], bank), [m])
        pr.leave(f"tb{t}", c)

    def block(kk, gen, slot, nxt):
        p, q, par = kk // NQ % 2, kk % NQ, kk % 2
        lk = (kk - 1) % (2 * NQ)
        lp, lq, lpar = lk // NQ, lk % NQ, lk % 2
        turn_p(lpar, 0)
        scores(p, q, 0)
        turn_p(lpar, 1)
        scores(p, q, 1)
        next(gen, None)
        max_a(par)
        next(gen, None)
        times_v(lp, 0)
        scores(p, q, 2)
        scores(p, q, 3)
        next(gen, None)
        max_b(par)
        turn_p(lpar, 2)
        times_v(lp, 1)
        turn_p(lpar, 3)
        exps(par)
        next(gen, None)
        next(gen, None)
        if q == 1:
            turn_y(slot)
        times_v(lp, 2)
        times_v(lp, 3)
        finish(lp, lpar, lq)
        next(gen, None)
        quantise(lq)
        if q == 0:
            load_rsm(lp, nxt)

    pr.straight()
    for t in P32[1:] + sums[1:]:
        pr.pool(lambda e, t=t: e.memset(t[:, :], 1.0))
    pr.pool(lambda e: e.memset(yq[:, :, :, :], 1.0))
    for t in (VX[1], VS[1]):
        pr.pool(lambda e, t=t: e.memset(t[:, :, :, :], 1.0))
    load(0, lambda i: 0)
    load(1, lambda i: 1)
    load_rsm(0, lambda i: 0)
    load_rsm(1, lambda i: 0)
    for _ in stage_a(0):
        pass

    def names():
        return (["pa", "pv", "pv_full", "expX", "expS", "negmax", "yq", "yq_read", "tb0", "tb1", "kn0", "kn1",
                 "kn2", "t320", "t321", "PT0", "PT1"]
                + [f"{n}{p}" for p in range(2) for n in ("A_done", "loaded", "values", "QK_read", "V_read", "exp",
                                                         "P_read", "sum_read", "rsm", "finished")]
                + [f"ready{p}_{bank}" for p in range(2) for bank in range(4)])

    pr.loop(NGB // 2)
    pr.carry(*names())
    for half in range(2):
        if half == 0:
            load(0, lambda i: i * 2 + 2)
        gen = stage_a(1 - half)
        for q in range(NQ):
            block(half * NQ + q, gen, lambda i, half=half: i * 2 + half, lambda i, half=half: i * 2 + half + 1)
        for _ in gen:
            pass
        if half == 0:
            load(1, lambda i: i * 2 + 3)
    pr.straight()
    turn.update(tb=0)
    for g in range(4):
        turn_p(1, g)
        times_v(1, g)
    finish(1, 1, NQ - 1)
    quantise(NQ - 1)
    turn_y(lambda i: NGB)


def layer0_projection(k, sb):
    pr, A, x, catq, gate = k["pr"], k["A"], k["x"], k["catq"], k["gate"]
    score = k["score"]
    NCH = 2 * G * HPG
    WIDE = 8 * H
    raw = [sb(f"raw{i}", [P, WIDE], F32) for i in range(2)]
    wp = sb("wp", [P, 2, NCH * H], BF16)
    w13 = sb("w13", [P, 2, 2, IC, NE * FF], BF16)
    w2 = sb("w2", [P, 2, NE, H], BF16)
    k.update(w13=w13, w2=w2)
    flat = lambda t: t.rearrange("p a b -> p (a b)")
    free = [[], []]
    pr.straight()

    def weights(p, src, hi, lo):
        l = pr.dma(f"wp{p}", lambda e: e.dma_start(raw[p][:, :], src), free[p])
        free[p] = [split(pr, raw[p][:, :], hi, lo, [l])]
        return free[p][0]

    proj = [weights(c % 2, flat(A["wprojT"][:, c * 8:(c + 1) * 8, :]), wp[:, 0, c * WIDE:(c + 1) * WIDE],
                    wp[:, 1, c * WIDE:(c + 1) * WIDE]) for c in range(NCH // 8)]
    for i, n in enumerate(("w1T", "w3T")):
        weights(i, flat(A[n]), flat(w13[:, i, 0, :, :]), flat(w13[:, i, 1, :, :]))
    weights(0, flat(A["w2T"]), flat(w2[:, 0, :, :]), flat(w2[:, 1, :, :]))
    layer1_ffn_weights(k, sb, raw, free)

    acc = [score[:, t * 512:t * 512 + H] for t in range(4)] + [b[:, 0:H] for b in (*k["tb"], k["pv"], k["pa"])]
    for quarter in range(NCH // 8):
        for t in range(NT):
            b, tt = t // TB, t % TB
            for chunk in range(8 * quarter, 8 * (quarter + 1)):
                g, x_, h = chunk // (2 * HPG), chunk // HPG % 2, chunk % HPG
                at = ((g * B + b + 1) * 2 * NQ + (x_ * TB + tt) * HPG + h) * P
                for part in range(2):
                    last = (chunk, part) == (NCH - 1, 1)
                    m = pr.pe(lambda e, t=t, at=at, chunk=chunk, part=part, last=last: e.matmul(
                        acc[t], catq[:, at:at + P], wp[:, part, chunk * H:(chunk + 1) * H],
                        start=(chunk == 0 and part == 0), stop=last),
                        [proj[quarter]], signal=last)
    for t in range(NT):
        d = pr.dve(lambda e, t=t: e.scalar_tensor_tensor(x[:, t, :], acc[t], gate[:, 0:1], x[:, t, :],
                                                         ALU.mult, ALU.add), [m])
    pr.leave("x", d)


def split(pr, src, hi, lo, after, hi_free=()):
    h = pr.act(lambda e: e.copy(hi, src), list(after) + list(hi_free))
    return pr.dve(lambda e: e.tensor_tensor(lo, src, hi, ALU.subtract), [h])


def norm_transposed(k, sb, name, eps, want32=False):
    pr, x, ident, score = k["pr"], k["x"], k["ident"], k["score"]
    xn = sb(name + "_xn", [P, NT, H], F32)
    xT = sb(name + "_xT", [P, 2, IC, NT * P], BF16)
    x32 = sb(name + "_x32", [P, IC, NT * P], F32) if want32 else None
    a = layernorm_rows(pr, x, xn, k["st"], k["mv"], k["rs"], k["mhalf"], eps, NT, [])
    outs = []
    for ic in range(IC):
        for q in range(2):
            bank = score[:, (2 * ic + q) * 512:(2 * ic + q + 1) * 512]
            cols = slice(q * 512, (q + 1) * 512)
            for t in range(4):
                tt = pr.pe(lambda e, bank=bank, t=t, q=q, ic=ic: e.transpose(
                    bank[:, t * P:(t + 1) * P], xn[:, 4 * q + t, ic * P:(ic + 1) * P], ident[:, :]), [a],
                    signal=(t == 3))
            w = split(pr, bank, xT[:, 0, ic, cols], xT[:, 1, ic, cols], [tt])
            if want32:
                w = pr.act(lambda e, bank=bank, ic=ic, cols=cols: e.copy(x32[:, ic, cols], bank), [w])
            outs.append(w)
    return xT, x32, outs


THREE = ((0, 0), (0, 1), (1, 0))


def layer0_ffn(k, sb):
    pr, A, x, gate, ident = k["pr"], k["A"], k["x"], k["gate"], k["ident"]
    score, tb, pv, pa = k["score"], k["tb"], k["pv"], k["pa"]
    pr.straight()
    wg = sb("wg", [P, IC, NE], F32)
    brow = sb("brow", [P, NE], F32)
    ld = pr.dma("in", lambda e: e.dma_start(wg[:, :, :], A["wgT"]))
    ld = pr.dma("in", lambda e: e.dma_start(brow[:, :], A["ffn_bias"].partition_broadcast(P)))
    w13, w2 = k["w13"], k["w2"]
    xT, x32, ready = norm_transposed(k, sb, "f", EPS5, want32=True)

    lg = pv[:, 0:NT * NE]
    for t in range(NT):
        for ic in range(IC):
            m = pr.pe(lambda e, t=t, ic=ic: e.matmul(lg[:, t * NE:(t + 1) * NE], x32[:, ic, t * P:(t + 1) * P],
                                                     wg[:, ic, :], start=(ic == 0), stop=(ic == IC - 1)),
                      ready + [ld], signal=(t == NT - 1 and ic == IC - 1))
    small = lambda n: sb(n, [P, NT, NE], F32)
    ex, sig, s1, eq, key, oh, oh2, ew = (small("r_" + n) for n in ("ex", "sig", "s1", "eq", "key", "oh", "oh2", "ew"))
    rank = small("r_rank")
    mx = sb("r_mx", [P, NT], F32)
    for e_ in range(NE):
        rk = pr.pool(lambda e, e_=e_: e.memset(rank[:, :, e_:e_ + 1], float(NE - e_)))
    bc = lambda ap: ap.unsqueeze(2).broadcast_to([P, NT, NE])
    a = pr.act(lambda e: e.activation(ex[:, :, :].rearrange("p a b -> p (a b)"), lg, ACT.Exp, scale=-1.0), [m])
    a = pr.dve(lambda e: e.tensor_scalar(ex[:, :, :], ex[:, :, :], 1.0, None, ALU.add), [a])
    a = pr.dve(lambda e: e.reciprocal(sig[:, :, :], ex[:, :, :]), [a])
    a = pr.dve(lambda e: e.tensor_tensor(s1[:, :, :], sig[:, :, :],
                                         brow[:, :].unsqueeze(1).broadcast_to([P, NT, NE]), ALU.add), [a])
    for hot in (oh, oh2):
        a = pr.dve(lambda e: e.tensor_reduce(mx[:, :], s1[:, :, :], AX.X, ALU.max), [a])
        a = pr.dve(lambda e: e.tensor_tensor(eq[:, :, :], s1[:, :, :], bc(mx[:, :]), ALU.is_equal), [a])
        a = pr.dve(lambda e: e.tensor_tensor(key[:, :, :], eq[:, :, :], rank[:, :, :], ALU.mult), [a, rk])
        a = pr.dve(lambda e: e.tensor_reduce(mx[:, :], key[:, :, :], AX.X, ALU.max), [a])
        a = pr.dve(lambda e, hot=hot: e.tensor_tensor(hot[:, :, :], key[:, :, :], bc(mx[:, :]), ALU.is_equal), [a])
        if hot is oh:
            a = pr.dve(lambda e: e.scalar_tensor_tensor(s1[:, :, :], oh[:, :, :], -1e30, s1[:, :, :],
                                                        ALU.mult, ALU.add), [a])
    a = pr.dve(lambda e: e.tensor_tensor(oh[:, :, :], oh[:, :, :], oh2[:, :, :], ALU.add), [a])
    a = pr.dve(lambda e: e.tensor_tensor(oh[:, :, :], oh[:, :, :], sig[:, :, :], ALU.mult), [a])
    a = pr.dve(lambda e: e.tensor_reduce(mx[:, :], oh[:, :, :], AX.X, ALU.add), [a])
    a = pr.dve(lambda e: e.reciprocal(mx[:, :], mx[:, :]), [a])
    ewr = pr.dve(lambda e: e.scalar_tensor_tensor(ew[:, :, :], oh[:, :, :], 0.5, bc(mx[:, :]), ALU.mult, ALU.mult), [a])

    th = [sb(f"f_th{i}", [P, 512], F32) for i in range(2)]
    gg = [sb(f"f_g{i}", [P, 512], F32) for i in range(2)]
    gT = [sb(f"f_gT{i}", [P, 2, 512], BF16) for i in range(2)]
    EH = NE // 2
    pairs = [(t, hf) for t in range(NT) for hf in range(2)]
    state, turned = {}, {}

    def up(n):
        t, hf = pairs[n]
        i = n % 2
        free = pr.of(f"h{i}")
        toks = []
        for w in range(2):
            bank = score[:, (2 * i + w) * 512:(2 * i + w + 1) * 512]
            passes = [(ic, a, b) for ic in range(IC) for a, b in THREE]
            for s, (ic, a, b) in enumerate(passes):
                m = pr.pe(lambda e, bank=bank, w=w, ic=ic, a=a, b=b, s=s: e.matmul(
                    bank, xT[:, a, ic, t * P:(t + 1) * P], w13[:, w, b, ic, hf * 512:(hf + 1) * 512],
                    start=(s == 0), stop=(s == 5)), free + ready, signal=(s == 5))
            toks.append(m)
        h1, h3 = (score[:, (2 * i + w) * 512:(2 * i + w + 1) * 512] for w in range(2))
        a = pr.act(lambda e: e.activation(th[i][:, :], h1, ACT.Tanh, scale=0.5), [toks[0]] + pr.of(f"th{i}"))
        a = pr.dve(lambda e: e.scalar_tensor_tensor(th[i][:, :], th[i][:, :], 1.0, h1, ALU.add, ALU.mult), [a])
        a = pr.dve(lambda e: e.tensor_tensor(th[i][:, :], th[i][:, :], h3, ALU.mult), [a, toks[1]])
        pr.leave(f"h{i}", a)
        w_ = ew[:, t, hf * EH:(hf + 1) * EH].unsqueeze(2).broadcast_to([P, EH, FF])
        a = pr.dve(lambda e: e.tensor_tensor(gg[i][:, :].rearrange("p (a b) -> p a b", a=EH),
                                             th[i][:, :].rearrange("p (a b) -> p a b", a=EH), w_, ALU.mult),
                   [a, ewr] + pr.of(f"gg{i}"))
        pr.leave(f"th{i}", a)
        state[n] = a

    def turn(n):
        i = n % 2
        for j in range(EH):
            m = pr.pe(lambda e, j=j: e.transpose(tb[i][:, j * P:(j + 1) * P], gg[i][:, j * FF:(j + 1) * FF], ident[:, :]),
                      [state[n]] + pr.of(f"tbf{i}"), signal=(j == EH - 1))
        pr.leave(f"gg{i}", m)
        s = split(pr, tb[i][:, :], gT[i][:, 0, :], gT[i][:, 1, :], [m], pr.of(f"gT{i}"))
        pr.leave(f"tbf{i}", s)
        turned[n] = s

    def down(n):
        t, hf = pairs[n]
        i = n % 2
        acc = (pv, pa)[t % 2]
        for j in range(EH):
            for c, (a, b) in enumerate(THREE):
                first, last = (hf, j, c) == (0, 0, 0), (hf, j, c) == (1, EH - 1, 2)
                m = pr.pe(lambda e, j=j, a=a, b=b, first=first, last=last, acc=acc: e.matmul(
                    acc[:, 0:H], gT[i][:, a, j * P:(j + 1) * P], w2[:, b, hf * EH + j, :], start=first, stop=last),
                    [turned[n]] + pr.of(f"acc{t % 2}"), signal=(j == EH - 1 and c == 2))
        pr.leave(f"gT{i}", m)
        if hf == 1:
            d = pr.dve(lambda e, acc=acc, t=t: e.scalar_tensor_tensor(x[:, t, :], acc[:, 0:H], gate[:, 2:3], x[:, t, :],
                                                                      ALU.mult, ALU.add), [m])
            pr.leave(f"acc{t % 2}", d)
            pr.leave("x", d)

    for n in range(len(pairs) + 2):
        if n < len(pairs):
            up(n)
        if n >= 2:
            down(n - 2)
        if 1 <= n <= len(pairs):
            turn(n - 1)


def layer1_attention(k, sb):
    pr, A, x, gate, ident, identb = k["pr"], k["A"], k["x"], k["gate"], k["ident"], k["identb"]
    score, tb, pv, pa, mhalf = k["score"], k["tb"], k["pv"], k["pa"], k["mhalf"]
    HQ, R = NH1 // 4, 4 * D1
    VC = 16
    w1 = sb("l1_w", [P, 2, IC, 3 * H], BF16)
    stg = [sb(f"l1_ctx{i}", [P, 2, IC, SC], BF16) for i in range(2)]
    QB = [sb(f"QB{i}", [P, HQ, 4, S], BF16) for i in range(2)]
    KT1 = [sb(f"KT1_{i}", [P, HQ, SC], BF16) for i in range(2)]
    V1 = [sb(f"V1_{i}", [P, KT, NH1, VC], F32) for i in range(2)]
    wf = V1[1][:, :, :, :].rearrange("p a b c -> p (a b c)")[:, 0:IC * 3 * H].rearrange("p (i c) -> p i c", i=IC)
    P1 = [sb(f"P1_{i}", [P, 4 * S], F32) for i in range(3)]
    xn = sb("l1_xn", [P, TB, H], F32)
    xT = sb("l1_xT", [P, 2, IC, P], BF16)
    st, mv, rs = sb("l1_st", [P, TB, 6], F32), sb("l1_mv", [P, TB, 2], F32), sb("l1_rs", [P, TB], F32)
    sq = sb("l1_sq", [P, H], F32)
    ss, rr, kn = ([sb(f"l1_{n}{i}", [P, w], F32) for i in range(3)] for n, w in (("ss", NH1), ("rr", NH1), ("kn", H)))
    stack = [sb(f"l1_stack{i}", [P, NH1, 4, D1], BF16) for i in range(2)]
    eps6 = sb("l1_eps6", [P, 1], F32)
    OS = [sb(f"l1_O{i}", [P, S], F32) for i in range(2)]
    den = sb("l1_den", [P, TB, 4], F32)
    att = sb("l1_att", [P, TB, 4, D1], F32)

    pr.straight()
    l = pr.dma("w0", lambda e: e.dma_start(wf, A["l1_wT"]))
    pr.leave("w1", split(pr, wf, w1[:, 0, :, :], w1[:, 1, :, :], [l]))
    e6 = pr.dve(lambda e: e.memset(eps6[:, :], EPS6))
    pr.leave("pv", pr.dve(lambda e: e.memset(pv[:, :], 0.0)))
    for i in range(2):
        z = pr.pool(lambda e, i=i: e.memset(V1[i][:, :, :, :], 0.0), pr.of("w1") if i else ())
        pr.leave(f"V_read{i}", pr.pool(lambda e, i=i: e.memset(V1[i][:, :, :, D1:D1 + 1], 1.0), [z]))
        pr.leave(f"QK_read{i}", pr.pool(lambda e, i=i: e.memset(QB[i][:, :, :, :], 0.0)))

    def load(p, n):
        a = pr.dma(f"ld{p}", lambda e: e.dma_start(
            stg[p][:, :, :, :].rearrange("p a b c -> p (a b c)").rearrange("p (o c) -> p o c", o=1),
            k["stage_d"][bass.ds(n(pr.i) % B, 1), :, 0:2 * IC * SC].rearrange("o p c -> p o c")), pr.of(f"prepared{p}"))
        pr.leave(f"loaded{p}", a)

    def rms_start(c, bank, rows, ready, before_loop):
        b = c % 3
        k_ = pr.act(lambda e: e.copy(kn[b][0:rows, :], bank), [ready] + pr.of(f"kn{b}"))
        a = pr.dve(lambda e: e.tensor_tensor(sq[0:rows, :], kn[b][0:rows, :], kn[b][0:rows, :], ALU.mult), [k_])
        a = pr.dve(lambda e: e.tensor_reduce(ss[b][0:rows, :], sq[0:rows, :].rearrange("p (h d) -> p h d", d=D1),
                                             AX.X, ALU.add), [a])
        if before_loop:
            a = pr.act(lambda e: e.activation(rr[b][0:rows, :], ss[b][0:rows, :], ACT.Sqrt, scale=1.0 / D1,
                                              bias=eps6[0:rows, 0:1]), [a, e6])
            return k_, pr.dve(lambda e: e.reciprocal(rr[b][0:rows, :], rr[b][0:rows, :]), [a])
        a = pr.pool(lambda e: e.tensor_scalar(rr[b][0:rows, :], ss[b][0:rows, :], 1.0 / D1, EPS6, ALU.mult, ALU.add),
                    [a], lone=True)
        return k_, pr.pool(lambda e: e.tensor_tensor(rr[b][0:rows, :], rr[b][0:rows, :], mhalf[0:rows, 0:NH1],
                                                     ALU.pow), [a])

    def rms_stack(c, rows, ready, keys):
        b, s = c % 3, c % 2
        heads = kn[b][0:rows, :].rearrange("p (h d) -> p h d", d=D1)
        a = pr.dve(lambda e: e.tensor_tensor(heads, heads, rr[b][0:rows, :].unsqueeze(2).broadcast_to(
            [rows, NH1, D1]), ALU.mult), [ready])
        twice = heads.unsqueeze(2).broadcast_to([rows, NH1, 2, D1])
        part = lambda i: stack[s][0:rows, :, 2 * i:2 * i + 2, :] if keys else stack[s][0:rows, :, i::2, :]
        a = pr.dve(lambda e: e.tensor_copy(part(0), twice), [a] + pr.of(f"stack{s}"))
        a = pr.dve(lambda e: e.tensor_tensor(part(1), twice, part(0), ALU.subtract), [a])
        pr.leave(f"kn{b}", a)
        return a

    def turn_stack(c, rows, ready):
        s = c % 2
        bank = tb[1][:, :].bitcast(BF16)
        st_ = stack[s][:, :, :, :].rearrange("p h s d -> p (h s d)")
        for q in range(HQ):
            m = pr.pe(lambda e, q=q: e.transpose(bank[:, q * P:q * P + rows], st_[0:rows, q * P:(q + 1) * P],
                                                 identb[0:rows, 0:rows]), [ready] + pr.of("tb1"), signal=(q == HQ - 1))
        pr.leave(f"stack{s}", m)
        return bank.rearrange("p (q t) -> p q t", q=HQ)[:, :, 0:rows], m

    def prepare(p, n, before_loop=False):
        outs, made, stacked, norm = [], {}, {}, {}
        xrow = lambda t: x[:, bass.ds(n(pr.i) % B * TB + t, 1), :].rearrange("p o d -> p (o d)")

        def norm_start():
            for t in range(TB):
                a = pr.dve(lambda e, t=t: e.bn_stats(st[:, t, :], xrow(t)), pr.of("x"))
            for t in range(TB):
                a = pr.dve(lambda e, t=t: e.bn_aggr(mv[:, t, :], st[:, t, :]), [a], lone=True)
            a = pr.pool(lambda e: e.tensor_scalar(rs[:, :], mv[:, :, 1], EPS5, None, ALU.add), [a], lone=True)
            norm["rs"] = pr.pool(lambda e: e.tensor_tensor(rs[:, :], rs[:, :], mhalf[:, 0:TB], ALU.pow), [a])

        def norm_end():
            for t in range(TB):
                norm["x"] = pr.dve(lambda e, t=t: e.tensor_scalar(
                    xn[:, t, :], xrow(t), mv[:, t, 0:1], rs[:, t:t + 1], ALU.subtract, ALU.mult),
                    [norm["rs"]] + pr.of("xn_read"))

        def turn_x(t):
            for ic in range(IC):
                m = pr.pe(lambda e, ic=ic: e.transpose(tb[0][:, ic * P:(ic + 1) * P], xn[:, t, ic * P:(ic + 1) * P],
                                                       ident[:, :]), [norm["x"]] + pr.of("tb0"), signal=(ic == IC - 1))
            pr.leave("xn_read", m)
            s = split(pr, tb[0][:, 0:IC * P], xT[:, 0, :, :].rearrange("p i t -> p (i t)"),
                      xT[:, 1, :, :].rearrange("p i t -> p (i t)"), [m], pr.of("xT_read"))
            pr.leave("tb0", s)
            norm["xT"] = s

        def query_product(t):
            for i, (ic, a, b) in enumerate((ic, a, b) for ic in range(IC) for a, b in THREE):
                m = pr.pe(lambda e, ic=ic, a=a, b=b, i=i: e.matmul(
                    pa[:, 0:H], xT[:, a, ic, :], w1[:, b, ic, 0:H], start=(i == 0), stop=(i == 5)),
                    [norm["xT"]] + pr.of("pa", "w1"), signal=(i == 5))
            pr.leave("xT_read", m)
            read, made[t] = rms_start(t, pa[:, 0:H], P, m, before_loop)
            pr.leave("pa", read)

        def key_product(c):
            t, rows = c - TB, P if c - TB < KT - 1 else TAIL
            for i, (ic, a, b) in enumerate((ic, a, b) for ic in range(IC) for a, b in THREE):
                m = pr.pe(lambda e, ic=ic, a=a, b=b, i=i: e.matmul(
                    pa[0:rows, :], stg[p][:, a, ic, t * P:t * P + rows], w1[:, b, ic, H:3 * H],
                    start=(i == 0), stop=(i == 5)), pr.of("pa", "w1", f"loaded{p}"), signal=(i == 5))
            read, made[c] = rms_start(c, pa[0:rows, 0:H], rows, m, before_loop)
            v = pr.act(lambda e: e.copy(V1[p][0:rows, t, :, 0:D1], pa[0:rows, H:2 * H].rearrange(
                "p (h d) -> p h d", d=D1)), [m] + pr.of(f"V_read{p}"))
            outs.append(v)
            pr.leave("pa", read, v)
            if t == KT - 1:
                pr.leave(f"prepared{p}", m)

        def finish(c):
            rows = TAIL if c == chunks - 1 else P
            bank, m = turn_stack(c, rows, stacked[c])
            if c < TB:
                for j in range(4):
                    r = pr.dve(lambda e, j=j: e.tensor_copy(
                        QB[p][j * R:(j + 1) * R, :, j, c * P:(c + 1) * P], bank[j * R:(j + 1) * R, :, :]),
                        [m] + pr.of(f"QK_read{p}"))
            else:
                at = (c - TB) * P
                r = pr.dve(lambda e: e.tensor_copy(KT1[p][:, :, at:at + rows], bank), [m] + pr.of(f"QK_read{p}"))
            pr.leave("tb1", r)
            outs.append(r)

        def stack_up(c):
            stacked[c] = rms_stack(c, TAIL if c == chunks - 1 else P, made[c], c >= TB)

        chunks = TB + KT
        at = lambda c: 3 + 3 * c
        work = [[] for _ in range(at(chunks - 1) + 7)]
        work[0].append(norm_start)
        work[1].append(norm_end)
        for c in range(chunks):
            if c < TB:
                work[at(c) - 1].append(lambda c=c: turn_x(c))
            work[at(c)].append(lambda c=c: query_product(c) if c < TB else key_product(c))
            work[at(c) + 4].append(lambda c=c: stack_up(c))
        for c in range(chunks):
            work[at(c) + 6].append(lambda c=c: finish(c))
        for pieces in work:
            for piece in pieces:
                piece()
            yield
        pr.leave(f"ready{p}", *outs)

    def attend(p, n, gen):
        steps = [(hq, t) for hq in range(HQ) for t in range(KT)]
        exps, copied = {}, {}

        def first(i):
            hq, t = steps[i]
            rows = P if t < KT - 1 else TAIL
            d = i % 2
            for h in range(2):
                m = pr.pe(lambda e, h=h: e.matmul(
                    score[0:rows, (2 * d + h) * 512:(2 * d + h + 1) * 512], KT1[p][:, hq, t * P:t * P + rows],
                    QB[p][:, hq, 2 * h:2 * h + 2, :], start=True, stop=True),
                    pr.of(f"s{d}", f"ready{p}"), signal=(h == 1))
            if i == len(steps) - 1:
                pr.leave(f"QK_read{p}", m)
            b = i % 3
            a = pr.act(lambda e: e.activation(P1[b][0:rows, :], score[0:rows, d * 1024:(d + 1) * 1024], ACT.Exp,
                                              scale=float(D1) ** -0.5), [m] + pr.of(f"P{b}"))
            pr.leave(f"s{d}", a)
            exps[i] = a

        def second(i):
            hq, t = steps[i]
            rows = P if t < KT - 1 else TAIL
            b, o = i % 3, hq % 2
            for j in range(4):
                m = pr.pe(lambda e, j=j: e.matmul(
                    pv[j * R:j * R + VC, 0:S], V1[p][0:rows, t, 4 * hq + j, :],
                    P1[b][0:rows, j * S:(j + 1) * S], start=(t == 0), stop=(t == KT - 1), skip_group_check=True),
                    [exps[i]] + pr.of("pv"), signal=(j == 3))
            pr.leave(f"P{b}", m)
            if i == len(steps) - 1:
                pr.leave(f"V_read{p}", m)
            if t == KT - 1:
                c = pr.dve(lambda e: e.tensor_copy(OS[o][:, :], pv[:, 0:S]), [m] + pr.of(f"OS{o}"))
                pr.leave("pv", c)
                copied[hq] = c

        def third(hq):
            o = hq % 2
            for tt in range(TB):
                m = pr.pe(lambda e, tt=tt: e.transpose(tb[0][:, tt * P:(tt + 1) * P], OS[o][:, tt * P:(tt + 1) * P],
                                                       ident[:, :]), [copied[hq]] + pr.of("tb0"), signal=(tt == TB - 1))
            pr.leave(f"OS{o}", m)
            v = tb[0][:, 0:TB * P].rearrange("p (t h c) -> p t h c", t=TB, h=4)
            r = pr.dve(lambda e: e.reciprocal(den[:, :, :], v[:, :, :, D1]), [m])
            r = pr.dve(lambda e: e.tensor_tensor(att[:, :, :, :], v[:, :, :, 0:D1],
                                                 den[:, :, :].unsqueeze(3).broadcast_to([P, TB, 4, D1]),
                                                 ALU.mult), [r])
            pr.leave("tb0", r)

            def xs():
                return x[:, bass.ds(n(pr.i) % B * TB, TB), hq * R:(hq + 1) * R]
            r = pr.dve(lambda e: e.scalar_tensor_tensor(
                xs(), att[:, :, :, :].rearrange("p t h d -> p t (h d)"), gate[:, 1:2], xs(), ALU.mult, ALU.add), [r])
            pr.leave("x", r)

        first(0)
        for i in range(1, len(steps) + 2):
            if i < len(steps):
                first(i)
            if i >= 2:
                second(i - 2)
            if i % 2 == 0:
                next(gen, None)
            if i >= 2 and steps[i - 2][1] == 1 and steps[i - 2][0]:
                third(steps[i - 2][0] - 1)
        for _ in gen:
            pass
        third(HQ - 1)

    load(0, lambda i: 0)
    load(1, lambda i: 1)
    for _ in prepare(0, lambda i: 0, True):
        pass
    pr.loop(B // 2)
    pr.carry(*(["x", "xn_read", "xT_read", "tb0", "tb1", "pa", "pv", "kn0", "kn1", "kn2", "stack0",
                "stack1", "s0", "s1", "P0", "P1", "P2", "OS0", "OS1"]
               + [f"{n}{p}" for p in range(2) for n in ("loaded", "prepared", "QK_read", "V_read", "ready")]))
    load(0, lambda i: 2 * i + 2)
    attend(0, lambda i: 2 * i, prepare(1, lambda i: 2 * i + 1))
    load(1, lambda i: 2 * i + 3)
    attend(1, lambda i: 2 * i + 1, prepare(0, lambda i: 2 * i + 2))


def layer1_ffn_weights(k, sb, raw, free):
    pr, A, gate, sc, wT, bias = k["pr"], k["A"], k["gate"], k["sc"], k["l1_ffn_w"], k["l1_ffn_b"]
    pb, nb = (sb(n, [P, H, NBITS], F32) for n in ("b_pb", "b_nb"))
    bits = sb("b_bits", [P, 3, NBITS], F32)
    wT32 = sb("b_w32", [P, IC, H], F32)
    coef = sb("b_coef", [P, NBITS], F32)
    l1, l2 = (pr.dma(f"w{p}", lambda e, p=p, n=n: e.dma_start(raw[p][:, :], A[n].rearrange("p a b c -> p (a b c)")),
                     free[p]) for p, n in enumerate(("pweight", "nweight")))
    pr.dma("in", lambda e: e.dma_start(pb[:, :, :].rearrange("p a b -> p (a b)"), A["pbias"].partition_broadcast(P)))
    pr.dma("in", lambda e: e.dma_start(nb[:, :, :].rearrange("p a b -> p (a b)"), A["nbias"].partition_broadcast(P)))
    l3 = pr.dma("in", lambda e: e.dma_start(bits[:, :, :].rearrange("p a b -> p (a b)"),
                                            A["bits"].partition_broadcast(P)))
    t1, t2 = (pr.act(lambda e, p=p: e.activation(raw[p][:, :], raw[p][:, :], ACT.Tanh, scale=0.5), [l])
              for p, l in ((0, l1), (1, l2)))
    c = pr.act(lambda e: e.activation(coef[:, :], bits[:, 2, :], ACT.Exp, scale=-1.0), [l3])
    c = pr.dve(lambda e: e.tensor_scalar(coef[:, :], coef[:, :], 1.0, None, ALU.add), [c])
    c = pr.dve(lambda e: e.reciprocal(coef[:, :], coef[:, :]), [c])
    c = pr.dve(lambda e: e.tensor_tensor(coef[:, :], coef[:, :], bits[:, 0, :], ALU.mult), [c])
    c = pr.dve(lambda e: e.tensor_scalar(coef[:, :], coef[:, :], sc("scale"), 0.5, ALU.mult, ALU.mult), [c])
    d = pr.dve(lambda e: e.tensor_tensor(raw[0][:, :], raw[0][:, :], raw[1][:, :], ALU.subtract), [t1, t2])
    soft = raw[0][:, :].rearrange("p (w n) -> p w n", n=NBITS)
    d = pr.dve(lambda e: e.tensor_tensor(soft, soft, coef[:, :].unsqueeze(1).broadcast_to([P, IC * H, NBITS]),
                                         ALU.mult), [d, c])
    d = pr.dve(lambda e: e.tensor_reduce(wT32[:, :, :].rearrange("p a b -> p (a b)"), soft, AX.X, ALU.add), [d])
    split(pr, wT32[:, :, :], wT[:, 0, :, :], wT[:, 1, :, :], [d])
    b = pr.dve(lambda e: e.tensor_tensor(pb[:, :, :], pb[:, :, :], nb[:, :, :], ALU.subtract), [l3])
    b = pr.dve(lambda e: e.tensor_tensor(pb[:, :, :], pb[:, :, :],
                                         bits[:, 1, :].unsqueeze(1).broadcast_to([P, H, NBITS]), ALU.mult), [b])
    b = pr.dve(lambda e: e.tensor_reduce(bias[:, :], pb[:, :, :], AX.X, ALU.add), [b])
    step = float(2 ** NBITS - 1)
    b = pr.dve(lambda e: e.tensor_scalar(bias[:, :], bias[:, :], 1.0, -1.0, ALU.min, ALU.max), [b])
    b = pr.dve(lambda e: e.tensor_scalar(bias[:, :], bias[:, :], step, ROUND_INT, ALU.mult, ALU.add), [b])
    b = pr.dve(lambda e: e.tensor_scalar(bias[:, :], bias[:, :], ROUND_INT, 1.0 / step, ALU.subtract, ALU.mult), [b])
    pr.dve(lambda e: e.tensor_scalar(bias[:, :], bias[:, :], sc("bscale"), gate[:, 3:4], ALU.mult, ALU.mult), [b])


def layer1_ffn(k, sb):
    pr, x, gate, score, wT, bias = k["pr"], k["x"], k["gate"], k["score"], k["l1_ffn_w"], k["l1_ffn_b"]
    pr.straight()
    xT, _, ready = norm_transposed(k, sb, "g", EPS5)
    passes = [(ic, a, c_) for ic in range(IC) for a, c_ in THREE]
    free = {i: list(ready) for i in range(4)}
    for t in range(NT):
        i = t % 4
        bank = score[:, i * 512:i * 512 + H]
        for n, (ic, a, w) in enumerate(passes):
            m = pr.pe(lambda e, t=t, ic=ic, a=a, w=w, n=n, bank=bank: e.matmul(
                bank, xT[:, a, ic, t * P:(t + 1) * P], wT[:, w, ic, :], start=(n == 0), stop=(n == 5)),
                free[i], signal=(n == 5))
        d = pr.dve(lambda e, t=t, bank=bank: e.scalar_tensor_tensor(x[:, t, :], bank, gate[:, 3:4], x[:, t, :],
                                                                    ALU.mult, ALU.add), [m])
        free[i] = [d]
        d = pr.dve(lambda e, t=t: e.tensor_tensor(x[:, t, :], x[:, t, :], bias[:, :], ALU.add), [d])
        pr.dma("out", lambda e, t=t: e.dma_start(k["out"][t * P:(t + 1) * P, :], x[:, t, :]), [d])


def kernel(**inputs):
    import numpy as np
    import concourse.bacc as bacc
    from concourse.bass_utils import run_bass_kernel_spmd

    nc = bacc.Bacc("TRN2", target_bir_lowering=False, num_devices=1)
    arrays, A = {}, {}
    for name, a in layout(np, inputs).items():
        arrays["in_" + name] = a
        A[name] = nc.dram_tensor("in_" + name, a.shape, mybir.dt.from_np(a.dtype), kind="ExternalInput").ap()
    out = nc.dram_tensor("out_0", (B * S, H), F32, kind="ExternalOutput").ap()
    build(nc, A, out)
    r = run_bass_kernel_spmd(nc, [arrays], core_ids=[0])
    return np.asarray(r.results[0]["out_0"]).reshape(B, S, H)


def layout(np, v):
    a = {n: np.ascontiguousarray(np.asarray(z)) for n, z in v.items()}
    l0 = lambda n: a["L0_xattn_" + n]

    def chunked(w):
        return w.reshape(w.shape[0] // P, P, -1).transpose(1, 0, 2)

    out = {}
    out["x"] = a["x"].reshape(B * S, H)
    out["ctxT"] = np.ascontiguousarray(chunked(a["ctx_2048"].reshape(B * SC, H).T).reshape(P, IC, B, SC))
    wt = {n: l0(n).T for n in ("wq", "wqx", "wk", "wv")}
    kv = l0("w_kv_x").T
    groups = []
    for g in range(G):
        s2, s1 = slice(g * HPG * D, (g + 1) * HPG * D), slice(g * D, (g + 1) * D)
        groups.append(chunked(np.concatenate(
            [wt["wq"][:, s2], wt["wqx"][:, s2], wt["wk"][:, s1], wt["wv"][:, s1], kv[:, s1],
             kv[:, G * D + g * D:G * D + (g + 1) * D]], axis=1)))
    out["w_all"] = np.ascontiguousarray(np.stack(groups))
    names = ["ln_w", "ln_b", "q_in_scale", "qx_in_scale", "k_in_scale", "v_in_scale"]
    out["cols"] = np.ascontiguousarray(np.concatenate([l0(n).reshape(IC, P).T for n in names], axis=1))
    out["dcols"] = np.ascontiguousarray(np.stack([l0(n) for n in DCOLS], axis=1))
    out["scal"] = np.concatenate([z.reshape(-1) for z in (
        l0("wq_scale"), l0("wqx_scale"), l0("wk_scale"), l0("wv_scale"), l0("proj_w_scale"), l0("proj_in_scale"),
        a["g_xattn"], a["g_ffn"], a["L1_ffn_scale"], a["L1_ffn_biasscale"])])
    fe = lambda z: z.reshape(2, G, HPG, D, -1).transpose(1, 0, 2, 3, 4).reshape(2 * G * HPG * D, -1)
    out["smooth"] = np.ascontiguousarray(fe(l0("proj_smooth")).reshape(P, 2 * G * HPG))
    out["wprojT"] = np.ascontiguousarray(fe(l0("wproj").T).reshape(2 * G * HPG, P, H).transpose(1, 0, 2))
    f = lambda n: a["L0_ffn_" + n]
    out["wgT"] = np.ascontiguousarray(chunked(f("Wg").T))
    out["w1T"] = np.ascontiguousarray(chunked(f("W1").reshape(NE * FF, H).T))
    out["w3T"] = np.ascontiguousarray(chunked(f("W3").reshape(NE * FF, H).T))
    out["w2T"] = np.ascontiguousarray(f("W2").transpose(2, 0, 1))
    out["ffn_bias"] = f("bias")
    kv1 = np.concatenate([a["L1_xattn_Wk"], a["L1_xattn_Wv"]], axis=0)
    out["l1_wT"] = np.ascontiguousarray(chunked(np.concatenate([a["L1_xattn_Wq"], kv1[0::2], kv1[1::2]], axis=0).T))
    for n in ("pweight", "nweight"):
        out[n] = np.ascontiguousarray(a["L1_ffn_" + n].transpose(1, 0, 2).reshape(IC, P, H, NBITS).transpose(1, 0, 2, 3))
    for n in ("pbias", "nbias"):
        out[n] = a["L1_ffn_" + n].reshape(-1)
    out["bits"] = np.concatenate([a["L1_ffn_exps"], a["L1_ffn_bexps"], a["L1_ffn_mask_weight"]])
    return out
```
